# Optimizing a Trainium2 kernel written in Bass

```python
import numpy as np
import jax
import jax.numpy as jnp

def _softmax(x, axis=-1):
    return jax.nn.softmax(x, axis=axis)

def _gelu(x):
    return jax.nn.gelu(x, approximate=True)

def _silu(x):
    return jax.nn.silu(x)

def _sigmoid(x):
    return jax.nn.sigmoid(x)

def _layernorm(x, axis=-1, eps=1e-05):
    m = jnp.mean(x, axis=axis, keepdims=True)
    v = jnp.var(x, axis=axis, keepdims=True)
    return (x - m) / jnp.sqrt(v + eps)

def _scatter_add(tgt, idx, src, axis=0):
    return tgt.at[idx].add(src)

def _segment_sum(src, seg, n):
    return jax.ops.segment_sum(src, seg, n)
kernel_name = 'mk_seq_preln_d1_jaxref_r8_e5b9c1'

def setup_inputs(seed: int=0):
    np.random.seed(seed)
    _w = jnp.asarray

    def _L0_attn_setup():
        import jax, jax.numpy as jnp
        import numpy as np
        EMBED_DIM = 128
        NUM_HEADS = 8
        HEAD_DIM = EMBED_DIM // NUM_HEADS
        NUM_QUBITS = 8
        CIRCUITS = 4
        DEPTH = 3
        WAVELENGTHS = 16
        SCALING = HEAD_DIM ** (-0.5)
        ERR_MIN = 1e-06
        TWO_PI = 2.0 * np.pi

        def _quantum_encode(x, photonic_phases):
            hd = x.shape[-1]
            norm = jnp.sqrt(jnp.sum(x * x, axis=-1, keepdims=True))
            normed = x / jnp.maximum(norm, 1e-12)
            ch = jnp.arange(hd)
            phases = photonic_phases[ch % WAVELENGTHS, ch]
            return normed * jnp.exp(1j * phases)

        def _entangle(state, gates):
            for depth in range(DEPTH):
                g = gates[depth, :NUM_HEADS - 1]
                theta = g[:, 0][None, None, :, None]
                phi = g[:, 1][None, None, :, None]
                s1 = state[:, :, :-1]
                s2 = state[:, :, 1:]
                cos_t = jnp.cos(theta / 2)
                sin_t = jnp.sin(theta / 2)
                ctrl = jnp.abs(s1) ** 2
                rot = cos_t * s2 + sin_t * jnp.exp(1j * phi) * jnp.conj(s2)
                new = ctrl * rot + (1.0 - ctrl) * s2
                state = jnp.concatenate([new, state[:, :, -1:]], axis=2)
            return state

        def _forward(query, W_qkv, b_qkv, W_out, b_out, quantum_weights, photonic_phases, entanglement_gates, superposition_logits):
            B, S, E = query.shape
            qkv = query @ W_qkv.T + b_qkv
            q, k, v = jnp.split(qkv, 3, axis=-1)
            q = q.reshape(B, S, NUM_HEADS, HEAD_DIM)
            k = k.reshape(B, S, NUM_HEADS, HEAD_DIM)
            v = v.reshape(B, S, NUM_HEADS, HEAD_DIM)
            qq = _quantum_encode(q, photonic_phases)
            kq = _quantum_encode(k, photonic_phases)
            vq = _quantum_encode(v, photonic_phases)
            q_ent = _entangle(qq, entanglement_gates)
            k_ent = _entangle(kq, entanglement_gates)
            coh = jnp.exp(1j * jnp.angle(jnp.sum(vq, axis=2, keepdims=True)))
            sup_w = jax.nn.softmax(superposition_logits)
            final = None
            for c in range(CIRCUITS):
                ratio = 0.5 + 0.3 * jnp.sin(quantum_weights[c, 0, 0])
                qa = jnp.sqrt(ratio) * q_ent
                ka = jnp.sqrt(1.0 - ratio) * k_ent
                pattern = jnp.einsum('bsid,bsjd->bsij', jnp.conj(qa), ka)
                mod = pattern * jnp.exp(1j * quantum_weights[c, 1, :])
                scores = jnp.abs(mod) ** 2 * SCALING
                probs = jax.nn.softmax(scores, axis=-1)
                amps = jnp.sqrt(probs + 1e-12)
                coh_phase = jnp.angle(jnp.sum(scores, axis=-1, keepdims=True))
                w = amps * jnp.cos(coh_phase)
                weighted = jnp.einsum('bsij,bsjd->bsid', w.astype(jnp.complex64), vq)
                co = weighted * coh
                amp = jnp.clip(jnp.abs(co), ERR_MIN, 1.0)
                ph = jnp.mod(jnp.angle(co), TWO_PI)
                corrected = amp * jnp.exp(1j * ph)
                contrib = sup_w[c] * corrected
                final = contrib if final is None else final + contrib
            measured = jnp.real(final).reshape(B, S, E)
            return measured @ W_out.T + b_out
        key = jax.random.key(seed)
        ks = jax.random.split(key, 8)
        B, S, E = (2, 256, EMBED_DIM)
        return {'query': jax.random.normal(ks[0], (B, S, E), jnp.float32), 'W_qkv': jax.random.normal(ks[1], (3 * E, E), jnp.float32) / np.sqrt(E).astype(np.float32), 'b_qkv': jnp.zeros((3 * E,), jnp.float32), 'W_out': jax.random.normal(ks[2], (E, E), jnp.float32) / np.sqrt(E).astype(np.float32), 'b_out': jnp.zeros((E,), jnp.float32), 'quantum_weights': jax.random.normal(ks[3], (CIRCUITS, NUM_QUBITS, NUM_QUBITS), jnp.float32) * 0.1, 'photonic_phases': jax.random.normal(ks[4], (WAVELENGTHS, E), jnp.float32) * np.float32(np.pi), 'entanglement_gates': jax.random.normal(ks[5], (DEPTH, NUM_HEADS, 4), jnp.float32) * 0.1, 'superposition_logits': jax.random.normal(ks[6], (CIRCUITS,), jnp.float32)}
    _L0_attn_in = _L0_attn_setup()

    def _L0_ffn_setup():
        import jax, jax.numpy as jnp
        import numpy as np
        H = 128
        I = 88
        E = 64
        TOP_K = 8
        NG = 8
        TOPK_GROUP = 4
        N_SHARED = 2
        ROUTED_SCALE = 2.5
        S_I = I * N_SHARED

        def _route(x, gate_w, gate_bias):
            T = x.shape[0]
            logits = x @ gate_w.T
            scores = jax.nn.sigmoid(logits)
            scores_for_choice = scores + gate_bias[None, :]
            grp = scores_for_choice.reshape(T, NG, E // NG)
            group_scores = jnp.sum(jax.lax.top_k(grp, 2)[0], axis=-1)
            _, gidx = jax.lax.top_k(group_scores, TOPK_GROUP)
            gmask = jnp.zeros((T, NG), dtype=scores.dtype).at[jnp.arange(T)[:, None], gidx].set(1.0)
            emask = jnp.repeat(gmask, E // NG, axis=1)
            masked = jnp.where(emask > 0, scores_for_choice, 0.0)
            _, topk_idx = jax.lax.top_k(masked, TOP_K)
            topk_w = jnp.take_along_axis(scores, topk_idx, axis=1)
            topk_w = topk_w / (jnp.sum(topk_w, axis=-1, keepdims=True) + 1e-20)
            topk_w = topk_w * ROUTED_SCALE
            rw = jnp.zeros((T, E), dtype=scores.dtype).at[jnp.arange(T)[:, None], topk_idx].add(topk_w)
            return rw

        def _mlp(x, gw, uw, dw):
            return jax.nn.silu(x @ gw.T) * (x @ uw.T) @ dw.T
        key = jax.random.key(seed)
        ks = jax.random.split(key, 10)
        sc = 0.02
        return {'hidden_states': jax.random.normal(ks[0], (1, 128, H), dtype=jnp.float32), 'gate_w': sc * jax.random.normal(ks[1], (E, H), dtype=jnp.float32), 'gate_bias': sc * jax.random.normal(ks[2], (E,), dtype=jnp.float32), 'Wg': sc * jax.random.normal(ks[3], (E, I, H), dtype=jnp.float32), 'Wu': sc * jax.random.normal(ks[4], (E, I, H), dtype=jnp.float32), 'Wd': sc * jax.random.normal(ks[5], (E, H, I), dtype=jnp.float32), 'Sg': sc * jax.random.normal(ks[6], (S_I, H), dtype=jnp.float32), 'Su': sc * jax.random.normal(ks[7], (S_I, H), dtype=jnp.float32), 'Sd': sc * jax.random.normal(ks[8], (H, S_I), dtype=jnp.float32)}
    _L0_ffn_in = _L0_ffn_setup()
    _d = {'L0_attn_query': _L0_attn_in['query'], 'L0_attn_W_qkv': _L0_attn_in['W_qkv'], 'L0_attn_b_qkv': _L0_attn_in['b_qkv'], 'L0_attn_W_out': _L0_attn_in['W_out'], 'L0_attn_b_out': _L0_attn_in['b_out'], 'L0_attn_quantum_weights': _L0_attn_in['quantum_weights'], 'L0_attn_photonic_phases': _L0_attn_in['photonic_phases'], 'L0_attn_entanglement_gates': _L0_attn_in['entanglement_gates'], 'L0_attn_superposition_logits': _L0_attn_in['superposition_logits'], 'L0_ffn_gate_w': _L0_ffn_in['gate_w'], 'L0_ffn_gate_bias': _L0_ffn_in['gate_bias'], 'L0_ffn_Wg': _L0_ffn_in['Wg'], 'L0_ffn_Wu': _L0_ffn_in['Wu'], 'L0_ffn_Wd': _L0_ffn_in['Wd'], 'L0_ffn_Sg': _L0_ffn_in['Sg'], 'L0_ffn_Su': _L0_ffn_in['Su'], 'L0_ffn_Sd': _L0_ffn_in['Sd']}
    _x0 = _d['L0_attn_query']
    _d['L0_attn_query'] = jax.random.normal(jax.random.fold_in(jax.random.key(seed), 1), (2, 1024, 128), dtype=_x0.dtype)
    del _x0
    return _d

def reference(L0_attn_query, L0_attn_W_qkv, L0_attn_b_qkv, L0_attn_W_out, L0_attn_b_out, L0_attn_quantum_weights, L0_attn_photonic_phases, L0_attn_entanglement_gates, L0_attn_superposition_logits, L0_ffn_gate_w, L0_ffn_gate_bias, L0_ffn_Wg, L0_ffn_Wu, L0_ffn_Wd, L0_ffn_Sg, L0_ffn_Su, L0_ffn_Sd):

    def _L0_attn_ref(query, W_qkv, b_qkv, W_out, b_out, quantum_weights, photonic_phases, entanglement_gates, superposition_logits):
        import jax, jax.numpy as jnp
        import numpy as np
        EMBED_DIM = 128
        NUM_HEADS = 8
        HEAD_DIM = EMBED_DIM // NUM_HEADS
        NUM_QUBITS = 8
        CIRCUITS = 4
        DEPTH = 3
        WAVELENGTHS = 16
        SCALING = HEAD_DIM ** (-0.5)
        ERR_MIN = 1e-06
        TWO_PI = 2.0 * np.pi

        def _quantum_encode(x, photonic_phases):
            hd = x.shape[-1]
            norm = jnp.sqrt(jnp.sum(x * x, axis=-1, keepdims=True))
            normed = x / jnp.maximum(norm, 1e-12)
            ch = jnp.arange(hd)
            phases = photonic_phases[ch % WAVELENGTHS, ch]
            return normed * jnp.exp(1j * phases)

        def _entangle(state, gates):
            for depth in range(DEPTH):
                g = gates[depth, :NUM_HEADS - 1]
                theta = g[:, 0][None, None, :, None]
                phi = g[:, 1][None, None, :, None]
                s1 = state[:, :, :-1]
                s2 = state[:, :, 1:]
                cos_t = jnp.cos(theta / 2)
                sin_t = jnp.sin(theta / 2)
                ctrl = jnp.abs(s1) ** 2
                rot = cos_t * s2 + sin_t * jnp.exp(1j * phi) * jnp.conj(s2)
                new = ctrl * rot + (1.0 - ctrl) * s2
                state = jnp.concatenate([new, state[:, :, -1:]], axis=2)
            return state

        def _forward(query, W_qkv, b_qkv, W_out, b_out, quantum_weights, photonic_phases, entanglement_gates, superposition_logits):
            B, S, E = query.shape
            qkv = query @ W_qkv.T + b_qkv
            q, k, v = jnp.split(qkv, 3, axis=-1)
            q = q.reshape(B, S, NUM_HEADS, HEAD_DIM)
            k = k.reshape(B, S, NUM_HEADS, HEAD_DIM)
            v = v.reshape(B, S, NUM_HEADS, HEAD_DIM)
            qq = _quantum_encode(q, photonic_phases)
            kq = _quantum_encode(k, photonic_phases)
            vq = _quantum_encode(v, photonic_phases)
            q_ent = _entangle(qq, entanglement_gates)
            k_ent = _entangle(kq, entanglement_gates)
            coh = jnp.exp(1j * jnp.angle(jnp.sum(vq, axis=2, keepdims=True)))
            sup_w = jax.nn.softmax(superposition_logits)
            final = None
            for c in range(CIRCUITS):
                ratio = 0.5 + 0.3 * jnp.sin(quantum_weights[c, 0, 0])
                qa = jnp.sqrt(ratio) * q_ent
                ka = jnp.sqrt(1.0 - ratio) * k_ent
                pattern = jnp.einsum('bsid,bsjd->bsij', jnp.conj(qa), ka)
                mod = pattern * jnp.exp(1j * quantum_weights[c, 1, :])
                scores = jnp.abs(mod) ** 2 * SCALING
                probs = jax.nn.softmax(scores, axis=-1)
                amps = jnp.sqrt(probs + 1e-12)
                coh_phase = jnp.angle(jnp.sum(scores, axis=-1, keepdims=True))
                w = amps * jnp.cos(coh_phase)
                weighted = jnp.einsum('bsij,bsjd->bsid', w.astype(jnp.complex64), vq)
                co = weighted * coh
                amp = jnp.clip(jnp.abs(co), ERR_MIN, 1.0)
                ph = jnp.mod(jnp.angle(co), TWO_PI)
                corrected = amp * jnp.exp(1j * ph)
                contrib = sup_w[c] * corrected
                final = contrib if final is None else final + contrib
            measured = jnp.real(final).reshape(B, S, E)
            return measured @ W_out.T + b_out
        return _forward(query, W_qkv, b_qkv, W_out, b_out, quantum_weights, photonic_phases, entanglement_gates, superposition_logits)

    def _L0_ffn_ref(hidden_states, gate_w, gate_bias, Wg, Wu, Wd, Sg, Su, Sd):
        import jax, jax.numpy as jnp
        import numpy as np
        H = 128
        I = 88
        E = 64
        TOP_K = 8
        NG = 8
        TOPK_GROUP = 4
        N_SHARED = 2
        ROUTED_SCALE = 2.5
        S_I = I * N_SHARED

        def _route(x, gate_w, gate_bias):
            T = x.shape[0]
            logits = x @ gate_w.T
            scores = jax.nn.sigmoid(logits)
            scores_for_choice = scores + gate_bias[None, :]
            grp = scores_for_choice.reshape(T, NG, E // NG)
            group_scores = jnp.sum(jax.lax.top_k(grp, 2)[0], axis=-1)
            _, gidx = jax.lax.top_k(group_scores, TOPK_GROUP)
            gmask = jnp.zeros((T, NG), dtype=scores.dtype).at[jnp.arange(T)[:, None], gidx].set(1.0)
            emask = jnp.repeat(gmask, E // NG, axis=1)
            masked = jnp.where(emask > 0, scores_for_choice, 0.0)
            _, topk_idx = jax.lax.top_k(masked, TOP_K)
            topk_w = jnp.take_along_axis(scores, topk_idx, axis=1)
            topk_w = topk_w / (jnp.sum(topk_w, axis=-1, keepdims=True) + 1e-20)
            topk_w = topk_w * ROUTED_SCALE
            rw = jnp.zeros((T, E), dtype=scores.dtype).at[jnp.arange(T)[:, None], topk_idx].add(topk_w)
            return rw

        def _mlp(x, gw, uw, dw):
            return jax.nn.silu(x @ gw.T) * (x @ uw.T) @ dw.T
        B, S, _ = hidden_states.shape
        x = hidden_states.reshape(B * S, H)
        rw = _route(x, gate_w, gate_bias)
        expert_out = jax.vmap(lambda gw_, uw_, dw_: _mlp(x, gw_, uw_, dw_))(Wg, Wu, Wd)
        routed = jnp.einsum('eth,te->th', expert_out, rw)
        shared = _mlp(x, Sg, Su, Sd)
        out = (routed + shared).reshape(B, S, H)
        return out
    x = L0_attn_query
    x = x + _L0_attn_ref(_layernorm(x, axis=-1), L0_attn_W_qkv, L0_attn_b_qkv, L0_attn_W_out, L0_attn_b_out, L0_attn_quantum_weights, L0_attn_photonic_phases, L0_attn_entanglement_gates, L0_attn_superposition_logits)
    x = x + _L0_ffn_ref(_layernorm(x, axis=-1), L0_ffn_gate_w, L0_ffn_gate_bias, L0_ffn_Wg, L0_ffn_Wu, L0_ffn_Wd, L0_ffn_Sg, L0_ffn_Su, L0_ffn_Sd)
    return x

_drawn_inputs = setup_inputs


def setup_inputs(seed=0):
    import zlib

    import numpy as np

    out = dict(_drawn_inputs(seed))
    spreads = {'L0_attn_b_qkv': (0.0, 0.501), 'L0_attn_b_out': (0.0, 0.1)}
    factors = {'L0_attn_quantum_weights': 8.0,
     'L0_attn_entanglement_gates': 8.0,
     'L0_attn_superposition_logits': 8.0,
     'L0_ffn_gate_w': 8.0,
     'L0_ffn_gate_bias': 8.0,
     'L0_ffn_Wg': 8.0,
     'L0_ffn_Wu': 8.0,
     'L0_ffn_Wd': 8.0,
     'L0_ffn_Sg': 8.0,
     'L0_ffn_Su': 8.0,
     'L0_ffn_Sd': 8.0}
    for name, (base, spread) in spreads.items():
        noise = np.random.default_rng([zlib.crc32(name.encode()), seed]).standard_normal(out[name].shape)
        drawn = base * np.exp(spread * noise) if base else spread * noise
        out[name] = jnp.asarray(drawn.astype(out[name].dtype))
    for name, factor in factors.items():
        out[name] = (out[name] * factor).astype(out[name].dtype)
    return out
```

```python
from contextlib import ExitStack

import numpy as np

import concourse.bass as bass
from concourse import mybir

F32 = mybir.dt.float32
F32R = mybir.dt.float32r
U32 = mybir.dt.uint32
ALU = mybir.AluOpType
ACT = mybir.ActivationFunctionType
AX = mybir.AxisListType

P = 128
T, E = 2048, 128
HEADS, D, CIRC, DEPTH = 8, 16, 4, 3
CHUNK = 512
NCHUNK = T // CHUNK
S = CHUNK // P
TILES = T // P
N4 = 4
NP = P // N4
NE, NI, NG, TOPG, TOPK = 64, 88, 8, 4, 8
SCALING = D ** -0.5
LN_EPS = 1e-5
PI = float(np.pi)
TWO_PI_A = 6.28125
TWO_PI_B = float(np.float32(2 * np.pi - 6.28125).view(np.uint32) & 0xFFFFF000) and float(
    (np.array([2 * np.pi - 6.28125], np.float32).view(np.uint32) & np.uint32(0xFFFFF000)).view(np.float32)[0])
TWO_PI_C = float(2 * np.pi - TWO_PI_A - TWO_PI_B)
ROUND = 1.5 * 2.0 ** 23
PI_SAFE = 3.1415925
TAKEN = -3.0e38

ROWS = NE * NI
MT = ROWS // P
PERIOD = 11
PERIODS = MT // PERIOD
EXPERTS = PERIOD * P // NI
SHARED = 2 * NI
LAG = 3
UNITS = PERIOD * NCHUNK

A_HALF, A_PREV, A_PHASE, A_PHASE2, A_CIRC = 0, 3, 6, 7, 8
NANG = 12


def segments():
    out = []
    for b in range(PERIOD):
        r = 0
        while r < P:
            e = (b * P + r) // NI
            n = min(P - r, (e + 1) * NI - (b * P + r))
            out.append((b, r, n, e))
            r += n
    return out


class Chain:

    def __init__(self, eng, sem, base, i):
        self.eng, self.sem, self.base, self.i, self.k = eng, sem, base, i, 0
        self.per = 0

    def at(self, per, i, first=0):
        self.per, self.i, self.k, self.first = per, i, 0, first
        return self

    def step(self, ins):
        ins.then_inc(self.sem, 1)
        self.k += 1
        return self.k

    def after(self, k):
        self.eng.wait_ge(self.sem, self.first + self.i * self.per + k)

    def link(self, ins):
        self.after(self.step(ins))


DVE_STEPS = 67




def build(nc, x_d, wqkv_d, bqkv_d, wout_d, bout_d, qw_d, phase_d, gates_d, logit_d,
          gw_d, gbias_d, wpack_d, out_d, counts):
    x_rows = x_d.rearrange("b s e -> (b s) e")
    out_rows = out_d.rearrange("b s e -> (b s) e")

    def dram(name, shape):
        return nc.dram_tensor(name, shape, F32, kind="Internal").ap()

    v_d = dram("v_rows", [T, E])
    k_d = dram("k_strips", [NCHUNK, S, 2, D, HEADS, P])
    q_d = dram("q_strips", [NCHUNK, S, 2, D, 2, HEADS, P])
    rw_d = dram("rw_rows", [NE, T])

    with ExitStack() as whole:
        def sem(name):
            return whole.enter_context(nc.semaphore(name))

        def keep(name, shape, dt=F32):
            return whole.enter_context(nc.sbuf_tensor(name, shape, dt))

        x = keep("x", [P, TILES, E])
        xhi = keep("xhi", [E, T], F32R)
        xlo = keep("xlo", [E, T], F32R)
        ident = keep("ident", [P, P])
        bank = [whole.enter_context(nc.psum_tensor(f"bank{n}", [P, 512], F32)) for n in range(8)]

        attention(nc, x_rows, wqkv_d, bqkv_d, wout_d, bout_d, qw_d, phase_d, gates_d, logit_d,
                  gw_d, gbias_d, v_d, k_d, q_d, rw_d, x, xhi, xlo, ident, bank, counts)
        experts(nc, wpack_d, rw_d, out_rows, x, xhi, xlo, ident, bank)


def attention(nc, x_rows, wqkv_d, bqkv_d, wout_d, bout_d, qw_d, phase_d, gates_d, logit_d,
              gw_d, gbias_d, v_d, k_d, q_d, rw_d, x, xhi, xlo, ident, bank, counts):
    with ExitStack() as ctx:
        def sb(name, shape, dt=F32):
            return ctx.enter_context(nc.sbuf_tensor(name, shape, dt))

        def sem(name):
            return ctx.enter_context(nc.semaphore(name))

        wqkv = sb("wqkv", [E, 3 * E])
        bqkv = sb("bqkv", [P, 3 * E])
        gwt = sb("gwt", [E, NE])
        gbias = sb("gbias", [P, NE])
        wout = sb("wout", [P, HEADS, 2, E])
        wout_in = sb("wout_in", [P, HEADS, E])
        bout = sb("bout", [E, 1])
        qw = sb("qw", [P, CIRC])
        logit = sb("logit", [P, CIRC])
        phase = sb("phase", [P, 1])
        gates = sb("gates", [P, DEPTH, 2, 2])
        own_head = sb("own_head", [P, 1])
        shift = sb("shift", [P, P])
        stay = sb("stay", [P, P])
        maps = sb("maps", [P, DEPTH, 3, P])
        ang = sb("ang", [P, 2, NANG])
        turns = sb("turns", [P, 2, NANG])
        sc = sb("sc", [P, 2, NANG])
        gain = sb("gain", [P, DEPTH, 2])
        ratio = sb("ratio", [P, CIRC])
        coef = sb("coef", [P, CIRC])
        coef_t = sb("coef_t", [P, CIRC])
        sup = sb("sup", [P, CIRC])
        sup_s = sb("sup_s", [P, 4])
        eps = sb("eps", [P, 2])
        tick = sb("tick", [P, 16])
        pair_sum = sb("pair_sum", [P, 32])
        pair_back = sb("pair_back", [P, 4, P])
        half_sel = sb("half_sel", [P, 2])
        before = sb("before", [P, NG, NG])
        st = sb("st", [P, S, 6])
        mv = sb("mv", [P, S, 2])
        std = sb("std", [P, S])
        rstd = sb("rstd", [P, S])
        rt = sb("rt", [P, S])
        xn = sb("xn", [P, S, E])
        xnT = sb("xnT", [E, CHUNK])
        qkv = sb("qkv", [P, S, 3 * HEADS, D])
        sq = sb("sq", [P, S, 3 * HEADS, D])
        ss = sb("ss", [P, S * 3 * HEADS])
        rn = sb("rn", [P, S * 3 * HEADS])
        vs = sb("vs", [P, S, D])
        vg = sb("vg", [P, S, D])
        vsg = sb("vsg", [P, S, HEADS, D])
        state = {(w, a): sb(f"state_{w}{a}", [P, CHUNK]) for w in "qk" for a in "xy"}
        sqr = {(w, a): sb(f"sqr_{w}{a}", [P, CHUNK]) for w in "qk" for a in "xy"}
        ctrl = {w: sb(f"ctrl_{w}", [P, CHUNK]) for w in "qk"}
        gain_t = {(w, a): sb(f"gain_{w}{a}", [P, CHUNK]) for w in "qk" for a in "xy"}
        fin = {(w, a): sb(f"fin_{w}{a}", [P, CHUNK]) for w, a in ("qx", "qy", "kx", "ky")}
        fin_nqy = sb("fin_nqy", [P, CHUNK])
        kbd = sb("kbd", [P, S, HEADS, P])
        qs = sb("qs", [P, 2, HEADS, P])
        vbd = sb("vbd", [P, NP, 8, D])
        psq = sb("psq", [P, NP, 2, HEADS])
        pt = sb("pt", [P, NP, HEADS])
        mx = sb("mx", [P, 2, 16])
        mb = sb("mb", [P, 2, 16, 8])
        dm = sb("dm", [P, NP, HEADS])
        ex = sb("ex", [P, NP, CIRC, HEADS])
        rz = sb("rz", [P, 256])
        pr = sb("pr", [P, NP, CIRC, HEADS])
        am = sb("am", [P, NP, CIRC, HEADS])
        amp = sb("amp", [P, 2, NP, CIRC, HEADS])
        mix = sb("mix", [P, 2 * NP, HEADS])
        yT = sb("yT", [E, S, NP, N4])
        xn2 = sb("xn2", [P, S, E])
        xn2T = sb("xn2T", [E, CHUNK])
        lg = sb("lg", [P, S, NE])
        el = sb("el", [P, S, NE])
        e1 = sb("e1", [P, S, NE])
        score = sb("score", [P, S, NE])
        choice = sb("choice", [P, S, NG, NE // NG])
        top = sb("top", [P, S, NG, 8])
        gs = sb("gs", [P, S, NG])
        gt = sb("gt", [P, S, NG, NG])
        ge = sb("ge", [P, S, NG, NG])
        rank = sb("rank", [P, S, NG])
        gm = sb("gm", [P, S, NG])
        masked = sb("masked", [P, S, NE])
        best = sb("best", [P, S, 8])
        rest = sb("rest", [P, S, NE])
        picked = sb("picked", [P, S, NE])
        wsum = sb("wsum", [P, S])
        wr = sb("wr", [P, S])
        rw = sb("rw", [P, S, NE])
        rwT = sb("rwT", [P, 2 * P])

        x_in, small_in, w_in = sem("x_in"), sem("small_in"), sem("w_in")
        v_stored, v_loaded = sem("v_stored"), sem("v_loaded")
        k_stored, k_loaded = sem("k_stored"), sem("k_loaded")
        q_stored, q_loaded = sem("q_stored"), sem("q_loaded")
        rw_stored = sem("rw_stored")
        consts, angles, sines, tables_ready, sup_exp = (
            sem(n) for n in ("consts", "angles", "sines", "tables_ready", "sup_exp"))
        dve_s, act_s, pool_s = sem("dve_steps"), sem("act_steps"), sem("pool_steps")
        (var1, std1, xn_ready, xT_ps, xT_ready, qkv_ps, qkv_ready, sq_ready, ss_ready, norm_ready,
         qk_ready, vsg_ready, qkT_ps, r_ready) = (sem(n) for n in (
             "var1", "std1", "xn_ready", "xT_ps", "xT_ready", "qkv_ps", "qkv_ready", "sq_ready", "ss_ready",
             "norm_ready", "qk_ready", "vsg_ready", "qkT_ps", "r_ready"))
        z_ps = {w: sem(f"z_ps_{w}") for w in "qk"}
        sqr_ready = {w: sem(f"sqr_ready_{w}") for w in "qk"}
        ctrl_ready = {w: sem(f"ctrl_ready_{w}") for w in "qk"}
        gain_ready = {w: sem(f"gain_ready_{w}") for w in "qk"}
        state_ready = {w: sem(f"state_ready_{w}") for w in "qk"}
        neg_ready, abs_ready = sem("neg_ready"), sem("abs_ready")
        (pat_ps, psq_ready, pt_ready, ptT_ps, mb_ready, mbT_ps, dm_ready, ex_ready, z_sum, rz_ready, rz_ps,
         pr_ready, am_ready, r_ps, amp_ready, mix_ready, y_ps, y_ready, yT_ps, x1_ready) = (sem(n) for n in (
             "pat_ps", "psq_ready", "pt_ready", "ptT_ps", "mb_ready", "mbT_ps", "dm_ready", "ex_ready", "z_sum",
             "rz_ready", "rz_ps", "pr_ready", "am_ready", "r_ps", "amp_ready", "mix_ready", "y_ps", "y_ready",
             "yT_ps", "x1_ready"))
        (var2, std2, xn2_ready, xn2T_ps, xn2T_ready, lg_ps, lg_ready, el_ready, rw_ready, rwT_ps,
         rwT_ready) = (sem(n) for n in (
             "var2", "std2", "xn2_ready", "xn2T_ps", "xn2T_ready", "lg_ps", "lg_ready", "el_ready", "rw_ready",
             "rwT_ps", "rwT_ready"))

        block = ctx.enter_context(nc.Block())

        @block.sync
        def _(sp):
            sp.dma_start(x[:, :, :], x_rows.rearrange("(t p) e -> p t e", p=P)).then_inc(x_in, 16)
            sp.dma_start(wqkv[:, :], wqkv_d).then_inc(w_in, 16)
            sp.dma_start(bqkv[:, :], bqkv_d).then_inc(w_in, 16)
            sp.dma_start(gwt[:, :], gw_d).then_inc(w_in, 16)
            sp.dma_start(gbias[:, :], gbias_d).then_inc(w_in, 16)
            with sp.Fori(0, NCHUNK) as i:
                sp.wait_ge(vsg_ready, i + 1)
                rows = v_d[bass.ds(i * CHUNK, CHUNK), :]
                sp.dma_start(rows.rearrange("(s n) e -> n s e", n=P),
                             vsg[:, :, :, :].rearrange("p s h d -> p s (h d)")).then_inc(v_stored, 16)
                sp.wait_ge(v_stored, i * 16 + 16)
                back = rows.rearrange("(s n f) (j d) -> s f j n d", s=S, f=N4, j=HEADS)
                for s in range(S):
                    for f in range(N4):
                        p0, t8 = 32 * f + 8 * s, (f % 2) * 4 + s
                        sp.dma_start(vbd[p0:p0 + HEADS, :, t8, :], back[s, f]).then_inc(v_loaded, 16)
                kc, qc = k_d[bass.ds(i, 1)], q_d[bass.ds(i, 1)]

                def put(dst, src, done):
                    for s in range(S):
                        sp.dma_start(dst[s], src[:, s * P:(s + 1) * P]).then_inc(done, 16)

                kv = kc.rearrange("a s c d h n -> (a s) c h d n")
                qv = qc.rearrange("a s c d v h n -> (a s) c v h d n")
                sp.wait_ge(state_ready["k"], i * 6 + 6)
                put([kv[s, 0] for s in range(S)], fin["k", "x"], k_stored)
                put([kv[s, 1] for s in range(S)], fin["k", "y"], k_stored)
                sp.wait_ge(state_ready["q"], i * 6 + 6)
                put([qv[s, 0, 0] for s in range(S)], fin["q", "x"], q_stored)
                put([qv[s, 1, 0] for s in range(S)], fin["q", "y"], q_stored)
                put([qv[s, 1, 1] for s in range(S)], fin["q", "x"], q_stored)
                sp.wait_ge(neg_ready, i + 1)
                put([qv[s, 0, 1] for s in range(S)], fin_nqy, q_stored)
                sp.wait_ge(k_stored, i * 16 * 2 * S + 16 * 2 * S)
                kb = kc.rearrange("a s c d h n -> (a s) (c d) (h n)")
                for s in range(S):
                    sp.dma_start(kbd[32 * s:32 * s + 32, s, :, :].rearrange("p h n -> p (h n)"), kb[s])\
                        .then_inc(k_loaded, 16)
                sp.wait_ge(q_stored, i * 16 * 4 * S + 16 * 4 * S)
                sp.dma_start(qs[:, :, :, :].rearrange("p v h n -> p (v h n)"),
                             qc.rearrange("a s c d v h n -> (a s c d) (v h n)")).then_inc(q_loaded, 16)
                sp.wait_ge(rwT_ready, i + 1)
                sp.nop(nofuse=True)
                rv = rw_d[:, bass.ds(i * CHUNK, CHUNK)].rearrange("e (b s n) -> s e b n", b=S // 2, s=2)
                for s in range(2):
                    sp.dma_start(rv[s], rwT[s * NE:(s + 1) * NE, :].rearrange("p (b n) -> p b n", b=S // 2))\
                        .then_inc(rw_stored, 16)
            sp.wait_ge(rw_stored, 16 * 2 * NCHUNK)

        @block.gpsimd
        def _(pool):
            c = Chain(pool, pool_s, 0, 0).at(0, 0)
            g = nc.gpsimd
            c.link(g.memset(ident[:, :], 0.0))
            c.link(g.affine_select(out=ident[:, :], in_=ident[:, :], compare_op=ALU.not_equal, fill=1.0,
                                   base=0, pattern=[[-1, P]], channel_multiplier=1))
            c.link(g.memset(shift[:, :], 0.0))
            c.link(g.affine_select(out=shift[:, :], in_=shift[:, :], compare_op=ALU.not_equal, fill=1.0,
                                   base=-D, pattern=[[-1, P]], channel_multiplier=1))
            c.link(g.memset(own_head[:, :], 1.0))
            c.link(g.affine_select(out=own_head[:, :], in_=own_head[:, :], compare_op=ALU.is_gt, fill=0.0,
                                   base=(HEADS - 1) * D, pattern=[[0, 1]], channel_multiplier=-1))
            c.link(g.affine_select(out=stay[:, :], in_=ident[:, :], compare_op=ALU.is_ge, fill=0.0,
                                   base=-(HEADS - 1) * D, pattern=[[0, P]], channel_multiplier=1))
            c.link(g.memset(pair_sum[:, :], 1.0))
            pv = pair_sum[:, :].rearrange("p (a m) -> p a m", a=2)
            c.link(g.affine_select(out=pv, in_=pv, compare_op=ALU.is_ge, fill=0.0, base=0,
                                   pattern=[[0, 2], [-8, 16]], channel_multiplier=1))
            c.link(g.affine_select(out=pv, in_=pv, compare_op=ALU.is_gt, fill=0.0, base=8,
                                   pattern=[[0, 2], [8, 16]], channel_multiplier=-1))
            c.link(g.memset(pair_back[:, :, :], 1.0))
            c.link(g.affine_select(out=pair_back[:, :, :], in_=pair_back[:, :, :], compare_op=ALU.is_ge, fill=0.0,
                                   base=0, pattern=[[256, 4], [1, P]], channel_multiplier=-8))
            c.link(g.affine_select(out=pair_back[:, :, :], in_=pair_back[:, :, :], compare_op=ALU.is_gt, fill=0.0,
                                   base=8, pattern=[[-256, 4], [-1, P]], channel_multiplier=8))
            hs = half_sel
            c.link(g.iota(turns[:, 0, 0:1], pattern=[[0, 1]], base=0, channel_multiplier=1,
                          allow_small_or_imprecise_dtypes=True))
            c.link(g.memset(before[:, :, :], 1.0))
            c.link(g.affine_select(out=before[:, :, :], in_=before[:, :, :], compare_op=ALU.is_gt, fill=0.0,
                                   base=0, pattern=[[1, NG], [-1, NG]], channel_multiplier=0))
            c.link(g.memset(eps[:, 0:1], LN_EPS))
            c.link(g.memset(eps[:, 1:2], 1e-12))
            c.link(g.memset(tick[:, :], 0.0))
            c.link(g.memset(kbd[:, :, :, :], 0.0))
            c.link(g.memset(vbd[:, :, :, :], 0.0))
            counts.append(("POOL_SETUP", c.k))
            g.memset(hs[:, :], 0.0).then_inc(consts, 1)
            pool.wait_ge(tables_ready, 1)
            with pool.Fori(0, NCHUNK) as i:
                for k in range(DEPTH):
                    for w in "qk":
                        pool.wait_ge(ctrl_ready[w], i * DEPTH + k + 1)
                        n = 4 + 2 * k + "qk".index(w)
                        g.tensor_tensor(tick[:, n:n + 1], tick[:, 2:3], tick[:, 2:3], ALU.add)
                        for a in range(2):
                            g.tensor_scalar(gain_t[w, "xy"[a]][:, :], ctrl[w][:, :], gain[:, k, a:a + 1], 1.0,
                                            ALU.mult, ALU.add).then_inc(gain_ready[w], 1)

        @block.vector
        def _(dve):
            v = nc.vector
            c = Chain(dve, dve_s, 0, 0).at(0, 0)
            dve.wait_ge(small_in, 16 * 7)
            dve.wait_ge(consts, 1)
            row = turns[:, 0, 0:1]
            c.link(v.tensor_scalar(turns[:, 0, 1:2], row, -7.5, 1.0 / 16, ALU.add, ALU.mult))
            c.link(v.tensor_scalar(turns[:, 0, 2:3], turns[:, 0, 1:2], ROUND, ROUND, ALU.add, ALU.subtract))
            c.link(v.tensor_scalar(turns[:, 0, 3:4], turns[:, 0, 2:3], -0.5, 0.5, ALU.add, ALU.mult))
            c.link(v.tensor_scalar(turns[:, 0, 4:5], turns[:, 0, 3:4], ROUND, ROUND, ALU.add, ALU.subtract))
            c.link(v.scalar_tensor_tensor(out=half_sel[:, 1:2], in0=turns[:, 0, 4:5], scalar=-2.0,
                                          in1=turns[:, 0, 2:3], op0=ALU.mult, op1=ALU.add))
            c.link(v.tensor_scalar(half_sel[:, 0:1], half_sel[:, 1:2], -1.0, 1.0, ALU.mult, ALU.add))
            own, prev = gates[:, :, 0, :], gates[:, :, 1, :]
            c.link(v.tensor_scalar(ang[:, 0, A_HALF:A_HALF + 3], own[:, :, 0], 0.5, None, ALU.mult))
            c.link(v.tensor_scalar(ang[:, 0, A_PREV:A_PREV + 3], prev[:, :, 1], -0.5, None, ALU.mult))
            c.link(v.tensor_scalar(turns[:, 0, 0:3], own[:, :, 1], own_head[:, 0:1], 0.5, ALU.mult, ALU.mult))
            c.link(v.tensor_tensor(ang[:, 0, A_PREV:A_PREV + 1], ang[:, 0, A_PREV:A_PREV + 1], phase[:, :],
                                   ALU.add))
            c.link(v.tensor_tensor(ang[:, 0, A_PREV + 1:A_PREV + 3], ang[:, 0, A_PREV + 1:A_PREV + 3],
                                   turns[:, 0, 0:2], ALU.add))
            c.link(v.tensor_copy(ang[:, 0, A_PHASE:A_PHASE + 1], phase[:, :]))
            c.link(v.tensor_scalar(ang[:, 0, A_PHASE2:A_PHASE2 + 1], phase[:, :], 2.0, None, ALU.mult))
            c.link(v.tensor_copy(ang[:, 0, A_CIRC:A_CIRC + CIRC], qw[:, :]))
            c.link(v.tensor_scalar(ang[:, 1, :], ang[:, 0, :], PI / 2, None, ALU.add))
            c.link(v.tensor_scalar(turns[:, :, :], ang[:, :, :], 1 / (2 * PI), ROUND, ALU.mult, ALU.add))
            c.link(v.tensor_scalar(turns[:, :, :], turns[:, :, :], ROUND, None, ALU.subtract))
            for part in (TWO_PI_A, TWO_PI_B, TWO_PI_C):
                c.link(v.scalar_tensor_tensor(out=ang[:, :, :], in0=turns[:, :, :], scalar=-part,
                                              in1=ang[:, :, :], op0=ALU.mult, op1=ALU.add))
            v.tensor_scalar(ang[:, :, :], ang[:, :, :], PI_SAFE, -PI_SAFE, ALU.min, ALU.max).then_inc(angles, 1)
            c.link(v.tensor_reduce(sup_s[:, 0:1], logit[:, :], AX.X, ALU.max))
            v.tensor_scalar(sup[:, :], logit[:, :], sup_s[:, 0:1], None, ALU.subtract).then_inc(sup_exp, 1)
            dve.wait_ge(sup_exp, 2)
            c.link(v.tensor_reduce(sup_s[:, 1:2], ratio[:, :], AX.X, ALU.add))
            c.link(v.reciprocal(sup_s[:, 2:3], sup_s[:, 1:2]))
            c.link(v.tensor_scalar(sup[:, :], ratio[:, :], sup_s[:, 2:3], None, ALU.mult))
            dve.wait_ge(sines, 1)
            sin, cos = sc[:, 0, :], sc[:, 1, :]
            c.link(v.tensor_tensor(gain[:, :, 0], cos[:, A_HALF:A_HALF + 3], sin[:, A_HALF:A_HALF + 3], ALU.add))
            c.link(v.tensor_tensor(gain[:, :, 1], cos[:, A_HALF:A_HALF + 3], sin[:, A_HALF:A_HALF + 3],
                                   ALU.subtract))
            c.link(v.tensor_scalar(gain[:, :, :], gain[:, :, :], -1.0, own_head[:, 0:1], ALU.add, ALU.mult))
            c.link(v.tensor_scalar(coef_t[:, :], sin[:, A_CIRC:A_CIRC + CIRC], 0.3, 0.5, ALU.mult, ALU.add))
            c.link(v.tensor_scalar(coef[:, :], coef_t[:, :], -SCALING, SCALING, ALU.mult, ALU.add))
            c.link(v.tensor_tensor(coef[:, :], coef[:, :], coef_t[:, :], ALU.mult))
            for k in range(DEPTH):
                col = A_PREV + k
                c.link(v.tensor_scalar(maps[:, k, 0, :], shift[:, :], cos[:, col:col + 1], None, ALU.mult))
                c.link(v.tensor_scalar(maps[:, k, 1, :], shift[:, :], sin[:, col:col + 1], None, ALU.mult))
                if k == 0:
                    for a, part in ((0, cos), (1, sin)):
                        c.link(v.scalar_tensor_tensor(out=maps[:, k, a, :], in0=stay[:, :],
                                                      scalar=part[:, A_PHASE:A_PHASE + 1], in1=maps[:, k, a, :],
                                                      op0=ALU.mult, op1=ALU.add))
                else:
                    c.link(v.tensor_tensor(maps[:, k, 0, :], maps[:, k, 0, :], stay[:, :], ALU.add))
                c.link(v.tensor_scalar(maps[:, k, 2, :], maps[:, k, 1, :], -1.0, None, ALU.mult))
            c.link(v.tensor_scalar(wout_in[:, :, :], wout_in[:, :, :], cos[:, A_PHASE2:A_PHASE2 + 1], None,
                                   ALU.mult))
            for t2 in range(2):
                c.link(v.tensor_scalar(wout[:, :, t2, :], wout_in[:, :, :], half_sel[:, t2:t2 + 1], None,
                                       ALU.mult))
            v.tensor_scalar(sup_s[:, 3:4], sup_s[:, 2:3], 1.0, None, ALU.mult).then_inc(tables_ready, 1)
            dve.wait_ge(tables_ready, 1)
            setup = c.k
            counts.append(("DVE_SETUP", setup))
            dve.wait_ge(x_in, 16)
            dve.wait_ge(w_in, 16 * 4)

            def carry():
                v.tensor_copy(tick[:, 1:2], tick[:, 0:1])

            def layer_norm(i, c, dst, var, std_ready, ready):
                carry()
                for s in range(S):
                    k = c.step(v.bn_stats(st[:, s, :], x[:, bass.ds(i * S + s, 1), :].rearrange("p a e -> p (a e)")))
                c.after(k)
                carry()
                for s in range(S):
                    k = c.step(v.bn_aggr(mv[:, s, :], st[:, s, :]))
                c.after(k)
                v.tensor_scalar(rt[:, :], mv[:, :, 1], LN_EPS, None, ALU.add).then_inc(var, 1)
                dve.wait_ge(std_ready, i + 1)
                c.link(v.reciprocal(rstd[:, :], std[:, :]))
                c.link(v.tensor_tensor(rt[:, :], rt[:, :], rstd[:, :], ALU.mult))
                c.link(v.tensor_tensor(rt[:, :], rt[:, :], rstd[:, :], ALU.mult))
                c.link(v.tensor_scalar(rt[:, :], rt[:, :], -0.5, 1.5, ALU.mult, ALU.add))
                c.link(v.tensor_tensor(rstd[:, :], rstd[:, :], rt[:, :], ALU.mult))
                for s in range(S):
                    ins = v.tensor_scalar(dst[:, s, :], x[:, bass.ds(i * S + s, 1), :].rearrange("p a e -> p (a e)"),
                                          mv[:, s, 0:1], rstd[:, s:s + 1], ALU.subtract, ALU.mult)
                    ins.then_inc(ready, 1)

            with dve.Fori(0, NCHUNK) as i:
                c = Chain(dve, dve_s, 0, 0).at(DVE_STEPS, i, setup)
                layer_norm(i, c, xn, var1, std1, xn_ready)
                for s in range(S):
                    dve.wait_ge(qkv_ps, i * S + s + 1)
                    v.tensor_tensor(qkv[:, s, :, :].rearrange("p h d -> p (h d)"), bank[(3, 4, 5, 2)[s]][:, 0:3 * E],
                                    bqkv[:, :], ALU.add).then_inc(qkv_ready, 1)
                dve.wait_ge(sq_ready, i + 1)
                c.link(v.tensor_reduce(ss[:, :], sq[:, :, :, :].rearrange("p s h d -> p (s h) d"), AX.X, ALU.add))
                v.tensor_scalar(ss[:, :], ss[:, :], 1e-24, None, ALU.max).then_inc(ss_ready, 1)
                dve.wait_ge(norm_ready, i + 1)
                c.link(v.reciprocal(rn[:, :], rn[:, :]))
                rnv = rn[:, :].rearrange("p (s h) -> p s h", s=S)
                for a in range(3):
                    h0 = a * HEADS
                    part = qkv[:, :, h0:h0 + HEADS, :]
                    ins = v.tensor_tensor(part, part,
                                          rnv[:, :, h0:h0 + HEADS].unsqueeze(3).to_broadcast([P, S, HEADS, D]),
                                          ALU.mult)
                    if a < 2:
                        ins.then_inc(qk_ready, 1)
                    else:
                        c.link(ins)
                vals = qkv[:, :, 2 * HEADS:3 * HEADS, :]
                c.link(v.tensor_reduce(vs[:, :, :], vals.rearrange("p s h d -> p s d h"), AX.X, ALU.add))
                c.link(v.tensor_scalar(vg[:, :, :], vs[:, :, :], 0.0, 2.0, ALU.is_ge, ALU.mult))
                c.link(v.tensor_scalar(vg[:, :, :], vg[:, :, :], 1.0, None, ALU.subtract))
                v.tensor_tensor(vsg[:, :, :, :], vals,
                                vg[:, :, :].unsqueeze(2).to_broadcast([P, S, HEADS, D]), ALU.mult)\
                    .then_inc(vsg_ready, 1)
                for k in range(DEPTH):
                    for w, b in (("q", 2), ("k", 4)):
                        if k:
                            dve.wait_ge(sqr_ready[w], i * (DEPTH - 1) + k)
                            v.tensor_tensor(ctrl[w][:, :], sqr[w, "x"][:, :], sqr[w, "y"][:, :], ALU.add)\
                                .then_inc(ctrl_ready[w], 1)
                    for w, b in (("q", 2), ("k", 4)):
                        for a in range(2):
                            dve.wait_ge(z_ps[w], i * 6 + 2 * k + 2)
                            dve.wait_ge(gain_ready[w], i * 6 + 2 * k + a + 1)
                            dst = (fin if k == DEPTH - 1 else state)[w, "xy"[a]]
                            v.tensor_tensor(dst[:, :], bank[b + a][:, :], gain_t[w, "xy"[a]][:, :], ALU.mult)\
                                .then_inc(state_ready[w], 1)
                dve.wait_ge(psq_ready, i + 1)
                v.tensor_tensor(pt[:, :, :], psq[:, :, 0, :], psq[:, :, 1, :], ALU.add).then_inc(pt_ready, 1)
                dve.wait_ge(ptT_ps, i + 1)
                c.link(v.tensor_reduce(mx[:, :, :], bank[7][:, 0:256].rearrange("p (b m j) -> p b m j", b=2, j=8),
                                       AX.X, ALU.max))
                v.tensor_copy(mb[:, :, :, :], mx[:, :, :].unsqueeze(3).to_broadcast([P, 2, 16, 8]))\
                    .then_inc(mb_ready, 1)
                dve.wait_ge(mbT_ps, i + 1)
                v.tensor_tensor(dm[:, :, :].rearrange("p n h -> p (n h)"), pt[:, :, :].rearrange("p n h -> p (n h)"),
                                bank[6][:, 0:256], ALU.subtract).then_inc(dm_ready, 1)
                dve.wait_ge(z_sum, i + 1)
                v.reciprocal(rz[:, :], bank[7][:, 0:256]).then_inc(rz_ready, 1)
                dve.wait_ge(rz_ps, i + 1)
                for g in range(4):
                    v.tensor_tensor(pr[:, 8 * g:8 * g + 8, :, :].rearrange("p n c h -> p (n c h)"),
                                    ex[:, 8 * g:8 * g + 8, :, :].rearrange("p n c h -> p (n c h)"),
                                    bank[g // 2][:, (g % 2) * 256:(g % 2) * 256 + 256], ALU.mult)\
                        .then_inc(pr_ready, 1)
                for r in range(2):
                    dve.wait_ge(r_ps, i * 2 + r + 1)
                    for h in range(2):
                        part = amp[:, h, 16 * r:16 * r + 16, :, :].rearrange("p n c h -> p (n c h)")
                        src = bank[(0, 1)[h] if r else (6, 7)[h]]
                        dve.wait_ge(abs_ready, i * 4 + 2 * r + h + 1)
                        c.link(v.tensor_scalar(part, part, 1e-6, 1.0, ALU.max, ALU.min))
                        ins = v.scalar_tensor_tensor(out=part.bitcast(U32), in0=src[:, :].bitcast(U32),
                                                     scalar=0x80000000, in1=part.bitcast(U32),
                                                     op0=ALU.bitwise_and, op1=ALU.bitwise_or)
                        ins.then_inc(amp_ready, 1)
                dve.wait_ge(amp_ready, i * 4 + 4)
                av = amp[:, :, :, :, :].rearrange("p h n c i -> p (h n) c i")
                c.link(v.tensor_scalar(mix[:, :, :], av[:, :, 0, :], sup[:, 0:1], None, ALU.mult))
                for q in range(1, CIRC):
                    ins = v.scalar_tensor_tensor(out=mix[:, :, :], in0=av[:, :, q, :], scalar=sup[:, q:q + 1],
                                                 in1=mix[:, :, :], op0=ALU.mult, op1=ALU.add)
                    if q < CIRC - 1:
                        c.link(ins)
                    else:
                        ins.then_inc(mix_ready, 1)
                dve.wait_ge(yT_ps, i + 1)
                xi = x[:, bass.ds(i * S, S), :]
                v.tensor_tensor(xi, xi, bank[7][:, :].rearrange("p (s e) -> p s e", s=S), ALU.add)\
                    .then_inc(x1_ready, 1)
                dve.wait_ge(x1_ready, i + 1)
                layer_norm(i, c, xn2, var2, std2, xn2_ready)
                dve.wait_ge(xn2T_ready, i + 1)
                hi = xhi[:, bass.ds(i * CHUNK, CHUNK)]
                c.link(v.tensor_copy(hi, xn2T[:, :]))
                c.step(v.tensor_tensor(xlo[:, bass.ds(i * CHUNK, CHUNK)], xn2T[:, :], hi.bitcast(F32), ALU.subtract))
                dve.wait_ge(lg_ps, i + 1)
                v.tensor_scalar(lg[:, :, :].rearrange("p s e -> p (s e)"), bank[1][:, 0:S * NE], -87.0, None,
                                ALU.max).then_inc(lg_ready, 1)
                dve.wait_ge(el_ready, i + 1)
                c.link(v.tensor_scalar(e1[:, :, :], el[:, :, :], 1.0, None, ALU.add))
                c.link(v.reciprocal(score[:, :, :], e1[:, :, :]))
                c.link(v.tensor_tensor(choice[:, :, :, :].rearrange("p s g k -> p s (g k)"), score[:, :, :],
                                       gbias[:, :].unsqueeze(1).to_broadcast([P, S, NE]), ALU.add))
                carry()
                for s in range(S):
                    for g in range(NG):
                        ins = v.max(top[:, s, g, :], choice[:, s, g, :])
                c.link(ins)
                c.link(v.tensor_tensor(gs[:, :, :], top[:, :, :, 0], top[:, :, :, 1], ALU.add))
                other = gs[:, :, :].unsqueeze(2).to_broadcast([P, S, NG, NG])
                own_g = gs[:, :, :].unsqueeze(3).to_broadcast([P, S, NG, NG])
                c.step(v.tensor_tensor(gt[:, :, :, :], other, own_g, ALU.is_gt))
                c.link(v.tensor_tensor(ge[:, :, :, :], other, own_g, ALU.is_equal))
                c.link(v.tensor_tensor(ge[:, :, :, :].rearrange("p s g k -> p s (g k)"),
                                       ge[:, :, :, :].rearrange("p s g k -> p s (g k)"),
                                       before[:, :, :].rearrange("p g k -> p (g k)").unsqueeze(1)
                                       .to_broadcast([P, S, NG * NG]), ALU.mult))
                c.link(v.tensor_tensor(gt[:, :, :, :], gt[:, :, :, :], ge[:, :, :, :], ALU.add))
                c.link(v.tensor_reduce(rank[:, :, :], gt[:, :, :, :], AX.X, ALU.add))
                c.link(v.tensor_scalar(gm[:, :, :], rank[:, :, :], TOPG - 0.5, None, ALU.is_lt))
                c.link(v.tensor_tensor(masked[:, :, :].rearrange("p s (g k) -> p s g k", g=NG), choice[:, :, :, :],
                                       gm[:, :, :].unsqueeze(3).to_broadcast([P, S, NG, NE // NG]), ALU.mult))
                carry()
                for s in range(S):
                    k = c.step(v.max(best[:, s, :], masked[:, s, :]))
                c.after(k)
                carry()
                for s in range(S):
                    k = c.step(v.match_replace(out=rest[:, s, :], in_to_replace=best[:, s, :],
                                               in_values=masked[:, s, :], imm_value=TAKEN))
                c.after(k)
                c.link(v.scalar_tensor_tensor(out=picked[:, :, :], in0=rest[:, :, :], scalar=TAKEN / 2,
                                              in1=score[:, :, :], op0=ALU.is_lt, op1=ALU.mult))
                c.link(v.tensor_reduce(wsum[:, :], picked[:, :, :], AX.X, ALU.add))
                c.link(v.tensor_scalar(wsum[:, :], wsum[:, :], 1e-20, None, ALU.add))
                c.link(v.reciprocal(wr[:, :], wsum[:, :]))
                c.link(v.tensor_scalar(wr[:, :], wr[:, :], 2.5, None, ALU.mult))
                v.tensor_tensor(rw[:, :, :], picked[:, :, :], wr[:, :].unsqueeze(2).to_broadcast([P, S, NE]),
                                ALU.mult).then_inc(rw_ready, 1)
                counts.append(("DVE_STEPS", c.k))

        @block.scalar
        def _(act):
            a_ = nc.scalar
            for dst, src in ((wout_in[:, :, :], wout_d), (bout[:, :], bout_d), (qw[:, :], qw_d),
                             (logit[:, :], logit_d), (phase[:, :], phase_d), (gates[:, :, :, :], gates_d)):
                act.dma_start(dst, src).then_inc(small_in, 16)
            act.dma_start(ratio[:, :], logit_d).then_inc(small_in, 16)
            act.wait_ge(sup_exp, 1)
            a_.activation(ratio[:, :], sup[:, :], ACT.Exp).then_inc(sup_exp, 1)
            act.wait_ge(angles, 1)
            a_.activation(sc[:, :, :], ang[:, :, :], ACT.Sin).then_inc(sines, 1)
            with act.Fori(0, NCHUNK) as i:
                act.wait_ge(var1, i + 1)
                a_.activation(std[:, :], rt[:, :], ACT.Sqrt).then_inc(std1, 1)
                act.wait_ge(xT_ps, i + 1)
                a_.activation(xnT[:, :], bank[2][:, :], ACT.Copy).then_inc(xT_ready, 1)
                act.wait_ge(qkv_ready, i * S + S)
                a_.activation(sq[:, :, :, :].rearrange("p s h d -> p (s h d)"),
                              qkv[:, :, :, :].rearrange("p s h d -> p (s h d)"), ACT.Square).then_inc(sq_ready, 1)
                act.wait_ge(ss_ready, i + 1)
                a_.activation(rn[:, :], ss[:, :], ACT.Sqrt).then_inc(norm_ready, 1)
                for w, b, n in (("q", 2, 0), ("k", 4, 1)):
                    act.wait_ge(qkT_ps, i * 2 + n + 1)
                    a_.activation(state[w, "x"][:, :], bank[b][:, :], ACT.Copy).then_inc(r_ready, 1)
                    a_.activation(ctrl[w][:, :], bank[b][:, :], ACT.Square).then_inc(ctrl_ready[w], 1)
                for k in range(1, DEPTH):
                    for w in "qk":
                        act.wait_ge(state_ready[w], i * 6 + 2 * k)
                        for a in "xy":
                            ins = a_.activation(sqr[w, a][:, :], state[w, a][:, :], ACT.Square)
                        ins.then_inc(sqr_ready[w], 1)
                act.wait_ge(state_ready["q"], i * 6 + 6)
                a_.activation(fin_nqy[:, :], fin["q", "y"][:, :], ACT.Copy, scale=-1.0).then_inc(neg_ready, 1)
                act.wait_ge(pat_ps, i + 1)
                a_.activation(psq[:, :, :, :].rearrange("p n v h -> p (n v h)"), bank[6][:, :], ACT.Square)\
                    .then_inc(psq_ready, 1)
                act.wait_ge(dm_ready, i + 1)
                for q in range(CIRC):
                    a_.activation(ex[:, :, q, :], dm[:, :, :], ACT.Exp, scale=coef[:, q:q + 1]).then_inc(ex_ready, 1)
                act.wait_ge(pr_ready, i * 4 + 4)
                a_.activation(am[:, :, :, :].rearrange("p n c h -> p (n c h)"),
                              pr[:, :, :, :].rearrange("p n c h -> p (n c h)"), ACT.Sqrt, bias=eps[:, 1:2])\
                    .then_inc(am_ready, 1)
                for r in range(2):
                    act.wait_ge(r_ps, i * 2 + r + 1)
                    for h in range(2):
                        a_.activation(amp[:, h, 16 * r:16 * r + 16, :, :].rearrange("p n c h -> p (n c h)"),
                                      bank[(0, 1)[h] if r else (6, 7)[h]][:, :], ACT.Abs).then_inc(abs_ready, 1)
                act.wait_ge(y_ps, i + 1)
                for q in range(4):
                    for t2 in range(2):
                        s = 2 * (q % 2) + t2
                        src = bank[(0, 1, 6, 7)[q]][:, t2 * 64:t2 * 64 + 64].rearrange("p (h n) -> p h n", h=2)
                        dst = yT[:, s, :, :].rearrange("p n (h f) -> p f h n", f=2)[:, q // 2]
                        a_.activation(dst, src, ACT.Identity, bias=bout[:, 0:1]).then_inc(y_ready, 1)
                act.wait_ge(var2, i + 1)
                a_.activation(std[:, :], rt[:, :], ACT.Sqrt).then_inc(std2, 1)
                act.wait_ge(xn2T_ps, i + 1)
                a_.activation(xn2T[:, :], bank[0][:, :], ACT.Copy).then_inc(xn2T_ready, 1)
                act.wait_ge(lg_ready, i + 1)
                a_.activation(el[:, :, :], lg[:, :, :], ACT.Exp, scale=-1.0).then_inc(el_ready, 1)
                act.wait_ge(rwT_ps, i + 1)
                a_.activation(rwT[:, :], bank[6][:, 0:2 * P], ACT.Copy).then_inc(rwT_ready, 1)

        @block.tensor
        def _(pe):
            t = nc.tensor
            pe.wait_ge(tables_ready, 1)
            pe.wait_ge(w_in, 16 * 4)
            with pe.Fori(0, NCHUNK) as i:
                pe.wait_ge(xn_ready, i * S + S)
                for s in range(S):
                    ins = t.transpose(bank[2][:, s * P:(s + 1) * P], xn[:, s, :], ident[:, :])
                ins.then_inc(xT_ps, 1)
                pe.wait_ge(xT_ready, i + 1)
                for s in range(S):
                    t.matmul(bank[(3, 4, 5, 2)[s]][:, 0:3 * E], xnT[:, s * P:(s + 1) * P], wqkv[:, :],
                             start=True, stop=True).then_inc(qkv_ps, 1)
                for n, b in ((0, 2), (1, 4)):
                    pe.wait_ge(qk_ready, i * 2 + n + 1)
                    for s in range(S):
                        ins = t.transpose(bank[b][:, s * P:(s + 1) * P],
                                          qkv[:, s, n * HEADS:(n + 1) * HEADS, :].rearrange("p h d -> p (h d)"),
                                          ident[:, :])
                    ins.then_inc(qkT_ps, 1)
                for k in range(DEPTH):
                    for n, (w, b) in enumerate((("q", 2), ("k", 4))):
                        sx, sy = state[w, "x"], state[w, "y"]
                        if k == 0:
                            pe.wait_ge(r_ready, i * 2 + n + 1)
                            pe.wait_ge(ctrl_ready[w], i * DEPTH + 1)
                            t.matmul(bank[b][:, :], maps[:, 0, 0, :], sx[:, :], start=True, stop=True)\
                                .then_inc(z_ps[w], 1)
                            t.matmul(bank[b + 1][:, :], maps[:, 0, 1, :], sx[:, :], start=True, stop=True)\
                                .then_inc(z_ps[w], 1)
                            continue
                        pe.wait_ge(state_ready[w], i * 6 + 2 * k)
                        t.matmul(bank[b][:, :], maps[:, k, 0, :], sx[:, :], start=True, stop=False)
                        t.matmul(bank[b][:, :], maps[:, k, 2, :], sy[:, :], start=False, stop=True)\
                            .then_inc(z_ps[w], 1)
                        t.matmul(bank[b + 1][:, :], maps[:, k, 1, :], sx[:, :], start=True, stop=False)
                        t.matmul(bank[b + 1][:, :], maps[:, k, 0, :], sy[:, :], start=False, stop=True)\
                            .then_inc(z_ps[w], 1)
                pe.wait_ge(k_loaded, i * 16 * S + 16 * S)
                pe.wait_ge(q_loaded, i * 16 + 16)
                for n in range(P):
                    f, n1 = n % N4, n // N4
                    ins = t.matmul(bank[6][32 * f:32 * f + 32, n1 * 16:n1 * 16 + 16],
                                   kbd[:, :, :, n].rearrange("p s h -> p s h"), qs[:, :, :, n],
                                   start=True, stop=True)
                ins.then_inc(pat_ps, 1)
                pe.wait_ge(pt_ready, i + 1)
                for b in range(2):
                    ins = t.transpose(bank[7][:, b * P:(b + 1) * P],
                                      pt[:, 16 * b:16 * b + 16, :].rearrange("p n h -> p (n h)"), ident[:, :])
                ins.then_inc(ptT_ps, 1)
                pe.wait_ge(mb_ready, i + 1)
                for b in range(2):
                    ins = t.transpose(bank[6][:, b * P:(b + 1) * P],
                                      mb[:, b, :, :].rearrange("p m j -> p (m j)"), ident[:, :])
                ins.then_inc(mbT_ps, 1)
                pe.wait_ge(ex_ready, i * 4 + 4)
                for g in range(4):
                    ins = t.matmul(bank[7][32 * g:32 * g + 32, 0:256], pair_sum[:, :],
                                   ex[:, 8 * g:8 * g + 8, :, :].rearrange("p n c h -> p (n c h)"),
                                   start=True, stop=True)
                ins.then_inc(z_sum, 1)
                pe.wait_ge(rz_ready, i + 1)
                for g in range(4):
                    ins = t.matmul(bank[g // 2][:, (g % 2) * 256:(g % 2) * 256 + 256], pair_back[:, g, :], rz[:, :],
                                   start=True, stop=True)
                ins.then_inc(rz_ps, 1)
                pe.wait_ge(v_loaded, i * 256 + 256)
                pe.wait_ge(am_ready, i + 1)
                for r in range(2):
                    for n in range(16):
                        n1 = 16 * r + n
                        for h in range(2):
                            b = (0, 1)[h] if r else (6, 7)[h]
                            ins = t.matmul(bank[b][:, n * 32:n * 32 + 32],
                                           vbd[64 * h:64 * h + 64, n1, :, :].rearrange("p t d -> p (t d)"),
                                           am[64 * h:64 * h + 64, n1, :, :].rearrange("p c h -> p (c h)"),
                                           start=True, stop=True)
                    ins.then_inc(r_ps, 1)
                pe.wait_ge(mix_ready, i + 1)
                for q in range(4):
                    for t2 in range(2):
                        for h in range(HEADS):
                            ins = t.matmul(bank[(0, 1, 6, 7)[q]][:, t2 * 64:t2 * 64 + 64],
                                           wout[32 * q:32 * q + 32, h, t2, :], mix[32 * q:32 * q + 32, :, h],
                                           start=(h == 0), stop=(h == HEADS - 1))
                ins.then_inc(y_ps, 1)
                pe.wait_ge(y_ready, i * 8 + 8)
                for s in range(S):
                    ins = t.transpose(bank[7][:, s * P:(s + 1) * P], yT[:, s, :, :].rearrange("p n f -> p (n f)"),
                                      ident[:, :])
                ins.then_inc(yT_ps, 1)
                pe.wait_ge(xn2_ready, i * S + S)
                for s in range(S):
                    ins = t.transpose(bank[0][:, s * P:(s + 1) * P], xn2[:, s, :], ident[:, :])
                ins.then_inc(xn2T_ps, 1)
                pe.wait_ge(xn2T_ready, i + 1)
                for s in range(S):
                    ins = t.matmul(bank[1][:, s * NE:(s + 1) * NE], xn2T[:, s * P:(s + 1) * P], gwt[:, :],
                                   start=True, stop=True)
                ins.then_inc(lg_ps, 1)
                pe.wait_ge(rw_ready, i + 1)
                for b in range(S // 2):
                    ins = t.transpose(bank[6][:, b * P:(b + 1) * P],
                                      rw[:, 2 * b:2 * b + 2, :].rearrange("p s e -> p (s e)"), ident[:, :])
                ins.then_inc(rwT_ps, 1)


def experts(nc, wpack_d, rw_d, out_rows, x, xhi, xlo, ident, bank):
    with ExitStack() as ctx:
        def sb(name, shape, dt=F32):
            return ctx.enter_context(nc.sbuf_tensor(name, shape, dt))

        def sem(name):
            return ctx.enter_context(nc.semaphore(name))

        RING = 4
        win = sb("win", [P, PERIOD, 3, P])
        whi = sb("whi", [P, PERIOD, 3, P], F32R)
        wlo = sb("wlo", [P, PERIOD, 3, P], F32R)
        rwb = sb("rwb", [P, PERIOD, T])
        act_g = sb("act_g", [P, RING, CHUNK])
        act_u = sb("act_u", [P, RING, CHUNK])
        hid = act_u
        hhi = sb("hhi", [P, RING, CHUNK], F32R)
        hlo = sb("hlo", [P, RING, CHUNK], F32R)
        outT = act_g

        w_loaded = [sem(f"w_loaded{b}") for b in range(PERIOD)]
        r_loaded = [sem(f"r_loaded{b}") for b in range(PERIOD)]
        whi_ready, wlo_ready, gate_ps, up_ps, silu_ready, au_ready, hid_ready, hhi_ready, hlo_ready, down_ps = (
            sem(n) for n in ("whi_ready", "wlo_ready", "gate_ps", "up_ps", "silu_ready", "au_ready", "hid_ready",
                             "hhi_ready", "hlo_ready", "down_ps"))
        outT_ready, outT_ps, res_ready, stored = (sem(n) for n in ("outT_ready", "outT_ps", "res_ready", "stored"))
        segs = segments()
        per_block = [sum(1 for s in segs if s[0] == b) for b in range(PERIOD)]
        SH = MT * NCHUNK

        block = ctx.enter_context(nc.Block())

        @block.sync
        def _(sp):
            def period(i, first):
                for b in range(PERIOD):
                    if not first:
                        sp.wait_ge(wlo_ready, (i - 1) * PERIOD + b + 1)
                        sp.nop(nofuse=True)
                    sp.dma_start(win[:, b, :, :], wpack_d[bass.ds(i * PERIOD + b, 1)]
                                 .rearrange("a p k c -> p (a k) c")).then_inc(w_loaded[b], 16)
                    if not first:
                        sp.wait_ge(hid_ready, (i - 1) * UNITS + (b + 1) * NCHUNK)
                    for _, r, n, e in [s for s in segs if s[0] == b]:
                        row = rw_d[bass.ds(i * EXPERTS + e, 1), :]
                        sp.dma_start(rwb[r:r + n, b, :], row.to_broadcast([n, T])).then_inc(r_loaded[b], 16)

            period(0, True)
            with sp.Fori(1, PERIODS) as i:
                period(i, False)
            for b in range(2):
                sp.wait_ge(wlo_ready, MT - PERIOD + b + 1)
                sp.dma_start(win[:, b, :, :], wpack_d[MT + b]).then_inc(w_loaded[b], 16)
            for c in range(NCHUNK):
                sp.wait_ge(res_ready, c + 1)
                sp.dma_start(out_rows[c * CHUNK:(c + 1) * CHUNK, :].rearrange("(s p) e -> p s e", p=P),
                             x[:, c * S:(c + 1) * S, :]).then_inc(stored, 16)
            sp.wait_ge(stored, 16 * NCHUNK)

        @block.gpsimd
        def _(pool):
            def unit(u, b, q, slot):
                pool.wait_ge(silu_ready, u + 1)
                pool.wait_ge(au_ready, u + 1)
                nc.gpsimd.tensor_tensor(hid[:, slot, :], act_g[:, slot, :], act_u[:, slot, :], ALU.mult)\
                    .then_inc(hid_ready, 1)

            def period(i, first):
                for b in range(PERIOD):
                    for q in range(NCHUNK):
                        u = b * NCHUNK + q
                        if not (first and u < RING):
                            pool.wait_ge(hlo_ready, i * UNITS + u - RING + 1)
                        unit(i * UNITS + u, b, q, u % RING)

            period(0, True)
            with pool.Fori(1, PERIODS) as i:
                period(i, False)
            for b in range(2):
                for q in range(NCHUNK):
                    u = SH + b * NCHUNK + q
                    pool.wait_ge(hlo_ready, u - RING + 1)
                    pool.wait_ge(silu_ready, u + 1)
                    pool.wait_ge(au_ready, u + 1)
                    nc.gpsimd.tensor_tensor(hid[0:NI, u % RING, :], act_g[0:NI, u % RING, :],
                                            act_u[0:NI, u % RING, :], ALU.mult).then_inc(hid_ready, 1)

        @block.scalar
        def _(act):
            a_ = nc.scalar

            def silu(u, slot, rows, wait_slot):
                act.wait_ge(gate_ps, u + 1)
                if wait_slot:
                    act.wait_ge(hid_ready, u - RING + 1)
                a_.activation(act_g[0:rows, slot, :], bank[4 + slot % 2][0:rows, :], ACT.Silu).then_inc(silu_ready, 1)

            def high(u, slot, rows, wait_slot):
                act.wait_ge(hid_ready, u + 1)
                if wait_slot:
                    act.wait_ge(down_ps, u - RING + 1)
                a_.activation(hhi[0:rows, slot, :], hid[0:rows, slot, :], ACT.Copy).then_inc(hhi_ready, 1)

            def period(i, first):
                for b in range(PERIOD):
                    for q in range(NCHUNK):
                        u = b * NCHUNK + q
                        silu(i * UNITS + u, u % RING, P, not (first and u < RING))
                        if not (first and u < 2):
                            v = u - 2
                            high(i * UNITS + v, v % RING, P, not (first and v < RING))

            period(0, True)
            with act.Fori(1, PERIODS) as i:
                period(i, False)
            for n in range(2 * NCHUNK):
                u = SH + n
                silu(u, u % RING, NI, True)
                high(u - 2, (u - 2) % RING, P if n < 2 else NI, True)
            for u in (SH + 2 * NCHUNK - 2, SH + 2 * NCHUNK - 1):
                high(u, u % RING, NI, True)
            for c in range(NCHUNK):
                act.wait_ge(down_ps, SH + NCHUNK + c + 1)
                a_.activation(outT[:, c, :], bank[c][:, :], ACT.Copy).then_inc(outT_ready, 1)

        @block.vector
        def _(dve):
            v = nc.vector

            def split(b):
                v.tensor_copy(whi[:, b, :, :], win[:, b, :, :]).then_inc(whi_ready, 1)

            def split_lo(n, b):
                dve.wait_ge(whi_ready, n)
                v.tensor_tensor(wlo[:, b, :, :], win[:, b, :, :], whi[:, b, :, :].bitcast(F32), ALU.subtract)\
                    .then_inc(wlo_ready, 1)

            def up(u, slot, rows, b, q, wait_slot):
                dve.wait_ge(up_ps, u + 1)
                if wait_slot:
                    dve.wait_ge(hlo_ready, u - RING + 1)
                src, dst = bank[6 + slot % 2][0:rows, :], act_u[0:rows, slot, :]
                if b is None:
                    v.tensor_copy(dst, src).then_inc(au_ready, 1)
                else:
                    v.tensor_tensor(dst, src, rwb[:, b, q * CHUNK:(q + 1) * CHUNK], ALU.mult).then_inc(au_ready, 1)

            def low(u, slot, rows, wait_slot):
                dve.wait_ge(hhi_ready, u + 1)
                if wait_slot:
                    dve.wait_ge(down_ps, u - RING + 1)
                v.tensor_tensor(hlo[0:rows, slot, :], hid[0:rows, slot, :], hhi[0:rows, slot, :].bitcast(F32),
                                ALU.subtract).then_inc(hlo_ready, 1)

            AHEAD = 2

            def period(i, first):
                for b in range(PERIOD):
                    for q in range(NCHUNK):
                        u = b * NCHUNK + q
                        if q == 0:
                            dve.wait_ge(r_loaded[b], 16 * per_block[b] * (i + 1))
                        if q == 1:
                            nb = (b + AHEAD) % PERIOD
                            wrap = b + AHEAD >= PERIOD
                            dve.wait_ge(w_loaded[nb], 16 * (i + 1 + wrap))
                            if wrap or not first:
                                dve.wait_ge(down_ps, i * UNITS + (b + AHEAD + 1 - PERIOD) * NCHUNK)
                            split(nb)
                        if q == 2:
                            nb = (b + AHEAD) % PERIOD
                            split_lo(i * PERIOD + b + AHEAD + 1, nb)
                        up(i * UNITS + u, u % RING, P, b, q, not (first and u < RING))
                        if not (first and u < 2):
                            w = u - 2
                            low(i * UNITS + w, w % RING, P, not (first and w < RING))

            for b in range(AHEAD):
                dve.wait_ge(w_loaded[b], 16)
                split(b)
                split_lo(b + 1, b)
            period(0, True)
            with dve.Fori(1, PERIODS) as i:
                period(i, False)
            for n in range(2 * NCHUNK):
                u = SH + n
                up(u, u % RING, NI, None, None, True)
                low(u - 2, (u - 2) % RING, P if n < 2 else NI, True)
            for u in (SH + 2 * NCHUNK - 2, SH + 2 * NCHUNK - 1):
                low(u, u % RING, NI, True)
            for c in range(NCHUNK):
                dve.wait_ge(outT_ps, c + 1)
                xi = slice(c * S, (c + 1) * S)
                v.tensor_tensor(x[:, xi, :], x[:, xi, :], bank[4 + c][:, :].rearrange("p (s e) -> p s e", s=S),
                                ALU.add).then_inc(res_ready, 1)

        @block.tensor
        def _(pe):
            t = nc.tensor

            def three(out, hi, lo, mhi, mlo, start, stop):
                t.matmul(out, hi, mhi, start=start, stop=False)
                t.matmul(out, hi, mlo, start=False, stop=False)
                return t.matmul(out, lo, mhi, start=False, stop=stop)

            def up(u, slot, rows, hi, lo, q, wait_slot):
                xs = slice(q * CHUNK, (q + 1) * CHUNK)
                if wait_slot:
                    pe.wait_ge(silu_ready, u - 1)
                three(bank[4 + slot % 2][0:rows, :], hi[:, 0, 0:rows], lo[:, 0, 0:rows], xhi[:, xs], xlo[:, xs],
                      True, True).then_inc(gate_ps, 1)
                if wait_slot:
                    pe.wait_ge(au_ready, u - 1)
                three(bank[6 + slot % 2][0:rows, :], hi[:, 1, 0:rows], lo[:, 1, 0:rows], xhi[:, xs], xlo[:, xs],
                      True, True).then_inc(up_ps, 1)

            def down(u, slot, rows, hi, lo, q, start, stop):
                pe.wait_ge(hlo_ready, u + 1)
                three(bank[q][:, :], hi[0:rows, 2, :], lo[0:rows, 2, :], hhi[0:rows, slot, :], hlo[0:rows, slot, :],
                      start, stop).then_inc(down_ps, 1)

            def period(i, first):
                for b in range(PERIOD):
                    pe.wait_ge(wlo_ready, i * PERIOD + b + 1)
                    for q in range(NCHUNK):
                        u = b * NCHUNK + q
                        up(i * UNITS + u, u % RING, P, whi[:, b], wlo[:, b], q,
                           not (first and u < 2))
                        if not (first and u < LAG):
                            w = (u - LAG) % UNITS
                            wb = w // NCHUNK
                            down(i * UNITS + u - LAG, w % RING, P, whi[:, wb], wlo[:, wb], w % NCHUNK,
                                 first and w < NCHUNK, False)

            period(0, True)
            with pe.Fori(1, PERIODS) as i:
                period(i, False)
            for n in range(2 * NCHUNK + LAG):
                u = SH + n
                if n < 2 * NCHUNK:
                    if n % NCHUNK == 0:
                        pe.wait_ge(wlo_ready, MT + n // NCHUNK + 1)
                    up(u, u % RING, NI, whi[:, n // NCHUNK], wlo[:, n // NCHUNK], n % NCHUNK, True)
                w = u - LAG
                if n < LAG:
                    wb = (UNITS - LAG + n) // NCHUNK
                    down(w, w % RING, P, whi[:, wb], wlo[:, wb], w % NCHUNK, False, False)
                else:
                    m = n - LAG
                    down(w, w % RING, NI, whi[:, m // NCHUNK], wlo[:, m // NCHUNK], m % NCHUNK, False,
                         m >= NCHUNK)
            for c in range(NCHUNK):
                pe.wait_ge(outT_ready, c + 1)
                for s in range(S):
                    ins = t.transpose(bank[4 + c][:, s * P:(s + 1) * P],
                                      outT[:, c, s * P:(s + 1) * P], ident[:, :])
                ins.then_inc(outT_ps, 1)


def _layouts(np_, i):
    c = np_.ascontiguousarray

    def rows(a):
        return c(np_.broadcast_to(a[None, :], (P, a.shape[0])))

    def blocks(g, u, d):
        n, k, _ = g.shape
        out = np_.zeros((n, P, 3, P), np_.float32)
        out[:, :, 0, :k] = g.transpose(0, 2, 1)
        out[:, :, 1, :k] = u.transpose(0, 2, 1)
        out[:, :k, 2, :] = d
        return out

    pre, ffn = "L0_attn_", "L0_ffn_"
    gates = i[pre + "entanglement_gates"][:, :, 0:2]
    own = np_.repeat(gates, D, axis=1).transpose(1, 0, 2)
    prev = np_.repeat(np_.roll(gates, 1, axis=1), D, axis=1).transpose(1, 0, 2)
    wout = i[pre + "W_out"].T.reshape(HEADS, D, E).transpose(1, 0, 2)
    wg = i[ffn + "Wg"].reshape(MT, P, E)
    wu = i[ffn + "Wu"].reshape(MT, P, E)
    wd = i[ffn + "Wd"].transpose(0, 2, 1).reshape(MT, P, E)
    shared = blocks(i[ffn + "Sg"].reshape(2, NI, E), i[ffn + "Su"].reshape(2, NI, E),
                    i[ffn + "Sd"].T.reshape(2, NI, E))
    return {
        "x": c(i[pre + "query"]),
        "wqkv": c(i[pre + "W_qkv"].T),
        "bqkv": rows(i[pre + "b_qkv"]),
        "wout": c(np_.tile(wout, (HEADS, 1, 1))),
        "bout": c(i[pre + "b_out"][:, None]),
        "qw": rows(i[pre + "quantum_weights"][:, 0, 0]),
        "phase": c(np_.tile(np_.diagonal(i[pre + "photonic_phases"][:D, :D]), HEADS)[:, None]),
        "gates": c(np_.stack([own, prev], axis=2)),
        "logit": rows(i[pre + "superposition_logits"]),
        "gw": c(i[ffn + "gate_w"].T),
        "gbias": rows(i[ffn + "gate_bias"]),
        "wpack": np_.concatenate([blocks(wg, wu, wd), shared]),
    }


def kernel(**inputs):
    import concourse.bacc as _bacc
    from concourse import mybir as _mybir
    from concourse.bass_utils import run_bass_kernel_spmd as _run

    nc = _bacc.Bacc("TRN2", target_bir_lowering=False, num_devices=1)
    arrays = _layouts(np, {k: np.asarray(v) for k, v in inputs.items()})
    args = [nc.dram_tensor(f"in_{n}", a.shape, _mybir.dt.float32, kind="ExternalInput").ap()
            for n, a in arrays.items()]
    out = nc.dram_tensor("out_0", (2, 1024, E), _mybir.dt.float32, kind="ExternalOutput").ap()
    counts = []
    build(nc, *args, out, counts)
    r = _run(nc, [{f"in_{n}": a for n, a in arrays.items()}], core_ids=[0])
    return r.results[0]["out_0"]
```

```python
from contextlib import ExitStack

import numpy as np

import concourse.bass as bass
from concourse import mybir

F32 = mybir.dt.float32
F32R = mybir.dt.float32r
U32 = mybir.dt.uint32
ALU = mybir.AluOpType
ACT = mybir.ActivationFunctionType
AX = mybir.AxisListType

P = 128
T, E = 2048, 128
HEADS, D, CIRC, DEPTH = 8, 16, 4, 3
CHUNK = 512
NCHUNK = T // CHUNK
S = CHUNK // P
TILES = T // P
N4 = 4
NP = P // N4
NE, NI, NG, TOPG, TOPK = 64, 88, 8, 4, 8
SCALING = D ** -0.5
LN_EPS = 1e-5
PI = float(np.pi)
TWO_PI_A = 6.28125
TWO_PI_B = float(np.float32(2 * np.pi - 6.28125).view(np.uint32) & 0xFFFFF000) and float(
    (np.array([2 * np.pi - 6.28125], np.float32).view(np.uint32) & np.uint32(0xFFFFF000)).view(np.float32)[0])
TWO_PI_C = float(2 * np.pi - TWO_PI_A - TWO_PI_B)
ROUND = 1.5 * 2.0 ** 23
PI_SAFE = 3.1415925
TAKEN = -3.0e38

ROWS = NE * NI
MT = ROWS // P
PERIOD = 11
PERIODS = MT // PERIOD
EXPERTS = PERIOD * P // NI
SHARED = 2 * NI
LAG = 3
UNITS = PERIOD * NCHUNK

A_HALF, A_PREV, A_PHASE, A_PHASE2, A_CIRC = 0, 3, 6, 7, 8
NANG = 12


def segments():
    out = []
    for b in range(PERIOD):
        r = 0
        while r < P:
            e = (b * P + r) // NI
            n = min(P - r, (e + 1) * NI - (b * P + r))
            out.append((b, r, n, e))
            r += n
    return out


class Chain:

    def __init__(self, eng, sem):
        self.eng, self.sem, self.base, self.k = eng, sem, 0, 0

    def start(self, base):
        self.base, self.k = base, 0

    def step(self, ins):
        ins.then_inc(self.sem, 1)
        self.k += 1
        return self.k

    def after(self, k):
        self.eng.wait_ge(self.sem, self.base + k)

    def link(self, ins):
        self.after(self.step(ins))


DVE_STEPS = 67


def has_before(n):
    return not (isinstance(n, int) and n == 0)


def build(nc, x_d, wqkv_d, bqkv_d, wout_d, bout_d, qw_d, phase_d, gates_d, logit_d,
          gw_d, gbias_d, wpack_d, out_d):
    x_rows = x_d.rearrange("b s e -> (b s) e")
    out_rows = out_d.rearrange("b s e -> (b s) e")

    def dram(name, shape):
        return nc.dram_tensor(name, shape, F32, kind="Internal").ap()

    v_d = dram("v_rows", [T, E])
    k_d = dram("k_strips", [NCHUNK, S, 2, HEADS, D, P])
    q_d = dram("q_strips", [NCHUNK, S, 2, 2, HEADS, D, P])
    y_d = dram("y_rows", [NCHUNK, HEADS, D, 8, 64])
    rw_d = dram("rw_rows", [NE, T])

    with ExitStack() as whole:
        def sem(name):
            return whole.enter_context(nc.semaphore(name))

        def keep(name, shape, dt=F32):
            return whole.enter_context(nc.sbuf_tensor(name, shape, dt))

        x = keep("x", [P, TILES, E])
        xhi = keep("xhi", [E, T], F32R)
        xlo = keep("xlo", [E, T], F32R)
        ident = keep("ident", [P, P])
        bank = [whole.enter_context(nc.psum_tensor(f"bank{n}", [P, 512], F32)) for n in range(8)]

        attention(nc, x_rows, wqkv_d, bqkv_d, wout_d, bout_d, qw_d, phase_d, gates_d, logit_d,
                  gw_d, gbias_d, v_d, k_d, q_d, y_d, rw_d, x, xhi, xlo, ident, bank)
        experts(nc, wpack_d, rw_d, out_rows, x, xhi, xlo, ident, bank)


def attention(nc, x_rows, wqkv_d, bqkv_d, wout_d, bout_d, qw_d, phase_d, gates_d, logit_d,
              gw_d, gbias_d, v_d, k_d, q_d, y_d, rw_d, x, xhi, xlo, ident, bank):
    with ExitStack() as ctx:
        def sb(name, shape, dt=F32):
            return ctx.enter_context(nc.sbuf_tensor(name, shape, dt))

        def sem(name):
            return ctx.enter_context(nc.semaphore(name))

        wqkv = sb("wqkv", [E, 3 * E])
        bqkv = sb("bqkv", [P, 3 * E])
        gwt = sb("gwt", [E, NE])
        gbias = sb("gbias", [P, NE])
        wout = sb("wout", [P, E])
        wout_in = sb("wout_in", [P, E])
        bout = sb("bout", [P, E])
        qw = sb("qw", [P, CIRC])
        logit = sb("logit", [P, CIRC])
        phase = sb("phase", [P, 1])
        gates = sb("gates", [P, DEPTH, 2, 2])
        own_head = sb("own_head", [P, 1])
        shift = sb("shift", [P, P])
        stay = sb("stay", [P, P])
        maps = sb("maps", [P, DEPTH, 3, P])
        ang = sb("ang", [P, 2, NANG])
        turns = sb("turns", [P, 2, NANG])
        sc = sb("sc", [P, 2, NANG])
        gain = sb("gain", [P, DEPTH, 2])
        ratio = sb("ratio", [P, CIRC])
        coef = sb("coef", [P, CIRC])
        coef_t = sb("coef_t", [P, CIRC])
        sup = sb("sup", [P, CIRC])
        sup_s = sb("sup_s", [P, 4])
        eps = sb("eps", [P, 2])
        ones = sb("ones", [1, P])
        tick = sb("tick", [P, 16])
        pair_sum = sb("pair_sum", [P, 32])
        pair_back = sb("pair_back", [P, 4, P])
        before = sb("before", [P, NG, NG])
        st = sb("st", [P, S, 6])
        mv = sb("mv", [P, S, 2])
        std = sb("std", [P, S])
        rstd = sb("rstd", [P, S])
        rt = sb("rt", [P, S])
        st2 = sb("st2", [P, S, 6])
        mv2 = sb("mv2", [P, S, 2])
        stdb = sb("stdb", [P, S])
        rstd2 = sb("rstd2", [P, S])
        rt2 = sb("rt2", [P, S])
        xn = sb("xn", [P, S, E])
        xnT = sb("xnT", [E, CHUNK])
        qkv = sb("qkv", [P, S, 3 * HEADS, D])
        sq = sb("sq", [P, S, 3 * HEADS, D])
        ss = sb("ss", [P, S * 3 * HEADS])
        rn = sb("rn", [P, S * 3 * HEADS])
        vs = sb("vs", [P, S, D])
        vg = sb("vg", [P, S, D])
        vsg = sb("vsg", [P, S, HEADS, D])
        state = {(w, a): sb(f"state_{w}{a}", [P, CHUNK]) for w in "qk" for a in "xy"}
        sqr = {(w, a): sb(f"sqr_{w}{a}", [P, CHUNK]) for w in "qk" for a in "xy"}
        ctrl = {w: sb(f"ctrl_{w}", [P, CHUNK]) for w in "qk"}
        gain_t = {(w, a): sb(f"gain_{w}{a}", [P, CHUNK]) for w in "qk" for a in "xy"}
        fin = {(w, a): sb(f"fin_{w}{a}", [P, CHUNK]) for w, a in ("qx", "qy", "kx", "ky")}
        fin_nqy = sb("fin_nqy", [P, CHUNK])
        kbd = sb("kbd", [P, S, HEADS, P])
        qs = sb("qs", [P, 2, HEADS, P])
        vbd = sb("vbd", [P, NP, 8, D])
        psq = sb("psq", [P, NP, 2, HEADS])
        pt = sb("pt", [P, NP, HEADS])
        mx = sb("mx", [P, 2, 16])
        mb = sb("mb", [P, 2, 16, 8])
        dm = sb("dm", [P, NP, HEADS])
        ex = sb("ex", [P, NP, CIRC, HEADS])
        rz = sb("rz", [P, 256])
        pr = sb("pr", [P, NP, CIRC, HEADS])
        am = sb("am", [P, NP, CIRC, HEADS])
        amp = sb("amp", [P, 2, NP, CIRC, HEADS])
        mix = sb("mix", [P, HEADS, 2 * NP])
        yin = sb("yin", [P, 8, 2 * NP])
        xn2 = sb("xn2", [P, S, E])
        xn2T = sb("xn2T", [E, CHUNK])
        lg = sb("lg", [P, S, NE])
        el = sb("el", [P, S, NE])
        e1 = sb("e1", [P, S, NE])
        score = sb("score", [P, S, NE])
        choice = sb("choice", [P, S, NG, NE // NG])
        top = sb("top", [P, S, NG, 8])
        gs = sb("gs", [P, S, NG])
        gt = sb("gt", [P, S, NG, NG])
        ge = sb("ge", [P, S, NG, NG])
        rank = sb("rank", [P, S, NG])
        gm = sb("gm", [P, S, NG])
        masked = sb("masked", [P, S, NE])
        best = sb("best", [P, S, 8])
        rest = sb("rest", [P, S, NE])
        picked = sb("picked", [P, S, NE])
        wsum = sb("wsum", [P, S])
        wr = sb("wr", [P, S])
        rw = sb("rw", [P, S, NE])
        rwT = sb("rwT", [P, NCHUNK * 2, P])

        x_in, small_in, w_in = sem("x_in"), sem("small_in"), sem("w_in")
        v_stored, v_loaded = sem("v_stored"), sem("v_loaded")
        k_stored, k_loaded = sem("k_stored"), sem("k_loaded")
        q_stored, q_loaded = sem("q_stored"), sem("q_loaded")
        y_stored, y_loaded = sem("y_stored"), sem("y_loaded")
        rw_stored = sem("rw_stored")
        consts, angles, sines, tables_ready, sup_exp = (
            sem(n) for n in ("consts", "angles", "sines", "tables_ready", "sup_exp"))
        dve_s, act_s, pool_s = sem("dve_steps"), sem("act_steps"), sem("pool_steps")
        (var1, std1, xn_ready, xT_ps, xT_ready, qkv_ps, qkv_ready, sq_ready, ss_ready, norm_ready,
         qk_ready, vsg_ready, qkT_ps, r_ready) = (sem(n) for n in (
             "var1", "std1", "xn_ready", "xT_ps", "xT_ready", "qkv_ps", "qkv_ready", "sq_ready", "ss_ready",
             "norm_ready", "qk_ready", "vsg_ready", "qkT_ps", "r_ready"))
        z_ps = {w: sem(f"z_ps_{w}") for w in "qk"}
        sqr_ready = {w: sem(f"sqr_ready_{w}") for w in "qk"}
        ctrl_ready = {w: sem(f"ctrl_ready_{w}") for w in "qk"}
        gain_ready = {w: sem(f"gain_ready_{w}") for w in "qk"}
        state_ready = {w: sem(f"state_ready_{w}") for w in "qk"}
        neg_ready, abs_ready = sem("neg_ready"), sem("abs_ready")
        (pat_ps, psq_ready, pt_ready, ptT_ps, mb_ready, mbT_ps, dm_ready, ex_ready, z_sum, rz_ready, rz_ps,
         pr_ready, am_ready, r_ps, amp_ready, mix_ready, y_ps, x1_ready) = (sem(n) for n in (
             "pat_ps", "psq_ready", "pt_ready", "ptT_ps", "mb_ready", "mbT_ps", "dm_ready", "ex_ready", "z_sum",
             "rz_ready", "rz_ps", "pr_ready", "am_ready", "r_ps", "amp_ready", "mix_ready", "y_ps", "x1_ready"))
        (var2, std2, xn2_ready, xn2T_ps, xn2T_ready, lg_ps, lg_ready, el_ready, rw_ready, rwT_ps,
         rwT_ready) = (sem(n) for n in (
             "var2", "std2", "xn2_ready", "xn2T_ps", "xn2T_ready", "lg_ps", "lg_ready", "el_ready", "rw_ready",
             "rwT_ps", "rwT_ready"))

        block = ctx.enter_context(nc.Block())

        @block.sync
        def _(sp):
            sp.dma_start(x[:, :, :], x_rows.rearrange("(t p) e -> p t e", p=P)).then_inc(x_in, 16)
            sp.dma_start(wqkv[:, :], wqkv_d).then_inc(w_in, 16)
            sp.dma_start(bqkv[:, :], bqkv_d).then_inc(w_in, 16)
            sp.dma_start(gwt[:, :], gw_d).then_inc(w_in, 16)
            sp.dma_start(gbias[:, :], gbias_d).then_inc(w_in, 16)

            def keys_queries(f):
                kc, qc = k_d[bass.ds(f, 1)], q_d[bass.ds(f, 1)]

                def put(dst, src, done):
                    sp.dma_start(dst, src[:, :].rearrange("p (s n) -> p s n", s=S)).then_inc(done, 16)

                kv = kc.rearrange("a s c h d n -> (a c) (h d) s n")
                qv = qc.rearrange("a s c v h d n -> (a c) v (h d) s n")
                sp.wait_ge(state_ready["k"], f * 6 + 6)
                put(kv[0], fin["k", "x"], k_stored)
                put(kv[1], fin["k", "y"], k_stored)
                sp.wait_ge(state_ready["q"], f * 6 + 6)
                put(qv[0, 0], fin["q", "x"], q_stored)
                put(qv[1, 0], fin["q", "y"], q_stored)
                put(qv[1, 1], fin["q", "x"], q_stored)
                sp.wait_ge(neg_ready, f + 1)
                put(qv[0, 1], fin_nqy, q_stored)
                sp.wait_ge(k_stored, f * 32 + 32)
                if has_before(f):
                    sp.wait_ge(pat_ps, f * 1)
                kb = kc.rearrange("a s c h d n -> (a s) c d h n")
                for s in range(S):
                    for a in range(2):
                        r = 32 * s + 16 * a
                        sp.dma_start(kbd[r:r + 16, s, :, :], kb[s, a]).then_inc(k_loaded, 16)
                sp.wait_ge(q_stored, f * 64 + 64)
                qb = qc.rearrange("a s c v h d n -> (a s) c d (v h) n")
                for s in range(S):
                    for a in range(2):
                        r = 32 * s + 16 * a
                        sp.dma_start(qs[r:r + 16, :, :, :].rearrange("p v h n -> p (v h) n"), qb[s, a])\
                            .then_inc(q_loaded, 16)

            def measured(b):
                sp.wait_ge(mix_ready, b + 1)
                yd = y_d[bass.ds(b, 1)].rearrange("a i d t c -> (a t) d i c")
                for t8 in range(8):
                    sp.dma_start(yd[2 * (t8 % S) + t8 // S], mix[16 * t8:16 * t8 + 16, :, :]).then_inc(y_stored, 16)
                sp.wait_ge(y_stored, b * 128 + 128)
                sp.dma_start(yin[:, :, :].rearrange("p t c -> p (t c)"),
                              y_d[bass.ds(b, 1)].rearrange("a i d t c -> (a i d) (t c)")).then_inc(y_loaded, 16)

            def routing_rows(r):
                sp.wait_ge(rwT_ready, r + 1)
                sp.nop(nofuse=True)
                rv = rw_d[:, bass.ds(r * CHUNK, CHUNK)].rearrange("e (b s n) -> s e b n", b=S // 2, s=2)
                for s in range(2):
                    sp.dma_start(rv[s], rwT[s * NE:(s + 1) * NE, bass.ds(r * 2, 2), :])\
                        .then_inc(rw_stored, 16)

            def stages(f=None, b=None, r=None):
                if f is not None:
                    keys_queries(f)
                if b is not None:
                    measured(b)
                if r is not None:
                    routing_rows(r)

            stages(f=0)
            stages(f=1, b=0)
            with sp.Fori(0, NCHUNK - 2) as j:
                stages(f=j + 2, b=j + 1, r=j)
            stages(b=NCHUNK - 1, r=NCHUNK - 2)
            stages(r=NCHUNK - 1)
            sp.wait_ge(rw_stored, 16 * 2 * NCHUNK)

        @block.gpsimd
        def _(pool):
            c = Chain(pool, pool_s)
            g = nc.gpsimd
            c.link(g.memset(ident[:, :], 0.0))
            c.link(g.affine_select(out=ident[:, :], in_=ident[:, :], compare_op=ALU.not_equal, fill=1.0,
                                   base=0, pattern=[[-1, P]], channel_multiplier=1))
            c.link(g.memset(shift[:, :], 0.0))
            c.link(g.affine_select(out=shift[:, :], in_=shift[:, :], compare_op=ALU.not_equal, fill=1.0,
                                   base=-D, pattern=[[-1, P]], channel_multiplier=1))
            c.link(g.memset(own_head[:, :], 1.0))
            c.link(g.affine_select(out=own_head[:, :], in_=own_head[:, :], compare_op=ALU.is_gt, fill=0.0,
                                   base=(HEADS - 1) * D, pattern=[[0, 1]], channel_multiplier=-1))
            c.link(g.affine_select(out=stay[:, :], in_=ident[:, :], compare_op=ALU.is_ge, fill=0.0,
                                   base=-(HEADS - 1) * D, pattern=[[0, P]], channel_multiplier=1))
            c.link(g.memset(pair_sum[:, :], 1.0))
            pv = pair_sum[:, :].rearrange("p (a m) -> p a m", a=2)
            c.link(g.affine_select(out=pv, in_=pv, compare_op=ALU.is_ge, fill=0.0, base=0,
                                   pattern=[[0, 2], [-8, 16]], channel_multiplier=1))
            c.link(g.affine_select(out=pv, in_=pv, compare_op=ALU.is_gt, fill=0.0, base=8,
                                   pattern=[[0, 2], [8, 16]], channel_multiplier=-1))
            c.link(g.memset(pair_back[:, :, :], 1.0))
            c.link(g.affine_select(out=pair_back[:, :, :], in_=pair_back[:, :, :], compare_op=ALU.is_ge, fill=0.0,
                                   base=0, pattern=[[256, 4], [1, P]], channel_multiplier=-8))
            c.link(g.affine_select(out=pair_back[:, :, :], in_=pair_back[:, :, :], compare_op=ALU.is_gt, fill=0.0,
                                   base=8, pattern=[[-256, 4], [-1, P]], channel_multiplier=8))
            c.link(g.memset(before[:, :, :], 1.0))
            c.link(g.affine_select(out=before[:, :, :], in_=before[:, :, :], compare_op=ALU.is_gt, fill=0.0,
                                   base=0, pattern=[[1, NG], [-1, NG]], channel_multiplier=0))
            c.link(g.memset(eps[:, 0:1], LN_EPS))
            c.link(g.memset(eps[:, 1:2], 1e-12))
            c.link(g.memset(tick[:, :], 0.0))
            c.link(g.memset(kbd[:, :, :, :], 0.0))
            c.link(g.memset(vbd[:, :, :, :], 0.0))
            g.memset(ones[:, :], 1.0).then_inc(consts, 1)
            pool.wait_ge(tables_ready, 1)

            def gains(f, k):
                for w in "qk":
                    pool.wait_ge(ctrl_ready[w], f * DEPTH + k + 1)
                    n = 4 + 2 * k + "qk".index(w)
                    g.tensor_tensor(tick[:, n:n + 1], tick[:, 2:3], tick[:, 2:3], ALU.add)
                    for a in range(2):
                        g.tensor_scalar(gain_t[w, "xy"[a]][:, :], ctrl[w][:, :], gain[:, k, a:a + 1], 1.0,
                                        ALU.mult, ALU.add).then_inc(gain_ready[w], 1)

            def carry(n):
                g.tensor_tensor(tick[:, n:n + 1], tick[:, 2:3], tick[:, 2:3], ALU.add)

            def values_out(f):
                pool.wait_ge(vsg_ready, f + 1)
                carry(10)
                pool.dma_start(v_d[bass.ds(f * CHUNK, CHUNK), :].rearrange("(s n) e -> n s e", n=P),
                               vsg[:, :, :, :].rearrange("p s h d -> p s (h d)")).then_inc(v_stored, 16)

            def values_in(f):
                pool.wait_ge(v_stored, f * 16 + 16)
                if has_before(f):
                    pool.wait_ge(r_ps, f * 2)
                carry(11)
                back = v_d[bass.ds(f * CHUNK, CHUNK), :].rearrange("(s f h n) (j d) -> s h f j n d", s=S, f=2, h=2,
                                                                   j=HEADS)
                for s in range(S):
                    for n4 in range(N4):
                        p0, t8 = 32 * n4 + 8 * s, (n4 % 2) * 4 + s
                        pool.dma_start(vbd[p0:p0 + HEADS, :, t8, :], back[s, n4 // 2, n4 % 2])\
                            .then_inc(v_loaded, 16)

            def stages(f=None, b=None, r=None):
                if f is not None:
                    gains(f, 0)
                    values_out(f)
                    gains(f, 1)
                    gains(f, 2)
                    values_in(f)

            stages(f=0)
            stages(f=1, b=0)
            with pool.Fori(0, NCHUNK - 2) as j:
                stages(f=j + 2, b=j + 1, r=j)

        @block.vector
        def _(dve):
            v = nc.vector
            c = Chain(dve, dve_s)
            dve.wait_ge(small_in, 16 * 7)
            dve.wait_ge(consts, 1)
            own, prev = gates[:, :, 0, :], gates[:, :, 1, :]
            c.link(v.tensor_scalar(ang[:, 0, A_HALF:A_HALF + 3], own[:, :, 0], 0.5, None, ALU.mult))
            c.link(v.tensor_scalar(ang[:, 0, A_PREV:A_PREV + 3], prev[:, :, 1], -0.5, None, ALU.mult))
            c.link(v.tensor_scalar(turns[:, 0, 0:3], own[:, :, 1], own_head[:, 0:1], 0.5, ALU.mult, ALU.mult))
            c.link(v.tensor_tensor(ang[:, 0, A_PREV:A_PREV + 1], ang[:, 0, A_PREV:A_PREV + 1], phase[:, :],
                                   ALU.add))
            c.link(v.tensor_tensor(ang[:, 0, A_PREV + 1:A_PREV + 3], ang[:, 0, A_PREV + 1:A_PREV + 3],
                                   turns[:, 0, 0:2], ALU.add))
            c.link(v.tensor_copy(ang[:, 0, A_PHASE:A_PHASE + 1], phase[:, :]))
            c.link(v.tensor_scalar(ang[:, 0, A_PHASE2:A_PHASE2 + 1], phase[:, :], 2.0, None, ALU.mult))
            c.link(v.tensor_copy(ang[:, 0, A_CIRC:A_CIRC + CIRC], qw[:, :]))
            c.link(v.tensor_scalar(ang[:, 1, :], ang[:, 0, :], PI / 2, None, ALU.add))
            c.link(v.tensor_scalar(turns[:, :, :], ang[:, :, :], 1 / (2 * PI), ROUND, ALU.mult, ALU.add))
            c.link(v.tensor_scalar(turns[:, :, :], turns[:, :, :], ROUND, None, ALU.subtract))
            for part in (TWO_PI_A, TWO_PI_B, TWO_PI_C):
                c.link(v.scalar_tensor_tensor(out=ang[:, :, :], in0=turns[:, :, :], scalar=-part,
                                              in1=ang[:, :, :], op0=ALU.mult, op1=ALU.add))
            v.tensor_scalar(ang[:, :, :], ang[:, :, :], PI_SAFE, -PI_SAFE, ALU.min, ALU.max).then_inc(angles, 1)
            c.link(v.tensor_reduce(sup_s[:, 0:1], logit[:, :], AX.X, ALU.max))
            v.tensor_scalar(sup[:, :], logit[:, :], sup_s[:, 0:1], None, ALU.subtract).then_inc(sup_exp, 1)
            dve.wait_ge(sup_exp, 2)
            c.link(v.tensor_reduce(sup_s[:, 1:2], ratio[:, :], AX.X, ALU.add))
            c.link(v.reciprocal(sup_s[:, 2:3], sup_s[:, 1:2]))
            c.link(v.tensor_scalar(sup[:, :], ratio[:, :], sup_s[:, 2:3], None, ALU.mult))
            dve.wait_ge(sines, 1)
            sin, cos = sc[:, 0, :], sc[:, 1, :]
            c.link(v.tensor_tensor(gain[:, :, 0], cos[:, A_HALF:A_HALF + 3], sin[:, A_HALF:A_HALF + 3], ALU.add))
            c.link(v.tensor_tensor(gain[:, :, 1], cos[:, A_HALF:A_HALF + 3], sin[:, A_HALF:A_HALF + 3],
                                   ALU.subtract))
            c.link(v.tensor_scalar(gain[:, :, :], gain[:, :, :], -1.0, own_head[:, 0:1], ALU.add, ALU.mult))
            c.link(v.tensor_scalar(coef_t[:, :], sin[:, A_CIRC:A_CIRC + CIRC], 0.3, 0.5, ALU.mult, ALU.add))
            c.link(v.tensor_scalar(coef[:, :], coef_t[:, :], -SCALING, SCALING, ALU.mult, ALU.add))
            c.link(v.tensor_tensor(coef[:, :], coef[:, :], coef_t[:, :], ALU.mult))
            for k in range(DEPTH):
                col = A_PREV + k
                c.link(v.tensor_scalar(maps[:, k, 0, :], shift[:, :], cos[:, col:col + 1], None, ALU.mult))
                c.link(v.tensor_scalar(maps[:, k, 1, :], shift[:, :], sin[:, col:col + 1], None, ALU.mult))
                if k == 0:
                    for a, part in ((0, cos), (1, sin)):
                        c.link(v.scalar_tensor_tensor(out=maps[:, k, a, :], in0=stay[:, :],
                                                      scalar=part[:, A_PHASE:A_PHASE + 1], in1=maps[:, k, a, :],
                                                      op0=ALU.mult, op1=ALU.add))
                else:
                    c.link(v.tensor_tensor(maps[:, k, 0, :], maps[:, k, 0, :], stay[:, :], ALU.add))
                c.link(v.tensor_scalar(maps[:, k, 2, :], maps[:, k, 1, :], -1.0, None, ALU.mult))
            c.link(v.tensor_scalar(wout[:, :], wout_in[:, :], cos[:, A_PHASE2:A_PHASE2 + 1], None, ALU.mult))
            v.tensor_scalar(sup_s[:, 3:4], sup_s[:, 2:3], 1.0, None, ALU.mult).then_inc(tables_ready, 1)
            dve.wait_ge(tables_ready, 1)
            dve.wait_ge(x_in, 16)
            dve.wait_ge(w_in, 16 * 4)

            def carry():
                v.tensor_copy(tick[:, 1:2], tick[:, 0:1])

            def moments(n, st, mv, rt, var):
                carry()
                for s in range(S):
                    k = c.step(v.bn_stats(st[:, s, :], x[:, bass.ds(n * S + s, 1), :].rearrange("p a e -> p (a e)")))
                c.after(k)
                carry()
                for s in range(S):
                    k = c.step(v.bn_aggr(mv[:, s, :], st[:, s, :]))
                c.after(k)
                v.tensor_scalar(rt[:, :], mv[:, :, 1], LN_EPS, None, ALU.add).then_inc(var, 1)

            def normalise(n, mv, rt, std, rstd, std_ready, dst, ready):
                dve.wait_ge(std_ready, n + 1)
                c.link(v.reciprocal(rstd[:, :], std[:, :]))
                c.link(v.tensor_tensor(rt[:, :], rt[:, :], rstd[:, :], ALU.mult))
                c.link(v.tensor_tensor(rt[:, :], rt[:, :], rstd[:, :], ALU.mult))
                c.link(v.tensor_scalar(rt[:, :], rt[:, :], -0.5, 1.5, ALU.mult, ALU.add))
                c.link(v.tensor_tensor(rstd[:, :], rstd[:, :], rt[:, :], ALU.mult))
                for s in range(S):
                    v.tensor_scalar(dst[:, s, :], x[:, bass.ds(n * S + s, 1), :].rearrange("p a e -> p (a e)"),
                                    mv[:, s, 0:1], rstd[:, s:s + 1], ALU.subtract, ALU.mult).then_inc(ready, 1)

            def project(f):
                for s in range(S):
                    dve.wait_ge(qkv_ps, f * S + s + 1)
                    v.tensor_tensor(qkv[:, s, :, :].rearrange("p h d -> p (h d)"), bank[(3, 4, 5, 2)[s]][:, 0:3 * E],
                                    bqkv[:, :], ALU.add).then_inc(qkv_ready, 1)

            def norms(f):
                dve.wait_ge(sq_ready, f + 1)
                c.link(v.tensor_reduce(ss[:, :], sq[:, :, :, :].rearrange("p s h d -> p (s h) d"), AX.X, ALU.add))
                v.tensor_scalar(ss[:, :], ss[:, :], 1e-24, None, ALU.max).then_inc(ss_ready, 1)

            def encode(f):
                dve.wait_ge(norm_ready, f + 1)
                c.link(v.reciprocal(rn[:, :], rn[:, :]))
                rnv = rn[:, :].rearrange("p (s h) -> p s h", s=S)
                for a in range(3):
                    h0 = a * HEADS
                    part = qkv[:, :, h0:h0 + HEADS, :]
                    ins = v.tensor_tensor(part, part,
                                          rnv[:, :, h0:h0 + HEADS].unsqueeze(3).to_broadcast([P, S, HEADS, D]),
                                          ALU.mult)
                    if a < 2:
                        ins.then_inc(qk_ready, 1)
                    else:
                        c.link(ins)

            def sign_values(f):
                vals = qkv[:, :, 2 * HEADS:3 * HEADS, :]
                c.link(v.tensor_reduce(vs[:, :, :], vals.rearrange("p s h d -> p s d h"), AX.X, ALU.add))
                c.link(v.tensor_scalar(vg[:, :, :], vs[:, :, :], 0.0, 2.0, ALU.is_ge, ALU.mult))
                c.link(v.tensor_scalar(vg[:, :, :], vg[:, :, :], 1.0, None, ALU.subtract))
                if has_before(f):
                    dve.wait_ge(v_stored, f * 16)
                v.tensor_tensor(vsg[:, :, :, :], vals,
                                vg[:, :, :].unsqueeze(2).to_broadcast([P, S, HEADS, D]), ALU.mult)\
                    .then_inc(vsg_ready, 1)

            def entangle(f, k):
                for w, b in (("q", 2), ("k", 4)):
                    if k:
                        dve.wait_ge(sqr_ready[w], f * (DEPTH - 1) + k)
                        v.tensor_tensor(ctrl[w][:, :], sqr[w, "x"][:, :], sqr[w, "y"][:, :], ALU.add)\
                            .then_inc(ctrl_ready[w], 1)
                if k == DEPTH - 1 and has_before(f):
                    dve.wait_ge(k_stored, f * 32)
                    dve.wait_ge(q_stored, f * 64)
                for w, b in (("q", 2), ("k", 4)):
                    for a in range(2):
                        dve.wait_ge(z_ps[w], f * 6 + 2 * k + 2)
                        dve.wait_ge(gain_ready[w], f * 6 + 2 * k + a + 1)
                        dst = (fin if k == DEPTH - 1 else state)[w, "xy"[a]]
                        v.tensor_tensor(dst[:, :], bank[b + a][:, :], gain_t[w, "xy"[a]][:, :], ALU.mult)\
                            .then_inc(state_ready[w], 1)

            def pattern_square(b):
                dve.wait_ge(psq_ready, b + 1)
                v.tensor_tensor(pt[:, :, :], psq[:, :, 0, :], psq[:, :, 1, :], ALU.add).then_inc(pt_ready, 1)

            def pattern_max(b):
                dve.wait_ge(ptT_ps, b + 1)
                c.link(v.tensor_reduce(mx[:, :, :], bank[7][:, 0:256].rearrange("p (b m j) -> p b m j", b=2, j=8),
                                       AX.X, ALU.max))
                v.tensor_copy(mb[:, :, :, :], mx[:, :, :].unsqueeze(3).to_broadcast([P, 2, 16, 8]))\
                    .then_inc(mb_ready, 1)

            def pattern_less_max(b):
                dve.wait_ge(mbT_ps, b + 1)
                v.tensor_tensor(dm[:, :, :].rearrange("p n h -> p (n h)"), pt[:, :, :].rearrange("p n h -> p (n h)"),
                                bank[6][:, 0:256], ALU.subtract).then_inc(dm_ready, 1)

            def one_over_sum(b):
                dve.wait_ge(z_sum, b + 1)
                v.reciprocal(rz[:, :], bank[7][:, 0:256]).then_inc(rz_ready, 1)

            def probabilities(b):
                dve.wait_ge(rz_ps, b + 1)
                for g in range(4):
                    v.tensor_tensor(pr[:, 8 * g:8 * g + 8, :, :].rearrange("p n c h -> p (n c h)"),
                                    ex[:, 8 * g:8 * g + 8, :, :].rearrange("p n c h -> p (n c h)"),
                                    bank[g // 2][:, (g % 2) * 256:(g % 2) * 256 + 256], ALU.mult)\
                        .then_inc(pr_ready, 1)

            def amplitudes(b, r):
                dve.wait_ge(r_ps, b * 2 + r + 1)
                for h in range(2):
                    part = amp[:, h, 16 * r:16 * r + 16, :, :].rearrange("p n c h -> p (n c h)")
                    src = bank[(0, 1)[h] if r else (6, 7)[h]]
                    dve.wait_ge(abs_ready, b * 4 + 2 * r + h + 1)
                    c.link(v.tensor_scalar(part, part, 1e-6, 1.0, ALU.max, ALU.min))
                    ins = v.scalar_tensor_tensor(out=part.bitcast(U32), in0=src[:, :].bitcast(U32),
                                                 scalar=0x80000000, in1=part.bitcast(U32),
                                                 op0=ALU.bitwise_and, op1=ALU.bitwise_or)
                    ins.then_inc(amp_ready, 1)

            def circuits(b):
                dve.wait_ge(amp_ready, b * 4 + 4)
                if has_before(b):
                    dve.wait_ge(y_stored, b * 128)
                av = amp[:, :, :, :, :].rearrange("p h n c i -> p c i (h n)")
                c.link(v.tensor_scalar(mix[:, :, :], av[:, 0, :, :], sup[:, 0:1], None, ALU.mult))
                for q in range(1, CIRC):
                    ins = v.scalar_tensor_tensor(out=mix[:, :, :], in0=av[:, q, :, :], scalar=sup[:, q:q + 1],
                                                 in1=mix[:, :, :], op0=ALU.mult, op1=ALU.add)
                    if q < CIRC - 1:
                        c.link(ins)
                    else:
                        ins.then_inc(mix_ready, 1)

            def residual(b):
                dve.wait_ge(y_ps, b + 1)
                xi = x[:, bass.ds(b * S, S), :]
                v.tensor_tensor(xi, xi, bank[1][:, :].rearrange("p (s e) -> p s e", s=S), ALU.add)\
                    .then_inc(x1_ready, 1)
                dve.wait_ge(x1_ready, b + 1)

            def logits(r):
                dve.wait_ge(xn2T_ready, r + 1)
                hi = xhi[:, bass.ds(r * CHUNK, CHUNK)]
                c.link(v.tensor_copy(hi, xn2T[:, :]))
                c.step(v.tensor_tensor(xlo[:, bass.ds(r * CHUNK, CHUNK)], xn2T[:, :], hi.bitcast(F32), ALU.subtract))
                dve.wait_ge(lg_ps, r + 1)
                v.tensor_scalar(lg[:, :, :].rearrange("p s e -> p (s e)"), bank[1][:, 0:S * NE], -87.0, None,
                                ALU.max).then_inc(lg_ready, 1)

            def scores(r):
                dve.wait_ge(el_ready, r + 1)
                c.link(v.tensor_scalar(e1[:, :, :], el[:, :, :], 1.0, None, ALU.add))
                c.link(v.reciprocal(score[:, :, :], e1[:, :, :]))
                c.link(v.tensor_tensor(choice[:, :, :, :].rearrange("p s g k -> p s (g k)"), score[:, :, :],
                                       gbias[:, :].unsqueeze(1).to_broadcast([P, S, NE]), ALU.add))

            def groups(r):
                carry()
                for s in range(S):
                    for g in range(NG):
                        ins = v.max(top[:, s, g, :], choice[:, s, g, :])
                c.link(ins)
                c.link(v.tensor_tensor(gs[:, :, :], top[:, :, :, 0], top[:, :, :, 1], ALU.add))
                other = gs[:, :, :].unsqueeze(2).to_broadcast([P, S, NG, NG])
                own_g = gs[:, :, :].unsqueeze(3).to_broadcast([P, S, NG, NG])
                c.step(v.tensor_tensor(gt[:, :, :, :], other, own_g, ALU.is_gt))
                c.link(v.tensor_tensor(ge[:, :, :, :], other, own_g, ALU.is_equal))
                c.link(v.tensor_tensor(ge[:, :, :, :].rearrange("p s g k -> p s (g k)"),
                                       ge[:, :, :, :].rearrange("p s g k -> p s (g k)"),
                                       before[:, :, :].rearrange("p g k -> p (g k)").unsqueeze(1)
                                       .to_broadcast([P, S, NG * NG]), ALU.mult))
                c.link(v.tensor_tensor(gt[:, :, :, :], gt[:, :, :, :], ge[:, :, :, :], ALU.add))
                c.link(v.tensor_reduce(rank[:, :, :], gt[:, :, :, :], AX.X, ALU.add))
                c.link(v.tensor_scalar(gm[:, :, :], rank[:, :, :], TOPG - 0.5, None, ALU.is_lt))
                c.link(v.tensor_tensor(masked[:, :, :].rearrange("p s (g k) -> p s g k", g=NG), choice[:, :, :, :],
                                       gm[:, :, :].unsqueeze(3).to_broadcast([P, S, NG, NE // NG]), ALU.mult))

            def experts_picked(r):
                carry()
                for s in range(S):
                    k = c.step(v.max(best[:, s, :], masked[:, s, :]))
                c.after(k)
                carry()
                for s in range(S):
                    k = c.step(v.match_replace(out=rest[:, s, :], in_to_replace=best[:, s, :],
                                               in_values=masked[:, s, :], imm_value=TAKEN))
                c.after(k)
                c.link(v.scalar_tensor_tensor(out=picked[:, :, :], in0=rest[:, :, :], scalar=TAKEN / 2,
                                              in1=score[:, :, :], op0=ALU.is_lt, op1=ALU.mult))
                c.link(v.tensor_reduce(wsum[:, :], picked[:, :, :], AX.X, ALU.add))
                c.link(v.tensor_scalar(wsum[:, :], wsum[:, :], 1e-20, None, ALU.add))
                c.link(v.reciprocal(wr[:, :], wsum[:, :]))
                c.link(v.tensor_scalar(wr[:, :], wr[:, :], 2.5, None, ALU.mult))
                v.tensor_tensor(rw[:, :, :], picked[:, :, :], wr[:, :].unsqueeze(2).to_broadcast([P, S, NE]),
                                ALU.mult).then_inc(rw_ready, 1)

            def stages(f=None, b=None, r=None):
                if f is not None:
                    moments(f, st, mv, rt, var1)
                    normalise(f, mv, rt, std, rstd, std1, xn, xn_ready)
                if b is not None:
                    pattern_square(b)
                if r is not None:
                    residual(r)
                    moments(r, st2, mv2, rt2, var2)
                if f is not None:
                    project(f)
                if r is not None:
                    normalise(r, mv2, rt2, stdb, rstd2, std2, xn2, xn2_ready)
                if b is not None:
                    pattern_max(b)
                if f is not None:
                    norms(f)
                if b is not None:
                    pattern_less_max(b)
                if f is not None:
                    encode(f)
                if r is not None:
                    logits(r)
                if f is not None:
                    sign_values(f)
                if b is not None:
                    one_over_sum(b)
                if f is not None:
                    entangle(f, 0)
                if b is not None:
                    probabilities(b)
                if f is not None:
                    entangle(f, 1)
                if r is not None:
                    scores(r)
                if b is not None:
                    amplitudes(b, 0)
                if f is not None:
                    entangle(f, 2)
                if r is not None:
                    groups(r)
                if b is not None:
                    amplitudes(b, 1)
                    circuits(b)
                if r is not None:
                    experts_picked(r)

            stages(f=0)
            stages(f=1, b=0)
            before_loop = c.k
            with dve.Fori(0, NCHUNK - 2) as j:
                c.start(j * DVE_STEPS + before_loop)
                stages(f=j + 2, b=j + 1, r=j)
                assert c.k == DVE_STEPS, c.k
            c.start(before_loop + (NCHUNK - 2) * DVE_STEPS)
            stages(b=NCHUNK - 1, r=NCHUNK - 2)
            stages(r=NCHUNK - 1)

        @block.scalar
        def _(act):
            a_ = nc.scalar
            for dst, src in ((wout_in[:, :], wout_d), (bout[:, :], bout_d), (qw[:, :], qw_d),
                             (logit[:, :], logit_d), (phase[:, :], phase_d), (gates[:, :, :, :], gates_d)):
                act.dma_start(dst, src).then_inc(small_in, 16)
            act.dma_start(ratio[:, :], logit_d).then_inc(small_in, 16)
            act.wait_ge(sup_exp, 1)
            a_.activation(ratio[:, :], sup[:, :], ACT.Exp).then_inc(sup_exp, 1)
            act.wait_ge(angles, 1)
            a_.activation(sc[:, :, :], ang[:, :, :], ACT.Sin).then_inc(sines, 1)

            def deviation(n, rt, std, var, ready):
                act.wait_ge(var, n + 1)
                a_.activation(std[:, :], rt[:, :], ACT.Sqrt).then_inc(ready, 1)

            def transposed(n, dst, src, ps, ready):
                act.wait_ge(ps, n + 1)
                a_.activation(dst[:, :], src[:, :], ACT.Copy).then_inc(ready, 1)

            def squares(f):
                act.wait_ge(qkv_ready, f * S + S)
                a_.activation(sq[:, :, :, :].rearrange("p s h d -> p (s h d)"),
                              qkv[:, :, :, :].rearrange("p s h d -> p (s h d)"), ACT.Square).then_inc(sq_ready, 1)

            def norms(f):
                act.wait_ge(ss_ready, f + 1)
                a_.activation(rn[:, :], ss[:, :], ACT.Sqrt).then_inc(norm_ready, 1)

            def encoded(f):
                for w, bk, n in (("q", 2, 0), ("k", 4, 1)):
                    act.wait_ge(qkT_ps, f * 2 + n + 1)
                    a_.activation(state[w, "x"][:, :], bank[bk][:, :], ACT.Copy).then_inc(r_ready, 1)
                    a_.activation(ctrl[w][:, :], bank[bk][:, :], ACT.Square).then_inc(ctrl_ready[w], 1)

            def state_squares(f, k):
                for w in "qk":
                    act.wait_ge(state_ready[w], f * 6 + 2 * k)
                    for a in "xy":
                        ins = a_.activation(sqr[w, a][:, :], state[w, a][:, :], ACT.Square)
                    ins.then_inc(sqr_ready[w], 1)

            def negative(f):
                act.wait_ge(state_ready["q"], f * 6 + 6)
                if has_before(f):
                    act.wait_ge(q_stored, f * 64)
                a_.activation(fin_nqy[:, :], fin["q", "y"][:, :], ACT.Copy, scale=-1.0).then_inc(neg_ready, 1)

            def pattern_squares(b):
                act.wait_ge(pat_ps, b + 1)
                a_.activation(psq[:, :, :, :].rearrange("p n v h -> p (n v h)"), bank[6][:, :], ACT.Square)\
                    .then_inc(psq_ready, 1)

            def exponentials(b):
                act.wait_ge(dm_ready, b + 1)
                for q in range(CIRC):
                    a_.activation(ex[:, :, q, :], dm[:, :, :], ACT.Exp, scale=coef[:, q:q + 1]).then_inc(ex_ready, 1)

            def amplitudes(b):
                act.wait_ge(pr_ready, b * 4 + 4)
                a_.activation(am[:, :, :, :].rearrange("p n c h -> p (n c h)"),
                              pr[:, :, :, :].rearrange("p n c h -> p (n c h)"), ACT.Sqrt, bias=eps[:, 1:2])\
                    .then_inc(am_ready, 1)

            def magnitudes(b, r):
                act.wait_ge(r_ps, b * 2 + r + 1)
                for h in range(2):
                    a_.activation(amp[:, h, 16 * r:16 * r + 16, :, :].rearrange("p n c h -> p (n c h)"),
                                  bank[(0, 1)[h] if r else (6, 7)[h]][:, :], ACT.Abs).then_inc(abs_ready, 1)

            def sigmoid(r):
                act.wait_ge(lg_ready, r + 1)
                a_.activation(el[:, :, :], lg[:, :, :], ACT.Exp, scale=-1.0).then_inc(el_ready, 1)

            def routing_rows(r):
                act.wait_ge(rwT_ps, r + 1)
                a_.activation(rwT[:, bass.ds(r * 2, 2), :].rearrange("p b n -> p (b n)"), bank[0][:, 0:2 * P], ACT.Copy).then_inc(rwT_ready, 1)

            def stages(f=None, b=None, r=None):
                if f is not None:
                    deviation(f, rt, std, var1, std1)
                    transposed(f, xnT, bank[2], xT_ps, xT_ready)
                if b is not None:
                    pattern_squares(b)
                if r is not None:
                    deviation(r, rt2, stdb, var2, std2)
                    transposed(r, xn2T, bank[0], xn2T_ps, xn2T_ready)
                if f is not None:
                    squares(f)
                    norms(f)
                if b is not None:
                    exponentials(b)
                if r is not None:
                    sigmoid(r)
                if f is not None:
                    encoded(f)
                if b is not None:
                    amplitudes(b)
                if f is not None:
                    state_squares(f, 1)
                if b is not None:
                    magnitudes(b, 0)
                if f is not None:
                    state_squares(f, 2)
                if b is not None:
                    magnitudes(b, 1)
                if f is not None:
                    negative(f)
                if r is not None:
                    routing_rows(r)

            stages(f=0)
            stages(f=1, b=0)
            with act.Fori(0, NCHUNK - 2) as j:
                stages(f=j + 2, b=j + 1, r=j)
            stages(b=NCHUNK - 1, r=NCHUNK - 2)
            stages(r=NCHUNK - 1)

        @block.tensor
        def _(pe):
            t = nc.tensor
            pe.wait_ge(tables_ready, 1)
            pe.wait_ge(w_in, 16 * 4)

            def transpose_x(n, bk, src, ready, ps):
                pe.wait_ge(ready, n * S + S)
                for s in range(S):
                    ins = t.transpose(bk[:, s * P:(s + 1) * P], src[:, s, :], ident[:, :])
                ins.then_inc(ps, 1)

            def project(f):
                pe.wait_ge(xT_ready, f + 1)
                for s in range(S):
                    t.matmul(bank[(3, 4, 5, 2)[s]][:, 0:3 * E], xnT[:, s * P:(s + 1) * P], wqkv[:, :],
                             start=True, stop=True).then_inc(qkv_ps, 1)

            def encode(f):
                for n, bk in ((0, 2), (1, 4)):
                    pe.wait_ge(qk_ready, f * 2 + n + 1)
                    for s in range(S):
                        ins = t.transpose(bank[bk][:, s * P:(s + 1) * P],
                                          qkv[:, s, n * HEADS:(n + 1) * HEADS, :].rearrange("p h d -> p (h d)"),
                                          ident[:, :])
                    ins.then_inc(qkT_ps, 1)

            def entangle(f, k):
                for n, (w, bk) in enumerate((("q", 2), ("k", 4))):
                    sx, sy = state[w, "x"], state[w, "y"]
                    if k == 0:
                        pe.wait_ge(r_ready, f * 2 + n + 1)
                        pe.wait_ge(ctrl_ready[w], f * DEPTH + 1)
                        t.matmul(bank[bk][:, :], maps[:, 0, 0, :], sx[:, :], start=True, stop=True)\
                            .then_inc(z_ps[w], 1)
                        t.matmul(bank[bk + 1][:, :], maps[:, 0, 1, :], sx[:, :], start=True, stop=True)\
                            .then_inc(z_ps[w], 1)
                        continue
                    pe.wait_ge(state_ready[w], f * 6 + 2 * k)
                    t.matmul(bank[bk][:, :], maps[:, k, 0, :], sx[:, :], start=True, stop=False)
                    t.matmul(bank[bk][:, :], maps[:, k, 2, :], sy[:, :], start=False, stop=True)\
                        .then_inc(z_ps[w], 1)
                    t.matmul(bank[bk + 1][:, :], maps[:, k, 1, :], sx[:, :], start=True, stop=False)
                    t.matmul(bank[bk + 1][:, :], maps[:, k, 0, :], sy[:, :], start=False, stop=True)\
                        .then_inc(z_ps[w], 1)

            def pattern(b, part):
                if part == 0:
                    pe.wait_ge(k_loaded, b * 128 + 128)
                    pe.wait_ge(q_loaded, b * 128 + 128)
                for n in range(64 * part, 64 * part + 64):
                    n4, n1 = 2 * (n // NP % 2) + n // (2 * NP), n % NP
                    ins = t.matmul(bank[6][32 * n4:32 * n4 + 32, n1 * 16:n1 * 16 + 16],
                                   kbd[:, :, :, n].rearrange("p s h -> p s h"), qs[:, :, :, n],
                                   start=True, stop=True)
                if part == 1:
                    ins.then_inc(pat_ps, 1)

            def pattern_max(b):
                pe.wait_ge(pt_ready, b + 1)
                for a in range(2):
                    ins = t.transpose(bank[7][:, a * P:(a + 1) * P],
                                      pt[:, 16 * a:16 * a + 16, :].rearrange("p n h -> p (n h)"), ident[:, :])
                ins.then_inc(ptT_ps, 1)

            def max_back(b):
                pe.wait_ge(mb_ready, b + 1)
                for a in range(2):
                    ins = t.transpose(bank[6][:, a * P:(a + 1) * P],
                                      mb[:, a, :, :].rearrange("p m j -> p (m j)"), ident[:, :])
                ins.then_inc(mbT_ps, 1)

            def sums(b):
                pe.wait_ge(ex_ready, b * 4 + 4)
                for g in range(4):
                    ins = t.matmul(bank[7][32 * g:32 * g + 32, 0:256], pair_sum[:, :],
                                   ex[:, 8 * g:8 * g + 8, :, :].rearrange("p n c h -> p (n c h)"),
                                   start=True, stop=True)
                ins.then_inc(z_sum, 1)

            def sums_back(b):
                pe.wait_ge(rz_ready, b + 1)
                for g in range(4):
                    ins = t.matmul(bank[g // 2][:, (g % 2) * 256:(g % 2) * 256 + 256], pair_back[:, g, :], rz[:, :],
                                   start=True, stop=True)
                ins.then_inc(rz_ps, 1)

            def weigh(b, r):
                if r == 0:
                    pe.wait_ge(v_loaded, b * 256 + 256)
                    pe.wait_ge(am_ready, b + 1)
                for n in range(16):
                    n1 = 16 * r + n
                    for h in range(2):
                        bk = (0, 1)[h] if r else (6, 7)[h]
                        ins = t.matmul(bank[bk][:, n * 32:n * 32 + 32],
                                       vbd[64 * h:64 * h + 64, n1, :, :].rearrange("p t d -> p (t d)"),
                                       am[64 * h:64 * h + 64, n1, :, :].rearrange("p c h -> p (c h)"),
                                       start=True, stop=True)
                ins.then_inc(r_ps, 1)

            def output(b):
                pe.wait_ge(y_loaded, b * 16 + 16)
                for s in range(S):
                    out = bank[1][:, s * P:(s + 1) * P]
                    t.matmul(out, yin[:, 2 * s:2 * s + 2, :].rearrange("p f c -> p (f c)"), wout[:, :],
                             start=True, stop=False)
                    ins = t.matmul(out, ones[0:1, :], bout[0:1, :], start=False, stop=True)
                ins.then_inc(y_ps, 1)

            def logits(r):
                pe.wait_ge(xn2T_ready, r + 1)
                for s in range(S):
                    ins = t.matmul(bank[1][:, s * NE:(s + 1) * NE], xn2T[:, s * P:(s + 1) * P], gwt[:, :],
                                   start=True, stop=True)
                ins.then_inc(lg_ps, 1)

            def routing_rows(r):
                pe.wait_ge(rw_ready, r + 1)
                for a in range(S // 2):
                    ins = t.transpose(bank[0][:, a * P:(a + 1) * P],
                                      rw[:, 2 * a:2 * a + 2, :].rearrange("p s e -> p (s e)"), ident[:, :])
                ins.then_inc(rwT_ps, 1)

            def stages(f=None, b=None, r=None):
                if b is not None:
                    pattern(b, 0)
                if f is not None:
                    transpose_x(f, bank[2], xn, xn_ready, xT_ps)
                if b is not None:
                    pattern(b, 1)
                if r is not None:
                    output(r)
                if f is not None:
                    project(f)
                if b is not None:
                    pattern_max(b)
                if r is not None:
                    transpose_x(r, bank[0], xn2, xn2_ready, xn2T_ps)
                if b is not None:
                    max_back(b)
                if f is not None:
                    encode(f)
                if r is not None:
                    logits(r)
                if b is not None:
                    sums(b)
                if f is not None:
                    entangle(f, 0)
                if b is not None:
                    sums_back(b)
                if f is not None:
                    entangle(f, 1)
                if b is not None:
                    weigh(b, 0)
                if f is not None:
                    entangle(f, 2)
                if b is not None:
                    weigh(b, 1)
                if r is not None:
                    routing_rows(r)

            stages(f=0)
            stages(f=1, b=0)
            with pe.Fori(0, NCHUNK - 2) as j:
                stages(f=j + 2, b=j + 1, r=j)
            stages(b=NCHUNK - 1, r=NCHUNK - 2)
            stages(r=NCHUNK - 1)


def experts(nc, wpack_d, rw_d, out_rows, x, xhi, xlo, ident, bank):
    with ExitStack() as ctx:
        def sb(name, shape, dt=F32):
            return ctx.enter_context(nc.sbuf_tensor(name, shape, dt))

        def sem(name):
            return ctx.enter_context(nc.semaphore(name))

        RING = 4
        win = sb("win", [P, PERIOD, 3, P])
        whi = sb("whi", [P, PERIOD, 3, P], F32R)
        wlo = sb("wlo", [P, PERIOD, 3, P], F32R)
        rwb = sb("rwb", [P, PERIOD, T])
        act_g = sb("act_g", [P, RING, CHUNK])
        act_u = sb("act_u", [P, RING, CHUNK])
        hid = act_u
        hhi = sb("hhi", [P, RING, CHUNK], F32R)
        hlo = sb("hlo", [P, RING, CHUNK], F32R)
        outT = act_g

        w_loaded = [sem(f"w_loaded{b}") for b in range(PERIOD)]
        r_loaded = [sem(f"r_loaded{b}") for b in range(PERIOD)]
        whi_ready, wlo_ready, gate_ps, up_ps, silu_ready, au_ready, hid_ready, hhi_ready, hlo_ready, down_ps = (
            sem(n) for n in ("whi_ready", "wlo_ready", "gate_ps", "up_ps", "silu_ready", "au_ready", "hid_ready",
                             "hhi_ready", "hlo_ready", "down_ps"))
        outT_ready, outT_ps, res_ready, stored = (sem(n) for n in ("outT_ready", "outT_ps", "res_ready", "stored"))
        segs = segments()
        per_block = [sum(1 for s in segs if s[0] == b) for b in range(PERIOD)]
        SH = MT * NCHUNK

        block = ctx.enter_context(nc.Block())

        @block.sync
        def _(sp):
            def period(i, first):
                for b in range(PERIOD):
                    if not first:
                        sp.wait_ge(wlo_ready, (i - 1) * PERIOD + b + 1)
                        sp.nop(nofuse=True)
                    sp.dma_start(win[:, b, :, :], wpack_d[bass.ds(i * PERIOD + b, 1)]
                                 .rearrange("a p k c -> p (a k) c")).then_inc(w_loaded[b], 16)
                    if not first:
                        sp.wait_ge(hid_ready, (i - 1) * UNITS + (b + 1) * NCHUNK)
                    for _, r, n, e in [s for s in segs if s[0] == b]:
                        row = rw_d[bass.ds(i * EXPERTS + e, 1), :]
                        sp.dma_start(rwb[r:r + n, b, :], row.to_broadcast([n, T])).then_inc(r_loaded[b], 16)

            period(0, True)
            with sp.Fori(1, PERIODS) as i:
                period(i, False)
            for b in range(2):
                sp.wait_ge(wlo_ready, MT - PERIOD + b + 1)
                sp.dma_start(win[:, b, :, :], wpack_d[MT + b]).then_inc(w_loaded[b], 16)
            for c in range(NCHUNK):
                sp.wait_ge(res_ready, c + 1)
                sp.dma_start(out_rows[c * CHUNK:(c + 1) * CHUNK, :].rearrange("(s p) e -> p s e", p=P),
                             x[:, c * S:(c + 1) * S, :]).then_inc(stored, 16)
            sp.wait_ge(stored, 16 * NCHUNK)

        @block.gpsimd
        def _(pool):
            def unit(u, b, q, slot):
                pool.wait_ge(silu_ready, u + 1)
                pool.wait_ge(au_ready, u + 1)
                nc.gpsimd.tensor_tensor(hid[:, slot, :], act_g[:, slot, :], act_u[:, slot, :], ALU.mult)\
                    .then_inc(hid_ready, 1)

            def period(i, first):
                for b in range(PERIOD):
                    for q in range(NCHUNK):
                        u = b * NCHUNK + q
                        if not (first and u < RING):
                            pool.wait_ge(hlo_ready, i * UNITS + u - RING + 1)
                        unit(i * UNITS + u, b, q, u % RING)

            period(0, True)
            with pool.Fori(1, PERIODS) as i:
                period(i, False)
            for b in range(2):
                for q in range(NCHUNK):
                    u = SH + b * NCHUNK + q
                    pool.wait_ge(hlo_ready, u - RING + 1)
                    pool.wait_ge(silu_ready, u + 1)
                    pool.wait_ge(au_ready, u + 1)
                    nc.gpsimd.tensor_tensor(hid[0:NI, u % RING, :], act_g[0:NI, u % RING, :],
                                            act_u[0:NI, u % RING, :], ALU.mult).then_inc(hid_ready, 1)

        @block.scalar
        def _(act):
            a_ = nc.scalar

            def silu(u, slot, rows, wait_slot):
                act.wait_ge(gate_ps, u + 1)
                if wait_slot:
                    act.wait_ge(hid_ready, u - RING + 1)
                a_.activation(act_g[0:rows, slot, :], bank[4 + slot % 2][0:rows, :], ACT.Silu).then_inc(silu_ready, 1)

            def high(u, slot, rows, wait_slot):
                act.wait_ge(hid_ready, u + 1)
                if wait_slot:
                    act.wait_ge(down_ps, u - RING + 1)
                a_.activation(hhi[0:rows, slot, :], hid[0:rows, slot, :], ACT.Copy).then_inc(hhi_ready, 1)

            def period(i, first):
                for b in range(PERIOD):
                    for q in range(NCHUNK):
                        u = b * NCHUNK + q
                        silu(i * UNITS + u, u % RING, P, not (first and u < RING))
                        if not (first and u < 2):
                            v = u - 2
                            high(i * UNITS + v, v % RING, P, not (first and v < RING))

            period(0, True)
            with act.Fori(1, PERIODS) as i:
                period(i, False)
            for n in range(2 * NCHUNK):
                u = SH + n
                silu(u, u % RING, NI, True)
                high(u - 2, (u - 2) % RING, P if n < 2 else NI, True)
            for u in (SH + 2 * NCHUNK - 2, SH + 2 * NCHUNK - 1):
                high(u, u % RING, NI, True)
            for c in range(NCHUNK):
                act.wait_ge(down_ps, SH + NCHUNK + c + 1)
                a_.activation(outT[:, c, :], bank[c][:, :], ACT.Copy).then_inc(outT_ready, 1)

        @block.vector
        def _(dve):
            v = nc.vector

            def split(b):
                v.tensor_copy(whi[:, b, :, :], win[:, b, :, :]).then_inc(whi_ready, 1)

            def split_lo(n, b):
                dve.wait_ge(whi_ready, n)
                v.tensor_tensor(wlo[:, b, :, :], win[:, b, :, :], whi[:, b, :, :].bitcast(F32), ALU.subtract)\
                    .then_inc(wlo_ready, 1)

            def up(u, slot, rows, b, q, wait_slot):
                dve.wait_ge(up_ps, u + 1)
                if wait_slot:
                    dve.wait_ge(hlo_ready, u - RING + 1)
                src, dst = bank[6 + slot % 2][0:rows, :], act_u[0:rows, slot, :]
                if b is None:
                    v.tensor_copy(dst, src).then_inc(au_ready, 1)
                else:
                    v.tensor_tensor(dst, src, rwb[:, b, q * CHUNK:(q + 1) * CHUNK], ALU.mult).then_inc(au_ready, 1)

            def low(u, slot, rows, wait_slot):
                dve.wait_ge(hhi_ready, u + 1)
                if wait_slot:
                    dve.wait_ge(down_ps, u - RING + 1)
                v.tensor_tensor(hlo[0:rows, slot, :], hid[0:rows, slot, :], hhi[0:rows, slot, :].bitcast(F32),
                                ALU.subtract).then_inc(hlo_ready, 1)

            AHEAD = 2

            def period(i, first):
                for b in range(PERIOD):
                    for q in range(NCHUNK):
                        u = b * NCHUNK + q
                        if q == 0:
                            dve.wait_ge(r_loaded[b], 16 * per_block[b] * (i + 1))
                        if q == 1:
                            nb = (b + AHEAD) % PERIOD
                            wrap = b + AHEAD >= PERIOD
                            dve.wait_ge(w_loaded[nb], 16 * (i + 1 + wrap))
                            if wrap or not first:
                                dve.wait_ge(down_ps, i * UNITS + (b + AHEAD + 1 - PERIOD) * NCHUNK)
                            split(nb)
                        if q == 2:
                            nb = (b + AHEAD) % PERIOD
                            split_lo(i * PERIOD + b + AHEAD + 1, nb)
                        up(i * UNITS + u, u % RING, P, b, q, not (first and u < RING))
                        if not (first and u < 2):
                            w = u - 2
                            low(i * UNITS + w, w % RING, P, not (first and w < RING))

            for b in range(AHEAD):
                dve.wait_ge(w_loaded[b], 16)
                split(b)
                split_lo(b + 1, b)
            period(0, True)
            with dve.Fori(1, PERIODS) as i:
                period(i, False)
            for n in range(2 * NCHUNK):
                u = SH + n
                up(u, u % RING, NI, None, None, True)
                low(u - 2, (u - 2) % RING, P if n < 2 else NI, True)
            for u in (SH + 2 * NCHUNK - 2, SH + 2 * NCHUNK - 1):
                low(u, u % RING, NI, True)
            for c in range(NCHUNK):
                dve.wait_ge(outT_ps, c + 1)
                xi = slice(c * S, (c + 1) * S)
                v.tensor_tensor(x[:, xi, :], x[:, xi, :], bank[4 + c][:, :].rearrange("p (s e) -> p s e", s=S),
                                ALU.add).then_inc(res_ready, 1)

        @block.tensor
        def _(pe):
            t = nc.tensor

            def three(out, hi, lo, mhi, mlo, start, stop):
                t.matmul(out, hi, mhi, start=start, stop=False)
                t.matmul(out, hi, mlo, start=False, stop=False)
                return t.matmul(out, lo, mhi, start=False, stop=stop)

            def up(u, slot, rows, hi, lo, q, wait_slot):
                xs = slice(q * CHUNK, (q + 1) * CHUNK)
                if wait_slot:
                    pe.wait_ge(silu_ready, u - 1)
                three(bank[4 + slot % 2][0:rows, :], hi[:, 0, 0:rows], lo[:, 0, 0:rows], xhi[:, xs], xlo[:, xs],
                      True, True).then_inc(gate_ps, 1)
                if wait_slot:
                    pe.wait_ge(au_ready, u - 1)
                three(bank[6 + slot % 2][0:rows, :], hi[:, 1, 0:rows], lo[:, 1, 0:rows], xhi[:, xs], xlo[:, xs],
                      True, True).then_inc(up_ps, 1)

            def down(u, slot, rows, hi, lo, q, start, stop):
                pe.wait_ge(hlo_ready, u + 1)
                three(bank[q][:, :], hi[0:rows, 2, :], lo[0:rows, 2, :], hhi[0:rows, slot, :], hlo[0:rows, slot, :],
                      start, stop).then_inc(down_ps, 1)

            def period(i, first):
                for b in range(PERIOD):
                    pe.wait_ge(wlo_ready, i * PERIOD + b + 1)
                    for q in range(NCHUNK):
                        u = b * NCHUNK + q
                        up(i * UNITS + u, u % RING, P, whi[:, b], wlo[:, b], q,
                           not (first and u < 2))
                        if not (first and u < LAG):
                            w = (u - LAG) % UNITS
                            wb = w // NCHUNK
                            down(i * UNITS + u - LAG, w % RING, P, whi[:, wb], wlo[:, wb], w % NCHUNK,
                                 first and w < NCHUNK, False)

            period(0, True)
            with pe.Fori(1, PERIODS) as i:
                period(i, False)
            for n in range(2 * NCHUNK + LAG):
                u = SH + n
                if n < 2 * NCHUNK:
                    if n % NCHUNK == 0:
                        pe.wait_ge(wlo_ready, MT + n // NCHUNK + 1)
                    up(u, u % RING, NI, whi[:, n // NCHUNK], wlo[:, n // NCHUNK], n % NCHUNK, True)
                w = u - LAG
                if n < LAG:
                    wb = (UNITS - LAG + n) // NCHUNK
                    down(w, w % RING, P, whi[:, wb], wlo[:, wb], w % NCHUNK, False, False)
                else:
                    m = n - LAG
                    down(w, w % RING, NI, whi[:, m // NCHUNK], wlo[:, m // NCHUNK], m % NCHUNK, False,
                         m >= NCHUNK)
            for c in range(NCHUNK):
                pe.wait_ge(outT_ready, c + 1)
                for s in range(S):
                    ins = t.transpose(bank[4 + c][:, s * P:(s + 1) * P],
                                      outT[:, c, s * P:(s + 1) * P], ident[:, :])
                ins.then_inc(outT_ps, 1)


def _layouts(np_, i):
    c = np_.ascontiguousarray

    def rows(a):
        return c(np_.broadcast_to(a[None, :], (P, a.shape[0])))

    def blocks(g, u, d):
        n, k, _ = g.shape
        out = np_.zeros((n, P, 3, P), np_.float32)
        out[:, :, 0, :k] = g.transpose(0, 2, 1)
        out[:, :, 1, :k] = u.transpose(0, 2, 1)
        out[:, :k, 2, :] = d
        return out

    pre, ffn = "L0_attn_", "L0_ffn_"
    gates = i[pre + "entanglement_gates"][:, :, 0:2]
    own = np_.repeat(gates, D, axis=1).transpose(1, 0, 2)
    prev = np_.repeat(np_.roll(gates, 1, axis=1), D, axis=1).transpose(1, 0, 2)
    wg = i[ffn + "Wg"].reshape(MT, P, E)
    wu = i[ffn + "Wu"].reshape(MT, P, E)
    wd = i[ffn + "Wd"].transpose(0, 2, 1).reshape(MT, P, E)
    shared = blocks(i[ffn + "Sg"].reshape(2, NI, E), i[ffn + "Su"].reshape(2, NI, E),
                    i[ffn + "Sd"].T.reshape(2, NI, E))
    return {
        "x": c(i[pre + "query"]),
        "wqkv": c(i[pre + "W_qkv"].T),
        "bqkv": rows(i[pre + "b_qkv"]),
        "wout": c(i[pre + "W_out"].T),
        "bout": rows(i[pre + "b_out"]),
        "qw": rows(i[pre + "quantum_weights"][:, 0, 0]),
        "phase": c(np_.tile(np_.diagonal(i[pre + "photonic_phases"][:D, :D]), HEADS)[:, None]),
        "gates": c(np_.stack([own, prev], axis=2)),
        "logit": rows(i[pre + "superposition_logits"]),
        "gw": c(i[ffn + "gate_w"].T),
        "gbias": rows(i[ffn + "gate_bias"]),
        "wpack": np_.concatenate([blocks(wg, wu, wd), shared]),
    }


def kernel(**inputs):
    import concourse.bacc as _bacc
    from concourse import mybir as _mybir
    from concourse.bass_utils import run_bass_kernel_spmd as _run

    nc = _bacc.Bacc("TRN2", target_bir_lowering=False, num_devices=1)
    arrays = _layouts(np, {k: np.asarray(v) for k, v in inputs.items()})
    args = [nc.dram_tensor(f"in_{n}", a.shape, _mybir.dt.float32, kind="ExternalInput").ap()
            for n, a in arrays.items()]
    out = nc.dram_tensor("out_0", (2, 1024, E), _mybir.dt.float32, kind="ExternalOutput").ap()
    build(nc, *args, out)
    r = _run(nc, [{f"in_{n}": a for n, a in arrays.items()}], core_ids=[0])
    return r.results[0]["out_0"]
```

```python
from contextlib import ExitStack

import numpy as np

import concourse.bass as bass
from concourse import mybir

F32 = mybir.dt.float32
F32R = mybir.dt.float32r
U32 = mybir.dt.uint32
ALU = mybir.AluOpType
ACT = mybir.ActivationFunctionType
AX = mybir.AxisListType

P = 128
T, E = 2048, 128
HEADS, D, CIRC, DEPTH = 8, 16, 4, 3
CHUNK = 512
NCHUNK = T // CHUNK
S = CHUNK // P
TILES = T // P
N4 = 4
NP = P // N4
NQ = 16
NE, NI, NG, TOPG, TOPK = 64, 88, 8, 4, 8
SCALING = D ** -0.5
LN_EPS = 1e-5
PI = float(np.pi)
TWO_PI_A = 6.28125
TWO_PI_B = float((np.array([2 * np.pi - TWO_PI_A], np.float32).view(np.uint32) & np.uint32(0xFFFFF000))
                 .view(np.float32)[0])
TWO_PI_C = float(2 * np.pi - TWO_PI_A - TWO_PI_B)
ROUND = 1.5 * 2.0 ** 23
PI_SAFE = 3.1415925
TAKEN = -3.0e38

ROWS = NE * NI
MT = ROWS // P
PERIOD = 11
PERIODS = MT // PERIOD
EXPERTS = PERIOD * P // NI
LAG = 4
UNITS = PERIOD * NCHUNK

A_HALF, A_PREV, A_PHASE, A_PHASE2, A_CIRC = 0, 3, 6, 7, 8
NANG = 12


def segments():
    out = []
    for b in range(PERIOD):
        r = 0
        while r < P:
            e = (b * P + r) // NI
            n = min(P - r, (e + 1) * NI - (b * P + r))
            out.append((b, r, n, e))
            r += n
    return out


class Chain:

    def __init__(self, eng, sem):
        self.eng, self.sem, self.base, self.k = eng, sem, 0, 0

    def start(self, base):
        self.base, self.k = base, 0

    def step(self, ins):
        ins.then_inc(self.sem, 1)
        self.k += 1
        return self.k

    def after(self, k):
        self.eng.wait_ge(self.sem, self.base + k)

    def link(self, ins):
        self.after(self.step(ins))


DVE_STEPS = 63
QUARTERS = ((0, 6), (2, 7), (1, 0), (3, 1))


def has_before(n):
    return not (isinstance(n, int) and n == 0)


def build(nc, x_d, wqkv_d, bqkv_d, wout_d, bout_d, qw_d, phase_d, gates_d, logit_d,
          gw_d, gbias_d, wpack_d, out_d):
    x_rows = x_d.rearrange("b s e -> (b s) e")
    out_rows = out_d.rearrange("b s e -> (b s) e")

    def dram(name, shape):
        return nc.dram_tensor(name, shape, F32, kind="Internal").ap()

    v_d = dram("v_rows", [T, E])
    k_d = dram("k_strips", [NCHUNK, S, 2, HEADS, D, P])
    q_d = dram("q_strips", [NCHUNK, S, 2, 2, HEADS, D, P])
    y_d = dram("y_rows", [NCHUNK, NQ, HEADS, D, P // S])
    rw_d = dram("rw_rows", [NE, T])

    with ExitStack() as whole:
        def sem(name):
            return whole.enter_context(nc.semaphore(name))

        def keep(name, shape, dt=F32):
            return whole.enter_context(nc.sbuf_tensor(name, shape, dt))

        x = keep("x", [P, TILES, E])
        xhi = keep("xhi", [E, T], F32R)
        xlo = keep("xlo", [E, T], F32R)
        ident = keep("ident", [P, P])
        win = keep("win", [P, PERIOD, 3, P])
        w_loaded = [sem(f"w_loaded{b}") for b in range(PERIOD)]
        bank = [whole.enter_context(nc.psum_tensor(f"bank{n}", [P, 512], F32)) for n in range(8)]

        attention(nc, x_rows, wqkv_d, bqkv_d, wout_d, bout_d, qw_d, phase_d, gates_d, logit_d,
                  gw_d, gbias_d, v_d, k_d, q_d, y_d, rw_d, wpack_d, win, w_loaded, x, xhi, xlo, ident, bank)
        experts(nc, wpack_d, win, w_loaded, rw_d, out_rows, x, xhi, xlo, ident, bank)


def attention(nc, x_rows, wqkv_d, bqkv_d, wout_d, bout_d, qw_d, phase_d, gates_d, logit_d,
              gw_d, gbias_d, v_d, k_d, q_d, y_d, rw_d, wpack_d, win, w_loaded, x, xhi, xlo, ident, bank):
    with ExitStack() as ctx:
        def sb(name, shape, dt=F32):
            return ctx.enter_context(nc.sbuf_tensor(name, shape, dt))

        def sem(name):
            return ctx.enter_context(nc.semaphore(name))

        wqkv = sb("wqkv", [E, 3 * E])
        bqkv = sb("bqkv", [P, 3 * E])
        gwt = sb("gwt", [E, NE])
        gbias = sb("gbias", [P, NE])
        wout = sb("wout", [P, E])
        wout_in = sb("wout_in", [P, E])
        bout = sb("bout", [P, E])
        qw = sb("qw", [P, CIRC])
        logit = sb("logit", [P, CIRC])
        phase = sb("phase", [P, 1])
        gates = sb("gates", [P, DEPTH, 2, 2])
        own_head = sb("own_head", [P, 1])
        shift = sb("shift", [P, P])
        stay = sb("stay", [P, P])
        maps = sb("maps", [P, DEPTH, 3, P])
        ang = sb("ang", [P, 2, NANG])
        turns = sb("turns", [P, 2, NANG])
        sc = sb("sc", [P, 2, NANG])
        gain = sb("gain", [P, DEPTH, 2])
        first = sb("first", [P, 2, 2])
        ratio = sb("ratio", [P, CIRC])
        coef = sb("coef", [P, CIRC])
        coef_t = sb("coef_t", [P, CIRC])
        sup = sb("sup", [P, CIRC])
        sup_s = sb("sup_s", [P, 4])
        eps = sb("eps", [P, 2])
        tick = sb("tick", [P, 16])
        pair_sum = sb("pair_sum", [P, 32])
        pair_back = sb("pair_back", [P, 4, P])
        before = sb("before", [P, NG, NG])
        st = sb("st", [P, S, 6])
        mv = sb("mv", [P, S, 2])
        std = sb("std", [P, S])
        rstd = sb("rstd", [P, S])
        rt = sb("rt", [P, S])
        st2 = sb("st2", [P, S, 6])
        mv2 = sb("mv2", [P, S, 2])
        stdb = sb("stdb", [P, S])
        rstd2 = sb("rstd2", [P, S])
        rt2 = sb("rt2", [P, S])
        xn = sb("xn", [P, S, E])
        xnT = sb("xnT", [E, CHUNK])
        qkv = sb("qkv", [P, S, 3 * HEADS, D])
        ss = sb("ss", [P, S * 3 * HEADS])
        rn = sb("rn", [P, S * 3 * HEADS])
        vs = sb("vs", [P, S, D])
        vg = sb("vg", [P, S, D])
        vsg = sb("vsg", [P, S, HEADS, D])
        state = {(w, a): sb(f"state_{w}{a}", [P, CHUNK]) for w in "qk" for a in "xy"}
        sqr_all = sb("sqr_all", [P, 4, CHUNK])
        sqr = {(w, a): sqr_all[:, 2 * n + m, :] for n, w in enumerate("qk") for m, a in enumerate("xy")}
        sq = sqr_all[:, 0:3, :].rearrange("p a (b d) -> p (a b) d", d=D)\
            .rearrange("p (s h) d -> p s h d", s=S)
        ctrl = {w: sb(f"ctrl_{w}", [P, CHUNK]) for w in "qk"}
        gain_t = {(w, a): sb(f"gain_{w}{a}", [P, CHUNK]) for w in "qk" for a in "xy"}
        fin = {(w, a): sb(f"fin_{w}{a}", [P, CHUNK]) for w, a in ("qx", "qy", "kx", "ky")}
        fin_nqy = sb("fin_nqy", [P, CHUNK])
        kbd = sb("kbd", [P, S, HEADS, P])
        qs = sb("qs", [P, 2, HEADS, P])
        vbd = sb("vbd", [P, NP, 8, D])
        psq = sb("psq", [P, NP, 2, HEADS])
        pt = sb("pt", [P, NP, HEADS])
        mx = sb("mx", [P, 2, 16])
        mb = sb("mb", [P, 2, 16, 8])
        dm = sb("dm", [P, NP, HEADS])
        ex = sb("ex", [P, NP, CIRC, HEADS])
        rz = sb("rz", [P, 256])
        pr = am = ex
        amp = sb("amp", [P, 4, CHUNK])
        mix = sb("mix", [P, CHUNK])
        yin = sb("yin", [P, NQ, P // S])
        circ = sb("circ", [P, CIRC, 32])
        circ_sum = sb("circ_sum", [P, 32])
        xn2 = sb("xn2", [P, S, E])
        xn2T = sb("xn2T", [E, CHUNK])
        lg = sb("lg", [P, S, NE])
        el = sb("el", [P, S, NE])
        score = sb("score", [P, S, NE])
        choice = sb("choice", [P, S, NG, NE // NG])
        top = sb("top", [P, S, NG, 8])
        gs = sb("gs", [P, S, NG])
        gt = sb("gt", [P, S, NG, NG])
        ge = sb("ge", [P, S, NG, NG])
        rank = sb("rank", [P, S, NG])
        gm = sb("gm", [P, S, NG])
        masked = sb("masked", [P, S, NE])
        best = sb("best", [P, S, 8])
        rest = e1 = sb("rest", [P, S, NE])
        picked = sb("picked", [P, S, NE])
        wsum = sb("wsum", [P, S])
        wr = sb("wr", [P, S])
        rw = sb("rw", [P, S + TILES, NE])
        rwT = sb("rwT", [P, NCHUNK * 2, P])

        (x0_in, x_in, small_in, w_in, gw_in, zeroed, x_split, tick_set, biased, map0_ready, gains_tabled,
         maps_tabled) = (sem(n) for n in (
             "x0_in", "x_in", "small_in", "w_in", "gw_in", "zeroed", "x_split", "tick_set", "biased", "map0_ready",
             "gains_tabled", "maps_tabled"))
        v_stored, v_loaded = sem("v_stored"), sem("v_loaded")
        k_stored, k_loaded = sem("k_stored"), sem("k_loaded")
        q_stored, q_loaded = sem("q_stored"), sem("q_loaded")
        y_stored, y_loaded = sem("y_stored"), sem("y_loaded")
        rw_stored = sem("rw_stored")
        consts, angles, sines, tables_ready, sup_exp = (
            sem(n) for n in ("consts", "angles", "sines", "tables_ready", "sup_exp"))
        dve_s, act_s, pool_s = sem("dve_steps"), sem("act_steps"), sem("pool_steps")
        (var1, std1, xn_ready, xT_ps, xT_ready, qkv_ps, qkv_ready, sq_ready, ss_ready, norm_ready,
         qk_ready, vsg_ready, qkT_ps, r_ready) = (sem(n) for n in (
             "var1", "std1", "xn_ready", "xT_ps", "xT_ready", "qkv_ps", "qkv_ready", "sq_ready", "ss_ready",
             "norm_ready", "qk_ready", "vsg_ready", "qkT_ps", "r_ready"))
        z_ps = {w: sem(f"z_ps_{w}") for w in "qk"}
        sqr_ready = {w: sem(f"sqr_ready_{w}") for w in "qk"}
        ctrl_ready = {w: sem(f"ctrl_ready_{w}") for w in "qk"}
        gain_ready = {w: sem(f"gain_ready_{w}") for w in "qk"}
        state_ready = {w: sem(f"state_ready_{w}") for w in "qk"}
        neg_ready, abs_ready = sem("neg_ready"), sem("abs_ready")
        (pat_ps, psq_ready, pt_ready, ptT_ps, mb_ready, mbT_ps, dm_ready, ex_ready, z_sum, rz_ready, rz_ps,
         pr_ready, am_ready, r_ps, amp_ready, mix_ps, mix_ready, y_ps, x1_ready) = (sem(n) for n in (
             "pat_ps", "psq_ready", "pt_ready", "ptT_ps", "mb_ready", "mbT_ps", "dm_ready", "ex_ready", "z_sum",
             "rz_ready", "rz_ps", "pr_ready", "am_ready", "r_ps", "amp_ready", "mix_ps", "mix_ready",
             "y_ps", "x1_ready"))
        (var2, std2, xn2_ready, xn2T_ps, xn2T_ready, lg_ps, lg_ready, el_ready, rw_ready, rwT_ps,
         rwT_ready) = (sem(n) for n in (
             "var2", "std2", "xn2_ready", "xn2T_ps", "xn2T_ready", "lg_ps", "lg_ready", "el_ready", "rw_ready",
             "rwT_ps", "rwT_ready"))

        sh_in = qkv[:, :, :, :].rearrange("p s h d -> p (s h d)")[:, 0:2 * 3 * P]\
            .rearrange("p (b k c) -> p b k c", b=2, k=3)
        sh_w = sb("sh_w", [P, 2, 2, 3, P], F32R)
        sh_act = [ctrl["q"], ctrl["k"]]
        sh_hid = [gain_t["q", "x"], gain_t["q", "y"]]
        sh_hi = [sb(f"sh_hi{n}", [P, CHUNK], F32R) for n in range(2)]
        sh_lo = [sb(f"sh_lo{n}", [P, CHUNK], F32R) for n in range(2)]
        sh_out = sqr["k", "x"]
        (sh_loaded, sh_hi_w, sh_w_ready, sh_gate_ps, sh_up_ps, sh_silu, sh_hid_ready, sh_hi_ready, sh_lo_ready,
         sh_down_ps, sh_out_ready, sh_outT_ps, sh_added) = (sem(n) for n in (
             "sh_loaded", "sh_hi_w", "sh_w_ready", "sh_gate_ps", "sh_up_ps", "sh_silu", "sh_hid_ready",
             "sh_hi_ready", "sh_lo_ready", "sh_down_ps", "sh_out_ready", "sh_outT_ps", "sh_added"))

        block = ctx.enter_context(nc.Block())

        @block.sync
        def _(sp):
            rows = x_rows.rearrange("(t p) e -> p t e", p=P)
            sp.dma_start(x[:, 0:S, :], rows[:, 0:S]).then_inc(x0_in, 16)
            sp.dma_start(wqkv[:, :], wqkv_d).then_inc(w_in, 16)
            sp.dma_start(bqkv[:, :], bqkv_d).then_inc(w_in, 16)
            for dst, src in ((wout_in[:, :], wout_d), (bout[:, :], bout_d), (qw[:, :], qw_d),
                             (logit[:, :], logit_d), (phase[:, :], phase_d), (gates[:, :, :, :], gates_d)):
                sp.dma_start(dst, src).then_inc(small_in, 16)
            sp.dma_start(x[:, S:TILES, :], rows[:, S:TILES]).then_inc(x_in, 16)
            sp.dma_start(gwt[:, :], gw_d).then_inc(gw_in, 16)
            sp.dma_start(gbias[:, :], gbias_d).then_inc(gw_in, 16)
            for n in range(PERIOD):
                sp.dma_start(win[:, n, :, :], wpack_d[n]).then_inc(w_loaded[n], 16)

            def values_out(f):
                sp.wait_ge(vsg_ready, f + 1)
                sp.nop(nofuse=True)
                sp.dma_start(v_d[bass.ds(f * CHUNK, CHUNK), :].rearrange("(s n) e -> n s e", n=P),
                               vsg[:, :, :, :].rearrange("p s h d -> p s (h d)")).then_inc(v_stored, 16)

            def values_in(f):
                sp.wait_ge(v_stored, f * 16 + 16)
                sp.nop(nofuse=True)
                if not has_before(f):
                    sp.wait_ge(zeroed, 2)
                if has_before(f):
                    sp.wait_ge(r_ps, f * 2)
                back = v_d[bass.ds(f * CHUNK, CHUNK), :].rearrange("(s h n f) (j d) -> s h f j n d", s=S, h=2, f=2,
                                                                   j=HEADS)
                for s in range(S):
                    for n4 in range(N4):
                        p0, t8 = 32 * n4 + 8 * s, (n4 % 2) * 4 + s
                        sp.dma_start(vbd[p0:p0 + HEADS, :, t8, :], back[s, n4 // 2, n4 % 2])\
                            .then_inc(v_loaded, 16)

            def keys_queries(f):
                kc, qc = k_d[bass.ds(f, 1)], q_d[bass.ds(f, 1)]

                def put(dst, src, done):
                    sp.dma_start(dst, src[:, :].rearrange("p (s n) -> p s n", s=S)).then_inc(done, 16)

                kv = kc.rearrange("a s c h d n -> (a c) (h d) s n")
                qv = qc.rearrange("a s c v h d n -> (a c) v (h d) s n")
                sp.wait_ge(state_ready["q"], f * 6 + 6)
                put(qv[0, 0], fin["q", "x"], q_stored)
                put(qv[1, 0], fin["q", "y"], q_stored)
                put(qv[1, 1], fin["q", "x"], q_stored)
                sp.wait_ge(state_ready["k"], f * 6 + 6)
                put(kv[0], fin["k", "x"], k_stored)
                put(kv[1], fin["k", "y"], k_stored)
                sp.wait_ge(neg_ready, f + 1)
                put(qv[0, 1], fin_nqy, q_stored)
                sp.wait_ge(k_stored, f * 32 + 32)
                if has_before(f):
                    sp.wait_ge(pat_ps, f)
                kb = kc.rearrange("a s c h d n -> (a s) c d h n")
                for s in range(S):
                    for a in range(2):
                        r = 32 * s + 16 * a
                        sp.dma_start(kbd[r:r + 16, s, :, :], kb[s, a]).then_inc(k_loaded, 16)
                sp.wait_ge(q_stored, f * 64 + 64)
                qb = qc.rearrange("a s c v h d n -> (a s) c d (v h) n")
                for s in range(S):
                    for a in range(2):
                        r = 32 * s + 16 * a
                        sp.dma_start(qs[r:r + 16, :, :, :].rearrange("p v h n -> p (v h) n"), qb[s, a])\
                            .then_inc(q_loaded, 16)

            def measured(b):
                sp.wait_ge(mix_ready, b + 1)
                yd = y_d[bass.ds(b, 1)]
                sp.dma_start(yd.rearrange("a g i d n -> (a g i) (d n)"), mix[:, :]).then_inc(y_stored, 16)
                sp.wait_ge(y_stored, b * 16 + 16)
                sp.dma_start(yin[:, :, :], yd.rearrange("a g i d n -> (a i d) g n")).then_inc(y_loaded, 16)

            def routing_rows(p):
                sp.wait_ge(rwT_ready, p + 1)
                rv = rw_d[:, p * 2 * CHUNK:(p + 1) * 2 * CHUNK].rearrange("e (b s n) -> s e b n", b=S, s=2)
                for s in range(2):
                    sp.dma_start(rv[s], rwT[s * NE:(s + 1) * NE, p * S:(p + 1) * S, :]).then_inc(rw_stored, 16)

            def shared_weights():
                sp.dma_start(sh_in, wpack_d[MT:MT + 2].rearrange("b p k c -> p b k c")).then_inc(sh_loaded, 16)

            def stages(f=None, b=None, w=None):
                if f is not None:
                    values_out(f)
                if w is not None:
                    measured(w)
                if b is not None:
                    values_in(b)
                if f is not None:
                    keys_queries(f)

            stages(f=0)
            stages(f=1, b=0)
            with sp.Fori(0, NCHUNK - 2) as j:
                stages(f=j + 2, b=j + 1, w=j)
            shared_weights()
            measured(NCHUNK - 2)
            values_in(NCHUNK - 1)
            measured(NCHUNK - 1)
            routing_rows(0)
            routing_rows(1)
            sp.wait_ge(rw_stored, 16 * 4)

        @block.gpsimd
        def _(pool):
            c = Chain(pool, pool_s)
            g = nc.gpsimd
            g.memset(tick[:, :], 0.0).then_inc(tick_set, 1)
            c.link(g.memset(ident[:, :], 0.0))
            c.link(g.affine_select(out=ident[:, :], in_=ident[:, :], compare_op=ALU.not_equal, fill=1.0,
                                   base=0, pattern=[[-1, P]], channel_multiplier=1))
            c.link(g.memset(shift[:, :], 0.0))
            c.link(g.affine_select(out=shift[:, :], in_=shift[:, :], compare_op=ALU.not_equal, fill=1.0,
                                   base=-D, pattern=[[-1, P]], channel_multiplier=1))
            c.link(g.memset(own_head[:, :], 1.0))
            c.link(g.affine_select(out=own_head[:, :], in_=own_head[:, :], compare_op=ALU.is_gt, fill=0.0,
                                   base=(HEADS - 1) * D, pattern=[[0, 1]], channel_multiplier=-1))
            c.link(g.affine_select(out=stay[:, :], in_=ident[:, :], compare_op=ALU.is_ge, fill=0.0,
                                   base=-(HEADS - 1) * D, pattern=[[0, P]], channel_multiplier=1))
            c.link(g.memset(pair_sum[:, :], 1.0))
            pv = pair_sum[:, :].rearrange("p (a m) -> p a m", a=2)
            c.link(g.affine_select(out=pv, in_=pv, compare_op=ALU.is_ge, fill=0.0, base=0,
                                   pattern=[[0, 2], [-8, 16]], channel_multiplier=1))
            c.link(g.affine_select(out=pv, in_=pv, compare_op=ALU.is_gt, fill=0.0, base=8,
                                   pattern=[[0, 2], [8, 16]], channel_multiplier=-1))
            c.link(g.memset(pair_back[:, :, :], 1.0))
            c.link(g.affine_select(out=pair_back[:, :, :], in_=pair_back[:, :, :], compare_op=ALU.is_ge, fill=0.0,
                                   base=0, pattern=[[256, 4], [1, P]], channel_multiplier=-8))
            c.link(g.affine_select(out=pair_back[:, :, :], in_=pair_back[:, :, :], compare_op=ALU.is_gt, fill=0.0,
                                   base=8, pattern=[[-256, 4], [-1, P]], channel_multiplier=8))
            c.link(g.memset(circ[:, :, :], 0.0))
            cv = circ[:, :, :].rearrange("p c (q i) -> p c q i", q=4)
            for q in range(CIRC):
                c.link(g.affine_select(out=cv[:, q], in_=cv[:, q], compare_op=ALU.not_equal, fill=1.0,
                                       base=-8 * q, pattern=[[-32, 4], [-1, 8]], channel_multiplier=1))
            c.link(g.memset(before[:, :, :], 1.0))
            c.link(g.affine_select(out=before[:, :, :], in_=before[:, :, :], compare_op=ALU.is_gt, fill=0.0,
                                   base=0, pattern=[[1, NG], [-1, NG]], channel_multiplier=0))
            c.link(g.memset(eps[:, 0:1], LN_EPS))
            c.link(g.memset(eps[:, 1:2], 1e-12))
            g.memset(score[:, :, :], 0.0)
            g.memset(choice[:, :, :, :], 0.0).then_inc(consts, 1)
            g.memset(vbd[:, :, :, :], 0.0).then_inc(zeroed, 1)
            g.memset(kbd[:, :, :, :], 0.0).then_inc(zeroed, 1)
            g.tensor_tensor(maps[:, 0, 0, :], shift[:, :], stay[:, :], ALU.add).then_inc(map0_ready, 1)
            pool.wait_ge(gains_tabled, 2)

            def gains(f, k):
                for w in "qk":
                    pool.wait_ge(ctrl_ready[w], f * DEPTH + k + 1)
                    n = 4 + 2 * k + "qk".index(w)
                    g.tensor_tensor(tick[:, n:n + 1], tick[:, 2:3], tick[:, 2:3], ALU.add)
                    for a in range(2):
                        by, add = (first[:, a, 0:1], first[:, a, 1:2]) if k == 0 else (gain[:, k, a:a + 1], 1.0)
                        g.tensor_scalar(gain_t[w, "xy"[a]][:, :], ctrl[w][:, :], by, add, ALU.mult, ALU.add)\
                            .then_inc(gain_ready[w], 1)

            def shared_low(n):
                pool.wait_ge(sh_hi_ready, n + 1)
                if n >= 2:
                    pool.wait_ge(sh_down_ps, n - 1)
                g.tensor_tensor(sh_lo[n % 2][0:NI, :], sh_hid[n % 2][0:NI, :], sh_hi[n % 2][0:NI, :].bitcast(F32),
                                ALU.subtract).then_inc(sh_lo_ready, 1)

            def bias(f):
                if not has_before(f):
                    pool.wait_ge(tables_ready, 1)
                pool.wait_ge(xn_ready, f * S + S)
                g.tensor_tensor(tick[:, 12:13], tick[:, 2:3], tick[:, 2:3], ALU.add)
                xi = x[:, bass.ds(f * S, S), :]
                g.tensor_tensor(xi, xi, bout[:, :].unsqueeze(1).to_broadcast([P, S, E]), ALU.add).then_inc(biased, 1)

            def stages(f=None, b=None, w=None):
                if f is not None:
                    gains(f, 0)
                    gains(f, 1)
                    gains(f, 2)
                    bias(f)

            stages(f=0)
            stages(f=1, b=0)
            with pool.Fori(0, NCHUNK - 2) as j:
                stages(f=j + 2, b=j + 1, w=j)
            for n in range(2 * NCHUNK):
                shared_low(n)

        @block.vector
        def _(dve):
            v = nc.vector
            c = Chain(dve, dve_s)

            def carry():
                v.tensor_copy(tick[:, 1:2], tick[:, 0:1])

            def moments(n, st, mv, rt, var):
                carry()
                for s in range(S):
                    k = c.step(v.bn_stats(st[:, s, :], x[:, bass.ds(n * S + s, 1), :].rearrange("p a e -> p (a e)")))
                c.after(k)
                carry()
                for s in range(S):
                    k = c.step(v.bn_aggr(mv[:, s, :], st[:, s, :]))
                c.after(k)
                v.tensor_scalar(rt[:, :], mv[:, :, 1], LN_EPS, None, ALU.add).then_inc(var, 1)

            def normalise(n, mv, rt, std, rstd, std_ready, dst, ready):
                dve.wait_ge(std_ready, n + 1)
                c.link(v.reciprocal(rstd[:, :], std[:, :]))
                c.link(v.tensor_tensor(rt[:, :], rt[:, :], rstd[:, :], ALU.mult))
                c.link(v.tensor_tensor(rt[:, :], rt[:, :], rstd[:, :], ALU.mult))
                c.link(v.tensor_scalar(rt[:, :], rt[:, :], -0.5, 1.5, ALU.mult, ALU.add))
                c.link(v.tensor_tensor(rstd[:, :], rstd[:, :], rt[:, :], ALU.mult))
                for s in range(S):
                    v.tensor_scalar(dst[:, s, :], x[:, bass.ds(n * S + s, 1), :].rearrange("p a e -> p (a e)"),
                                    mv[:, s, 0:1], rstd[:, s:s + 1], ALU.subtract, ALU.mult).then_inc(ready, 1)

            def project(f):
                for s in range(S):
                    dve.wait_ge(qkv_ps, f * S + s + 1)
                    v.tensor_tensor(qkv[:, s, :, :].rearrange("p h d -> p (h d)"), bank[(3, 4, 5, 2)[s]][:, 0:3 * E],
                                    bqkv[:, :], ALU.add).then_inc(qkv_ready, 1)

            def norms(f):
                dve.wait_ge(sq_ready, f + 1)
                c.link(v.tensor_reduce(ss[:, :], sq[:, :, :, :].rearrange("p s h d -> p (s h) d"), AX.X, ALU.add))
                v.tensor_scalar(ss[:, :], ss[:, :], 1e-24, None, ALU.max).then_inc(ss_ready, 1)

            def encode(f):
                dve.wait_ge(norm_ready, f + 1)
                c.link(v.reciprocal(rn[:, :], rn[:, :]))
                rnv = rn[:, :].rearrange("p (s h) -> p s h", s=S)
                for a in range(3):
                    h0 = a * HEADS
                    part = qkv[:, :, h0:h0 + HEADS, :]
                    ins = v.tensor_tensor(part, part,
                                          rnv[:, :, h0:h0 + HEADS].unsqueeze(3).to_broadcast([P, S, HEADS, D]),
                                          ALU.mult)
                    if a < 2:
                        ins.then_inc(qk_ready, 1)
                    else:
                        c.link(ins)

            def sign_values(f):
                vals = qkv[:, :, 2 * HEADS:3 * HEADS, :]
                c.link(v.tensor_reduce(vs[:, :, :], vals.rearrange("p s h d -> p s d h"), AX.X, ALU.add))
                c.link(v.tensor_scalar(vg[:, :, :], vs[:, :, :], 0.0, 2.0, ALU.is_ge, ALU.mult))
                c.link(v.tensor_scalar(vg[:, :, :], vg[:, :, :], 1.0, None, ALU.subtract))
                if has_before(f):
                    dve.wait_ge(v_stored, f * 16)
                v.tensor_tensor(vsg[:, :, :, :], vals,
                                vg[:, :, :].unsqueeze(2).to_broadcast([P, S, HEADS, D]), ALU.mult)\
                    .then_inc(vsg_ready, 1)

            def entangle(f, k):
                for w, b in (("q", 2), ("k", 4)):
                    if k:
                        dve.wait_ge(sqr_ready[w], f * (DEPTH - 1) + k)
                        v.tensor_tensor(ctrl[w][:, :], sqr[w, "x"], sqr[w, "y"], ALU.add)\
                            .then_inc(ctrl_ready[w], 1)
                if k == DEPTH - 1 and has_before(f):
                    dve.wait_ge(k_stored, f * 32)
                    dve.wait_ge(q_stored, f * 64)
                for w, b in (("q", 2), ("k", 4)):
                    for a in range(2):
                        dve.wait_ge(z_ps[w], f * 6 + 2 * k + 2)
                        dve.wait_ge(gain_ready[w], f * 6 + 2 * k + a + 1)
                        dst = (fin if k == DEPTH - 1 else state)[w, "xy"[a]]
                        v.tensor_tensor(dst[:, :], bank[b + (a if k else 0)][:, :], gain_t[w, "xy"[a]][:, :], ALU.mult)\
                            .then_inc(state_ready[w], 1)

            def pattern_square(b):
                dve.wait_ge(psq_ready, b + 1)
                v.tensor_tensor(pt[:, :, :], psq[:, :, 0, :], psq[:, :, 1, :], ALU.add).then_inc(pt_ready, 1)

            def pattern_max(b):
                dve.wait_ge(ptT_ps, b + 1)
                c.link(v.tensor_reduce(mx[:, :, :], bank[7][:, 0:256].rearrange("p (b m j) -> p b m j", b=2, j=8),
                                       AX.X, ALU.max))
                v.tensor_copy(mb[:, :, :, :], mx[:, :, :].unsqueeze(3).to_broadcast([P, 2, 16, 8]))\
                    .then_inc(mb_ready, 1)

            def pattern_less_max(b):
                dve.wait_ge(mbT_ps, b + 1)
                v.tensor_tensor(dm[:, :, :].rearrange("p n h -> p (n h)"), pt[:, :, :].rearrange("p n h -> p (n h)"),
                                bank[6][:, 0:256], ALU.subtract).then_inc(dm_ready, 1)

            def one_over_sum(b):
                dve.wait_ge(z_sum, b + 1)
                v.reciprocal(rz[:, :], bank[7][:, 0:256]).then_inc(rz_ready, 1)

            def probabilities(b):
                dve.wait_ge(rz_ps, b + 1)
                for g in range(4):
                    v.tensor_tensor(pr[:, 8 * g:8 * g + 8, :, :].rearrange("p n c h -> p (n c h)"),
                                    ex[:, 8 * g:8 * g + 8, :, :].rearrange("p n c h -> p (n c h)"),
                                    bank[g // 2][:, (g % 2) * 256:(g % 2) * 256 + 256], ALU.mult)\
                        .then_inc(pr_ready, 1)

            def amplitudes(b, k):
                m, bk = QUARTERS[k]
                dve.wait_ge(abs_ready, b * 4 + k + 1)
                c.link(v.tensor_scalar(amp[:, m, :], amp[:, m, :], 1e-6, 1.0, ALU.max, ALU.min))
                v.scalar_tensor_tensor(out=amp[:, m, :].bitcast(U32), in0=bank[bk][:, :].bitcast(U32),
                                       scalar=0x80000000, in1=amp[:, m, :].bitcast(U32),
                                       op0=ALU.bitwise_and, op1=ALU.bitwise_or).then_inc(amp_ready, 1)

            def residual(b):
                dve.wait_ge(y_ps, b + 1)
                dve.wait_ge(biased, b + 1)
                xi = x[:, bass.ds(b * S, S), :]
                v.tensor_tensor(xi, xi, bank[1][:, :].rearrange("p (s e) -> p s e", s=S), ALU.add)\
                    .then_inc(x1_ready, 1)
                dve.wait_ge(x1_ready, b + 1)

            def logits(r):
                dve.wait_ge(xn2T_ready, r + 1)
                hi = xhi[:, bass.ds(r * CHUNK, CHUNK)]
                c.link(v.tensor_copy(hi, xn2T[:, :]))
                v.tensor_tensor(xlo[:, bass.ds(r * CHUNK, CHUNK)], xn2T[:, :], hi.bitcast(F32), ALU.subtract)\
                    .then_inc(x_split, 1)
                dve.wait_ge(lg_ps, r + 1)
                v.tensor_scalar(lg[:, :, :].rearrange("p s e -> p (s e)"), bank[1][:, 0:S * NE], -87.0, None,
                                ALU.max).then_inc(lg_ready, 1)

            def scores(r):
                if not has_before(r):
                    dve.wait_ge(gw_in, 16 * 2)
                dve.wait_ge(el_ready, r + 1)
                c.link(v.tensor_scalar(e1[:, :, :], el[:, :, :], 1.0, None, ALU.add))
                c.link(v.reciprocal(score[:, :, :], e1[:, :, :]))
                c.link(v.tensor_tensor(choice[:, :, :, :].rearrange("p s g k -> p s (g k)"), score[:, :, :],
                                       gbias[:, :].unsqueeze(1).to_broadcast([P, S, NE]), ALU.add))

            def groups():
                carry()
                for s in range(S):
                    for g in range(NG):
                        ins = v.max(top[:, s, g, :], choice[:, s, g, :])
                c.link(ins)
                c.link(v.tensor_tensor(gs[:, :, :], top[:, :, :, 0], top[:, :, :, 1], ALU.add))
                other = gs[:, :, :].unsqueeze(2).to_broadcast([P, S, NG, NG])
                own_g = gs[:, :, :].unsqueeze(3).to_broadcast([P, S, NG, NG])
                c.step(v.tensor_tensor(gt[:, :, :, :], other, own_g, ALU.is_gt))
                c.link(v.tensor_tensor(ge[:, :, :, :], other, own_g, ALU.is_equal))
                c.link(v.tensor_tensor(ge[:, :, :, :].rearrange("p s g k -> p s (g k)"),
                                       ge[:, :, :, :].rearrange("p s g k -> p s (g k)"),
                                       before[:, :, :].rearrange("p g k -> p (g k)").unsqueeze(1)
                                       .to_broadcast([P, S, NG * NG]), ALU.mult))
                c.link(v.tensor_tensor(gt[:, :, :, :], gt[:, :, :, :], ge[:, :, :, :], ALU.add))
                c.link(v.tensor_reduce(rank[:, :, :], gt[:, :, :, :], AX.X, ALU.add))
                c.link(v.tensor_scalar(gm[:, :, :], rank[:, :, :], TOPG - 0.5, None, ALU.is_lt))
                c.link(v.tensor_tensor(masked[:, :, :].rearrange("p s (g k) -> p s g k", g=NG), choice[:, :, :, :],
                                       gm[:, :, :].unsqueeze(3).to_broadcast([P, S, NG, NE // NG]), ALU.mult))

            def experts_picked(w):
                carry()
                for s in range(S):
                    k = c.step(v.max(best[:, s, :], masked[:, s, :]))
                c.after(k)
                carry()
                for s in range(S):
                    k = c.step(v.match_replace(out=rest[:, s, :], in_to_replace=best[:, s, :],
                                               in_values=masked[:, s, :], imm_value=TAKEN))
                c.after(k)
                c.link(v.scalar_tensor_tensor(out=picked[:, :, :], in0=rest[:, :, :], scalar=TAKEN / 2,
                                              in1=score[:, :, :], op0=ALU.is_lt, op1=ALU.mult))
                c.link(v.tensor_reduce(wsum[:, :], picked[:, :, :], AX.X, ALU.add))
                c.link(v.tensor_scalar(wsum[:, :], wsum[:, :], 1e-20, None, ALU.add))
                c.link(v.reciprocal(wr[:, :], wsum[:, :]))
                c.link(v.tensor_scalar(wr[:, :], wr[:, :], 2.5, None, ALU.mult))
                v.tensor_tensor(rw[:, bass.ds(w * S, S), :], picked[:, :, :],
                                wr[:, :].unsqueeze(2).to_broadcast([P, S, NE]), ALU.mult).then_inc(rw_ready, 1)

            def angles_table():
                dve.wait_ge(consts, 1)
                dve.wait_ge(small_in, 16 * 6)
                own, prev = gates[:, :, 0, :], gates[:, :, 1, :]
                c.link(v.tensor_scalar(ang[:, 0, A_HALF:A_HALF + 3], own[:, :, 0], 0.5, None, ALU.mult))
                c.link(v.tensor_scalar(ang[:, 0, A_PREV:A_PREV + 3], prev[:, :, 1], -0.5, None, ALU.mult))
                c.link(v.tensor_scalar(turns[:, 0, 0:3], own[:, :, 1], own_head[:, 0:1], 0.5, ALU.mult, ALU.mult))
                c.link(v.tensor_tensor(ang[:, 0, A_PREV:A_PREV + 1], phase[:, :], turns[:, 0, 0:1], ALU.subtract))
                c.link(v.tensor_tensor(ang[:, 0, A_PREV + 1:A_PREV + 3], ang[:, 0, A_PREV + 1:A_PREV + 3],
                                       turns[:, 0, 0:2], ALU.add))
                c.link(v.tensor_copy(ang[:, 0, A_PHASE:A_PHASE + 1], phase[:, :]))
                c.link(v.tensor_scalar(ang[:, 0, A_PHASE2:A_PHASE2 + 1], phase[:, :], 2.0, None, ALU.mult))
                c.link(v.tensor_copy(ang[:, 0, A_CIRC:A_CIRC + CIRC], qw[:, :]))
                c.link(v.tensor_scalar(ang[:, 1, :], ang[:, 0, :], PI / 2, None, ALU.add))
                c.link(v.tensor_scalar(turns[:, :, :], ang[:, :, :], 1 / (2 * PI), ROUND, ALU.mult, ALU.add))
                c.link(v.tensor_scalar(turns[:, :, :], turns[:, :, :], ROUND, None, ALU.subtract))
                for part in (TWO_PI_A, TWO_PI_B, TWO_PI_C):
                    c.link(v.scalar_tensor_tensor(out=ang[:, :, :], in0=turns[:, :, :], scalar=-part,
                                                  in1=ang[:, :, :], op0=ALU.mult, op1=ALU.add))
                v.tensor_scalar(ang[:, :, :], ang[:, :, :], PI_SAFE, -PI_SAFE, ALU.min, ALU.max).then_inc(angles, 1)
                c.link(v.tensor_reduce(sup_s[:, 0:1], logit[:, :], AX.X, ALU.max))
                v.tensor_scalar(sup[:, :], logit[:, :], sup_s[:, 0:1], None, ALU.subtract).then_inc(sup_exp, 1)

            def gains_table():
                dve.wait_ge(sines, 1)
                sin, cos = sc[:, 0, :], sc[:, 1, :]
                c.link(v.tensor_tensor(gain[:, :, 0], cos[:, A_HALF:A_HALF + 3], sin[:, A_HALF:A_HALF + 3], ALU.add))
                c.link(v.tensor_tensor(gain[:, :, 1], cos[:, A_HALF:A_HALF + 3], sin[:, A_HALF:A_HALF + 3],
                                       ALU.subtract))
                c.link(v.tensor_scalar(gain[:, :, :], gain[:, :, :], -1.0, own_head[:, 0:1], ALU.add, ALU.mult))
                for a, part in ((0, cos), (1, sin)):
                    c.link(v.tensor_tensor(first[:, a, 0:1], gain[:, 0, a:a + 1], part[:, A_PREV:A_PREV + 1], ALU.mult))
                    v.tensor_copy(first[:, a, 1:2], part[:, A_PREV:A_PREV + 1]).then_inc(gains_tabled, 1)

            def maps_table():
                sin, cos = sc[:, 0, :], sc[:, 1, :]
                for k in range(1, DEPTH):
                    col = A_PREV + k
                    c.link(v.tensor_scalar(maps[:, k, 0, :], shift[:, :], cos[:, col:col + 1], None, ALU.mult))
                    c.link(v.tensor_scalar(maps[:, k, 1, :], shift[:, :], sin[:, col:col + 1], None, ALU.mult))
                    c.link(v.tensor_tensor(maps[:, k, 0, :], maps[:, k, 0, :], stay[:, :], ALU.add))
                    v.tensor_scalar(maps[:, k, 2, :], maps[:, k, 1, :], -1.0, None, ALU.mult).then_inc(maps_tabled, 1)

            def weights_table():
                sin, cos = sc[:, 0, :], sc[:, 1, :]
                dve.wait_ge(sup_exp, 2)
                c.link(v.tensor_reduce(sup_s[:, 1:2], ratio[:, :], AX.X, ALU.add))
                c.link(v.reciprocal(sup_s[:, 2:3], sup_s[:, 1:2]))
                c.link(v.tensor_scalar(sup[:, :], ratio[:, :], sup_s[:, 2:3], None, ALU.mult))
                c.link(v.tensor_scalar(circ_sum[:, :], circ[:, 0, :], sup[:, 0:1], None, ALU.mult))
                for q in range(1, CIRC):
                    c.link(v.scalar_tensor_tensor(out=circ_sum[:, :], in0=circ[:, q, :], scalar=sup[:, q:q + 1],
                                                  in1=circ_sum[:, :], op0=ALU.mult, op1=ALU.add))
                c.link(v.tensor_scalar(coef_t[:, :], sin[:, A_CIRC:A_CIRC + CIRC], 0.3, 0.5, ALU.mult, ALU.add))
                c.link(v.tensor_scalar(coef[:, :], coef_t[:, :], -SCALING, SCALING, ALU.mult, ALU.add))
                c.link(v.tensor_tensor(coef[:, :], coef[:, :], coef_t[:, :], ALU.mult))
                c.link(v.tensor_scalar(wout[:, :], wout_in[:, :], cos[:, A_PHASE2:A_PHASE2 + 1], None, ALU.mult))
                v.tensor_scalar(sup_s[:, 3:4], sup_s[:, 2:3], 1.0, None, ALU.mult).then_inc(tables_ready, 1)
                dve.wait_ge(tables_ready, 1)

            def shared_split():
                dve.wait_ge(sh_loaded, 16)
                v.tensor_copy(sh_w[:, 0], sh_in).then_inc(sh_hi_w, 1)
                dve.wait_ge(sh_hi_w, 1)
                v.tensor_tensor(sh_w[:, 1], sh_in, sh_w[:, 0].bitcast(F32), ALU.subtract).then_inc(sh_w_ready, 1)

            def shared_hidden(n):
                dve.wait_ge(sh_silu, n + 1)
                dve.wait_ge(sh_up_ps, n + 1)
                if n >= 2:
                    dve.wait_ge(sh_lo_ready, n - 1)
                v.tensor_tensor(sh_hid[n % 2][0:NI, :], sh_act[n % 2][0:NI, :], bank[3][0:NI, :], ALU.mult)\
                    .then_inc(sh_hid_ready, 1)

            def shared_add(q):
                dve.wait_ge(sh_outT_ps, q + 1)
                xi = x[:, q * S:(q + 1) * S, :]
                v.tensor_tensor(xi, xi, bank[5][:, :].rearrange("p (s e) -> p s e", s=S), ALU.add).then_inc(sh_added, 1)

            def stages(f=None, b=None, w=None):
                if f is not None:
                    moments(f, st, mv, rt, var1)
                    normalise(f, mv, rt, std, rstd, std1, xn, xn_ready)
                if w is not None:
                    amplitudes(w, 0)
                    amplitudes(w, 1)
                if f is not None:
                    project(f)
                if w is not None:
                    groups()
                if f is not None:
                    norms(f)
                if w is not None:
                    amplitudes(w, 2)
                    amplitudes(w, 3)
                if f is not None:
                    encode(f)
                if b is not None:
                    pattern_square(b)
                if f is not None:
                    sign_values(f)
                if b is not None:
                    pattern_max(b)
                if f is not None:
                    entangle(f, 0)
                if w is not None:
                    experts_picked(w)
                if b is not None:
                    pattern_less_max(b)
                if f is not None:
                    entangle(f, 1)
                if w is not None:
                    residual(w)
                if b is not None:
                    one_over_sum(b)
                if w is not None:
                    moments(w, st2, mv2, rt2, var2)
                    normalise(w, mv2, rt2, stdb, rstd2, std2, xn2, xn2_ready)
                if b is not None:
                    probabilities(b)
                if f is not None:
                    entangle(f, 2)
                if w is not None:
                    logits(w)
                    scores(w)

            dve.wait_ge(tick_set, 1)
            dve.wait_ge(x0_in, 16)
            moments(0, st, mv, rt, var1)
            normalise(0, mv, rt, std, rstd, std1, xn, xn_ready)
            angles_table()
            dve.wait_ge(w_in, 16 * 2)
            project(0)
            gains_table()
            norms(0)
            encode(0)
            maps_table()
            sign_values(0)
            entangle(0, 0)
            weights_table()
            entangle(0, 1)
            entangle(0, 2)
            dve.wait_ge(x_in, 16)
            stages(f=1, b=0)
            before_loop = c.k
            with dve.Fori(0, NCHUNK - 2) as j:
                c.start(j * DVE_STEPS + before_loop)
                stages(f=j + 2, b=j + 1, w=j)
                assert c.k == DVE_STEPS, c.k
            c.start(before_loop + (NCHUNK - 2) * DVE_STEPS)
            amplitudes(NCHUNK - 2, 0)
            amplitudes(NCHUNK - 2, 1)
            amplitudes(NCHUNK - 2, 2)
            amplitudes(NCHUNK - 2, 3)
            shared_split()
            groups()
            experts_picked(NCHUNK - 2)
            pattern_square(NCHUNK - 1)
            pattern_max(NCHUNK - 1)
            shared_hidden(0)
            pattern_less_max(NCHUNK - 1)
            residual(NCHUNK - 2)
            shared_hidden(1)
            one_over_sum(NCHUNK - 1)
            moments(NCHUNK - 2, st2, mv2, rt2, var2)
            normalise(NCHUNK - 2, mv2, rt2, stdb, rstd2, std2, xn2, xn2_ready)
            probabilities(NCHUNK - 1)
            logits(NCHUNK - 2)
            shared_hidden(2)
            scores(NCHUNK - 2)
            amplitudes(NCHUNK - 1, 0)
            amplitudes(NCHUNK - 1, 1)
            shared_hidden(3)
            amplitudes(NCHUNK - 1, 2)
            amplitudes(NCHUNK - 1, 3)
            shared_add(0)
            shared_hidden(4)
            groups()
            shared_add(1)
            shared_hidden(5)
            experts_picked(NCHUNK - 1)
            residual(NCHUNK - 1)
            moments(NCHUNK - 1, st2, mv2, rt2, var2)
            normalise(NCHUNK - 1, mv2, rt2, stdb, rstd2, std2, xn2, xn2_ready)
            logits(NCHUNK - 1)
            scores(NCHUNK - 1)
            shared_hidden(6)
            groups()
            shared_hidden(7)
            experts_picked(NCHUNK)
            shared_add(2)
            shared_add(3)

        @block.scalar
        def _(act):
            a_ = nc.scalar

            def deviation(n, rt, std, var, ready):
                act.wait_ge(var, n + 1)
                a_.activation(std[:, :], rt[:, :], ACT.Sqrt).then_inc(ready, 1)

            def transposed(n, dst, src, ps, ready):
                act.wait_ge(ps, n + 1)
                a_.activation(dst[:, :], src[:, :], ACT.Copy).then_inc(ready, 1)

            def squares(f):
                act.wait_ge(qkv_ready, f * S + S)
                a_.activation(sq[:, :, :, :].rearrange("p s h d -> p (s h d)"),
                              qkv[:, :, :, :].rearrange("p s h d -> p (s h d)"), ACT.Square).then_inc(sq_ready, 1)

            def norms(f):
                act.wait_ge(ss_ready, f + 1)
                a_.activation(rn[:, :], ss[:, :], ACT.Sqrt).then_inc(norm_ready, 1)

            def encoded(f):
                for w, bk, n in (("q", 2, 0), ("k", 4, 1)):
                    act.wait_ge(qkT_ps, f * 2 + n + 1)
                    a_.activation(state[w, "x"][:, :], bank[bk][:, :], ACT.Copy).then_inc(r_ready, 1)
                    a_.activation(ctrl[w][:, :], bank[bk][:, :], ACT.Square).then_inc(ctrl_ready[w], 1)

            def state_squares(f, k):
                for w in "qk":
                    act.wait_ge(state_ready[w], f * 6 + 2 * k)
                    for a in "xy":
                        ins = a_.activation(sqr[w, a], state[w, a][:, :], ACT.Square)
                    ins.then_inc(sqr_ready[w], 1)

            def negative(f):
                act.wait_ge(state_ready["q"], f * 6 + 6)
                if has_before(f):
                    act.wait_ge(q_stored, f * 64)
                a_.activation(fin_nqy[:, :], fin["q", "y"][:, :], ACT.Copy, scale=-1.0).then_inc(neg_ready, 1)

            def pattern_squares(b):
                act.wait_ge(pat_ps, b + 1)
                a_.activation(psq[:, :, :, :].rearrange("p n v h -> p (n v h)"), bank[6][:, :], ACT.Square)\
                    .then_inc(psq_ready, 1)

            def exponentials(b):
                act.wait_ge(dm_ready, b + 1)
                for q in range(CIRC):
                    a_.activation(ex[:, :, q, :], dm[:, :, :], ACT.Exp, scale=coef[:, q:q + 1]).then_inc(ex_ready, 1)

            def amplitudes(b):
                act.wait_ge(pr_ready, b * 4 + 4)
                a_.activation(am[:, :, :, :].rearrange("p n c h -> p (n c h)"),
                              pr[:, :, :, :].rearrange("p n c h -> p (n c h)"), ACT.Sqrt, bias=eps[:, 1:2])\
                    .then_inc(am_ready, 1)

            def magnitudes(b, k):
                m, bk = QUARTERS[k]
                act.wait_ge(r_ps, b * 2 + k // 2 + 1)
                a_.activation(amp[:, m, :], bank[bk][:, :], ACT.Abs).then_inc(abs_ready, 1)

            def measured(b):
                act.wait_ge(mix_ps, b + 1)
                a_.activation(mix[:, :], bank[7][:, :], ACT.Copy).then_inc(mix_ready, 1)

            def sigmoid(r):
                act.wait_ge(lg_ready, r + 1)
                a_.activation(el[:, :, :], lg[:, :, :], ACT.Exp, scale=-1.0).then_inc(el_ready, 1)

            def routing_rows(p):
                act.wait_ge(rwT_ps, p + 1)
                a_.activation(rwT[:, p * S:(p + 1) * S, :].rearrange("p b n -> p (b n)"), bank[2 + p][:, :], ACT.Copy)\
                    .then_inc(rwT_ready, 1)

            def shared_gate(n):
                act.wait_ge(sh_gate_ps, n + 1)
                a_.activation(sh_act[n % 2][0:NI, :], bank[2][0:NI, :], ACT.Silu).then_inc(sh_silu, 1)

            def shared_high(n):
                act.wait_ge(sh_hid_ready, n + 1)
                if n >= 2:
                    act.wait_ge(sh_down_ps, n - 1)
                a_.activation(sh_hi[n % 2][0:NI, :], sh_hid[n % 2][0:NI, :], ACT.Copy).then_inc(sh_hi_ready, 1)

            def shared_output(q):
                act.wait_ge(sh_down_ps, 2 * q + 2)
                if q:
                    act.wait_ge(sh_outT_ps, q)
                a_.activation(sh_out, bank[4][:, :], ACT.Copy).then_inc(sh_out_ready, 1)

            def stages(f=None, b=None, w=None):
                if f is not None:
                    deviation(f, rt, std, var1, std1)
                if w is not None:
                    magnitudes(w, 0)
                    magnitudes(w, 1)
                if f is not None:
                    transposed(f, xnT, bank[2], xT_ps, xT_ready)
                if w is not None:
                    magnitudes(w, 2)
                if f is not None:
                    squares(f)
                    norms(f)
                if w is not None:
                    magnitudes(w, 3)
                if b is not None:
                    pattern_squares(b)
                if f is not None:
                    encoded(f)
                if w is not None:
                    measured(w)
                if f is not None:
                    state_squares(f, 1)
                if b is not None:
                    exponentials(b)
                if f is not None:
                    state_squares(f, 2)
                if w is not None:
                    deviation(w, rt2, stdb, var2, std2)
                if b is not None:
                    amplitudes(b)
                if w is not None:
                    transposed(w, xn2T, bank[6], xn2T_ps, xn2T_ready)
                    sigmoid(w)
                if f is not None:
                    negative(f)

            deviation(0, rt, std, var1, std1)
            transposed(0, xnT, bank[2], xT_ps, xT_ready)
            act.wait_ge(sup_exp, 1)
            a_.activation(ratio[:, :], sup[:, :], ACT.Exp).then_inc(sup_exp, 1)
            act.wait_ge(angles, 1)
            a_.activation(sc[:, :, :], ang[:, :, :], ACT.Sin).then_inc(sines, 1)
            squares(0)
            norms(0)
            encoded(0)
            state_squares(0, 1)
            state_squares(0, 2)
            negative(0)
            stages(f=1, b=0)
            with act.Fori(0, NCHUNK - 2) as j:
                stages(f=j + 2, b=j + 1, w=j)
            magnitudes(NCHUNK - 2, 0)
            magnitudes(NCHUNK - 2, 1)
            magnitudes(NCHUNK - 2, 2)
            magnitudes(NCHUNK - 2, 3)
            pattern_squares(NCHUNK - 1)
            measured(NCHUNK - 2)
            shared_gate(0)
            shared_high(0)
            exponentials(NCHUNK - 1)
            shared_gate(1)
            shared_high(1)
            deviation(NCHUNK - 2, rt2, stdb, var2, std2)
            shared_output(0)
            amplitudes(NCHUNK - 1)
            transposed(NCHUNK - 2, xn2T, bank[6], xn2T_ps, xn2T_ready)
            shared_gate(2)
            sigmoid(NCHUNK - 2)
            shared_high(2)
            magnitudes(NCHUNK - 1, 0)
            magnitudes(NCHUNK - 1, 1)
            shared_gate(3)
            shared_high(3)
            magnitudes(NCHUNK - 1, 2)
            magnitudes(NCHUNK - 1, 3)
            shared_output(1)
            shared_gate(4)
            measured(NCHUNK - 1)
            shared_high(4)
            shared_gate(5)
            shared_high(5)
            shared_output(2)
            routing_rows(0)
            deviation(NCHUNK - 1, rt2, stdb, var2, std2)
            transposed(NCHUNK - 1, xn2T, bank[6], xn2T_ps, xn2T_ready)
            sigmoid(NCHUNK - 1)
            shared_gate(6)
            shared_high(6)
            shared_gate(7)
            shared_high(7)
            routing_rows(1)
            shared_output(3)

        @block.tensor
        def _(pe):
            t = nc.tensor
            def transpose_x(n, bk, src, ready, ps):
                if not has_before(n) and src is xn:
                    pe.wait_ge(consts, 1)
                pe.wait_ge(ready, n * S + S)
                for s in range(S):
                    ins = t.transpose(bk[:, s * P:(s + 1) * P], src[:, s, :], ident[:, :])
                ins.then_inc(ps, 1)

            def project(f):
                if not has_before(f):
                    pe.wait_ge(w_in, 16 * 2)
                pe.wait_ge(xT_ready, f + 1)
                for s in range(S):
                    t.matmul(bank[(3, 4, 5, 2)[s]][:, 0:3 * E], xnT[:, s * P:(s + 1) * P], wqkv[:, :],
                             start=True, stop=True).then_inc(qkv_ps, 1)

            def encode(f):
                for n, bk in ((0, 2), (1, 4)):
                    pe.wait_ge(qk_ready, f * 2 + n + 1)
                    for s in range(S):
                        ins = t.transpose(bank[bk][:, s * P:(s + 1) * P],
                                          qkv[:, s, n * HEADS:(n + 1) * HEADS, :].rearrange("p h d -> p (h d)"),
                                          ident[:, :])
                    ins.then_inc(qkT_ps, 1)

            def entangle(f, k):
                if not has_before(f) and k < 2:
                    pe.wait_ge(maps_tabled if k else map0_ready, k + 1)
                for n, (w, bk) in enumerate((("q", 2), ("k", 4))):
                    sx, sy = state[w, "x"], state[w, "y"]
                    if k == 0:
                        pe.wait_ge(r_ready, f * 2 + n + 1)
                        pe.wait_ge(ctrl_ready[w], f * DEPTH + 1)
                        t.matmul(bank[bk][:, :], maps[:, 0, 0, :], sx[:, :], start=True, stop=True)\
                            .then_inc(z_ps[w], 2)
                        continue
                    pe.wait_ge(state_ready[w], f * 6 + 2 * k)
                    t.matmul(bank[bk][:, :], maps[:, k, 0, :], sx[:, :], start=True, stop=False)
                    t.matmul(bank[bk][:, :], maps[:, k, 2, :], sy[:, :], start=False, stop=True)\
                        .then_inc(z_ps[w], 1)
                    t.matmul(bank[bk + 1][:, :], maps[:, k, 1, :], sx[:, :], start=True, stop=False)
                    t.matmul(bank[bk + 1][:, :], maps[:, k, 0, :], sy[:, :], start=False, stop=True)\
                        .then_inc(z_ps[w], 1)

            def pattern(b):
                pe.wait_ge(k_loaded, b * 128 + 128)
                pe.wait_ge(q_loaded, b * 128 + 128)
                if has_before(b):
                    pe.wait_ge(amp_ready, b * 4 - 3)
                for n in range(P):
                    n4, n1 = 2 * (n // 64) + n % 2, n % 64 // 2
                    ins = t.matmul(bank[6][32 * n4:32 * n4 + 32, n1 * 16:n1 * 16 + 16],
                                   kbd[:, :, :, n].rearrange("p s h -> p s h"), qs[:, :, :, n],
                                   start=True, stop=True)
                ins.then_inc(pat_ps, 1)

            def pattern_max(b):
                if has_before(b):
                    pe.wait_ge(mix_ready, b)
                pe.wait_ge(pt_ready, b + 1)
                for a in range(2):
                    ins = t.transpose(bank[7][:, a * P:(a + 1) * P],
                                      pt[:, 16 * a:16 * a + 16, :].rearrange("p n h -> p (n h)"), ident[:, :])
                ins.then_inc(ptT_ps, 1)

            def max_back(b):
                pe.wait_ge(mb_ready, b + 1)
                for a in range(2):
                    ins = t.transpose(bank[6][:, a * P:(a + 1) * P],
                                      mb[:, a, :, :].rearrange("p m j -> p (m j)"), ident[:, :])
                ins.then_inc(mbT_ps, 1)

            def sums(b):
                pe.wait_ge(ex_ready, b * 4 + 4)
                for g in range(4):
                    ins = t.matmul(bank[7][32 * g:32 * g + 32, 0:256], pair_sum[:, :],
                                   ex[:, 8 * g:8 * g + 8, :, :].rearrange("p n c h -> p (n c h)"),
                                   start=True, stop=True)
                ins.then_inc(z_sum, 1)

            def sums_back(b):
                pe.wait_ge(rz_ready, b + 1)
                for g in range(4):
                    ins = t.matmul(bank[g // 2][:, (g % 2) * 256:(g % 2) * 256 + 256], pair_back[:, g, :], rz[:, :],
                                   start=True, stop=True)
                ins.then_inc(rz_ps, 1)

            def weigh(b, r):
                if r == 0:
                    pe.wait_ge(v_loaded, b * 256 + 256)
                    pe.wait_ge(am_ready, b + 1)
                    pe.nop(nofuse=True)
                elif isinstance(b, int) and b > 0:
                    pe.wait_ge(lg_ready, b)
                for n in range(16):
                    for h in range(2):
                        q, slot, n1, bk = n // 4, n % 4, 16 * r + n, QUARTERS[2 * r + h][1]
                        out = bank[bk][32 * q:32 * q + 32, :].rearrange("p (d e t) -> p e t d", d=D, e=4)
                        ins = t.matmul(out[:, slot], am[64 * h:64 * h + 64, n1, :, :].rearrange("p c i -> p (c i)"),
                                       vbd[64 * h:64 * h + 64, n1, :, :], start=True, stop=True)
                ins.then_inc(r_ps, 1)

            def circuits(b):
                for k, (m, _) in enumerate(QUARTERS):
                    pe.wait_ge(amp_ready, b * 4 + max(k, 1) + 1)
                    ins = t.matmul(bank[7][32 * m:32 * m + 32, :], circ_sum[:, :], amp[:, m, :],
                                   start=True, stop=True)
                ins.then_inc(mix_ps, 1)

            def output(b):
                pe.wait_ge(y_loaded, b * 16 + 16)
                for s in range(S):
                    out = bank[1][:, s * P:(s + 1) * P]
                    strip = yin[:, :, :].rearrange("p g (n s) -> p s (g n)", s=S)[:, s]
                    ins = t.matmul(out, strip, wout[:, :], start=True, stop=True)
                ins.then_inc(y_ps, 1)

            def logits(r):
                if not has_before(r):
                    pe.wait_ge(gw_in, 16 * 2)
                pe.wait_ge(xn2T_ready, r + 1)
                for s in range(S):
                    ins = t.matmul(bank[1][:, s * NE:(s + 1) * NE], xn2T[:, s * P:(s + 1) * P], gwt[:, :],
                                   start=True, stop=True)
                ins.then_inc(lg_ps, 1)

            def routing_rows(p):
                pe.wait_ge(rw_ready, 2 * p + 3)
                for a in range(p * S, (p + 1) * S):
                    ins = t.transpose(bank[2 + p][:, (a - p * S) * P:(a - p * S + 1) * P],
                                      rw[:, S + 2 * a:S + 2 * a + 2, :].rearrange("p s e -> p (s e)"), ident[:, :])
                ins.then_inc(rwT_ps, 1)

            def three(out, w, b, k, mhi, mlo, start, stop, rows=P):
                cols = P if k == 2 else NI
                hi, lo = sh_w[0:rows, 0, b, k, 0:cols], sh_w[0:rows, 1, b, k, 0:cols]
                t.matmul(out, hi, mhi, start=start, stop=False)
                t.matmul(out, hi, mlo, start=False, stop=False)
                return t.matmul(out, lo, mhi, start=False, stop=stop)

            def shared_up(n):
                q = n // 2
                xs = slice(q * CHUNK, (q + 1) * CHUNK)
                if n == 0:
                    pe.wait_ge(sh_w_ready, 1)
                else:
                    pe.wait_ge(sh_silu, n)
                    pe.wait_ge(sh_hid_ready, n)
                pe.wait_ge(x_split, q + 1)
                three(bank[2][0:NI, :], sh_w, n % 2, 0, xhi[:, xs], xlo[:, xs], True, True).then_inc(sh_gate_ps, 1)
                three(bank[3][0:NI, :], sh_w, n % 2, 1, xhi[:, xs], xlo[:, xs], True, True).then_inc(sh_up_ps, 1)

            def shared_down(n):
                pe.wait_ge(sh_lo_ready, n + 1)
                if n >= 2 and n % 2 == 0:
                    pe.wait_ge(sh_out_ready, n // 2)
                three(bank[4][:, :], sh_w, n % 2, 2, sh_hi[n % 2][0:NI, :], sh_lo[n % 2][0:NI, :],
                      n % 2 == 0, n % 2 == 1, rows=NI).then_inc(sh_down_ps, 1)

            def shared_back(q):
                pe.wait_ge(sh_out_ready, q + 1)
                if q:
                    pe.wait_ge(sh_added, q)
                for s in range(S):
                    ins = t.transpose(bank[5][:, s * P:(s + 1) * P], sh_out[:, s * P:(s + 1) * P], ident[:, :])
                ins.then_inc(sh_outT_ps, 1)

            def stages(f=None, b=None, w=None):
                if w is not None:
                    weigh(w, 0)
                if f is not None:
                    transpose_x(f, bank[2], xn, xn_ready, xT_ps)
                    project(f)
                if w is not None:
                    weigh(w, 1)
                if b is not None:
                    pattern(b)
                if w is not None:
                    circuits(w)
                if f is not None:
                    encode(f)
                    entangle(f, 0)
                if b is not None:
                    pattern_max(b)
                    max_back(b)
                if f is not None:
                    entangle(f, 1)
                if w is not None:
                    output(w)
                if b is not None:
                    sums(b)
                    sums_back(b)
                if f is not None:
                    entangle(f, 2)
                if w is not None:
                    transpose_x(w, bank[6], xn2, xn2_ready, xn2T_ps)
                    logits(w)

            stages(f=0)
            stages(f=1, b=0)
            with pe.Fori(0, NCHUNK - 2) as j:
                stages(f=j + 2, b=j + 1, w=j)
            weigh(NCHUNK - 2, 0)
            weigh(NCHUNK - 2, 1)
            pattern(NCHUNK - 1)
            circuits(NCHUNK - 2)
            shared_up(0)
            pattern_max(NCHUNK - 1)
            max_back(NCHUNK - 1)
            shared_up(1)
            shared_down(0)
            output(NCHUNK - 2)
            sums(NCHUNK - 1)
            sums_back(NCHUNK - 1)
            shared_down(1)
            transpose_x(NCHUNK - 2, bank[6], xn2, xn2_ready, xn2T_ps)
            shared_up(2)
            shared_back(0)
            logits(NCHUNK - 2)
            weigh(NCHUNK - 1, 0)
            shared_down(2)
            shared_up(3)
            weigh(NCHUNK - 1, 1)
            shared_down(3)
            shared_up(4)
            circuits(NCHUNK - 1)
            shared_down(4)
            shared_back(1)
            shared_up(5)
            output(NCHUNK - 1)
            shared_down(5)
            routing_rows(0)
            transpose_x(NCHUNK - 1, bank[6], xn2, xn2_ready, xn2T_ps)
            logits(NCHUNK - 1)
            shared_up(6)
            shared_back(2)
            shared_up(7)
            shared_down(6)
            routing_rows(1)
            shared_down(7)
            shared_back(3)



def experts(nc, wpack_d, win, w_loaded, rw_d, out_rows, x, xhi, xlo, ident, bank):
    with ExitStack() as ctx:
        def sb(name, shape, dt=F32):
            return ctx.enter_context(nc.sbuf_tensor(name, shape, dt))

        def sem(name):
            return ctx.enter_context(nc.semaphore(name))

        RING = 4
        whi = sb("whi", [P, PERIOD, 3, P], F32R)
        wlo = sb("wlo", [P, PERIOD, 3, P], F32R)
        rwb = sb("rwb", [P, PERIOD, T])
        act_g = sb("act_g", [P, RING, CHUNK])
        act_u = sb("act_u", [P, RING, CHUNK])
        hid = act_u
        hhi = sb("hhi", [P, RING, CHUNK], F32R)
        hlo = sb("hlo", [P, RING, CHUNK], F32R)
        outT = act_g

        r_loaded = [sem(f"r_loaded{b}") for b in range(PERIOD)]
        whi_ready, wlo_ready, gate_ps, up_ps, silu_ready, au_ready, hid_ready, hhi_ready, hlo_ready, down_ps = (
            sem(n) for n in ("whi_ready", "wlo_ready", "gate_ps", "up_ps", "silu_ready", "au_ready", "hid_ready",
                             "hhi_ready", "hlo_ready", "down_ps"))
        outT_ready, outT_ps, res_ready, stored = (sem(n) for n in ("outT_ready", "outT_ps", "res_ready", "stored"))
        segs = segments()
        per_block = [sum(1 for s in segs if s[0] == b) for b in range(PERIOD)]

        block = ctx.enter_context(nc.Block())

        @block.sync
        def _(sp):
            def period(i, first):
                for b in range(PERIOD):
                    if not first:
                        sp.wait_ge(wlo_ready, (i - 1) * PERIOD + b + 1)
                        sp.nop(nofuse=True)
                        sp.dma_start(win[:, b, :, :], wpack_d[bass.ds(i * PERIOD + b, 1)]
                                     .rearrange("a p k c -> p (a k) c")).then_inc(w_loaded[b], 16)
                    if not first:
                        sp.wait_ge(hid_ready, (i - 1) * UNITS + (b + 1) * NCHUNK)
                    for _, r, n, e in [s for s in segs if s[0] == b]:
                        row = rw_d[bass.ds(i * EXPERTS + e, 1), :]
                        sp.dma_start(rwb[r:r + n, b, :], row.to_broadcast([n, T])).then_inc(r_loaded[b], 16)

            period(0, True)
            with sp.Fori(1, PERIODS) as i:
                period(i, False)
            for c in range(NCHUNK):
                sp.wait_ge(res_ready, c + 1)
                sp.dma_start(out_rows[c * CHUNK:(c + 1) * CHUNK, :].rearrange("(s p) e -> p s e", p=P),
                             x[:, c * S:(c + 1) * S, :]).then_inc(stored, 16)
            sp.wait_ge(stored, 16 * NCHUNK)

        @block.gpsimd
        def _(pool):
            def unit(u, b, q, slot):
                pool.wait_ge(silu_ready, u + 1)
                pool.wait_ge(au_ready, u + 1)
                nc.gpsimd.tensor_tensor(hid[:, slot, :], act_g[:, slot, :], act_u[:, slot, :], ALU.mult)\
                    .then_inc(hid_ready, 1)

            def period(i, first):
                for b in range(PERIOD):
                    for q in range(NCHUNK):
                        u = b * NCHUNK + q
                        if not (first and u < RING):
                            pool.wait_ge(hlo_ready, i * UNITS + u - RING + 1)
                        unit(i * UNITS + u, b, q, u % RING)

            period(0, True)
            with pool.Fori(1, PERIODS) as i:
                period(i, False)

        @block.scalar
        def _(act):
            a_ = nc.scalar

            def silu(u, slot, rows, wait_slot):
                act.wait_ge(gate_ps, u + 1)
                if wait_slot:
                    act.wait_ge(hid_ready, u - RING + 1)
                a_.activation(act_g[0:rows, slot, :], bank[4 + slot % 2][0:rows, :], ACT.Silu).then_inc(silu_ready, 1)

            def high(u, slot, rows, wait_slot):
                act.wait_ge(hid_ready, u + 1)
                if wait_slot:
                    act.wait_ge(down_ps, u - RING + 1)
                a_.activation(hhi[0:rows, slot, :], hid[0:rows, slot, :], ACT.Copy).then_inc(hhi_ready, 1)

            def period(i, first):
                for b in range(PERIOD):
                    for q in range(NCHUNK):
                        u = b * NCHUNK + q
                        silu(i * UNITS + u, u % RING, P, not (first and u < RING))
                        if not (first and u < 2):
                            v = u - 2
                            high(i * UNITS + v, v % RING, P, not (first and v < RING))

            period(0, True)
            with act.Fori(1, PERIODS) as i:
                period(i, False)
            for u in (UNITS * PERIODS - 2, UNITS * PERIODS - 1):
                high(u, u % RING, P, True)
            for c in range(NCHUNK):
                act.wait_ge(down_ps, UNITS * PERIODS - NCHUNK + c + 1)
                a_.activation(outT[:, c, :], bank[c][:, :], ACT.Copy).then_inc(outT_ready, 1)

        @block.vector
        def _(dve):
            v = nc.vector

            def split(b):
                v.tensor_copy(whi[:, b, :, :], win[:, b, :, :]).then_inc(whi_ready, 1)

            def split_lo(n, b):
                dve.wait_ge(whi_ready, n)
                v.tensor_tensor(wlo[:, b, :, :], win[:, b, :, :], whi[:, b, :, :].bitcast(F32), ALU.subtract)\
                    .then_inc(wlo_ready, 1)

            def up(u, slot, rows, b, q, wait_slot):
                dve.wait_ge(up_ps, u + 1)
                if wait_slot:
                    dve.wait_ge(hlo_ready, u - RING + 1)
                src, dst = bank[6 + slot % 2][0:rows, :], act_u[0:rows, slot, :]
                if b is None:
                    v.tensor_copy(dst, src).then_inc(au_ready, 1)
                else:
                    v.tensor_tensor(dst, src, rwb[:, b, q * CHUNK:(q + 1) * CHUNK], ALU.mult).then_inc(au_ready, 1)

            def low(u, slot, rows, wait_slot):
                dve.wait_ge(hhi_ready, u + 1)
                if wait_slot:
                    dve.wait_ge(down_ps, u - RING + 1)
                v.tensor_tensor(hlo[0:rows, slot, :], hid[0:rows, slot, :], hhi[0:rows, slot, :].bitcast(F32),
                                ALU.subtract).then_inc(hlo_ready, 1)

            AHEAD = 2

            def period(i, first, last=False):
                for b in range(PERIOD):
                    for q in range(NCHUNK):
                        u = b * NCHUNK + q
                        if q == 0:
                            dve.wait_ge(r_loaded[b], 16 * per_block[b] * (i + 1))
                        if q == 1 and not (last and b + AHEAD >= PERIOD):
                            nb = (b + AHEAD) % PERIOD
                            wrap = b + AHEAD >= PERIOD
                            dve.wait_ge(w_loaded[nb], 16 * (i + 1 + wrap))
                            if wrap or not first:
                                dve.wait_ge(down_ps, i * UNITS + (b + AHEAD + 1 - PERIOD) * NCHUNK)
                            split(nb)
                        if q == 2 and not (last and b + AHEAD >= PERIOD):
                            nb = (b + AHEAD) % PERIOD
                            split_lo(i * PERIOD + b + AHEAD + 1, nb)
                        up(i * UNITS + u, u % RING, P, b, q, not (first and u < RING))
                        if not (first and u < 2):
                            w = u - 2
                            low(i * UNITS + w, w % RING, P, not (first and w < RING))

            for b in range(AHEAD):
                dve.wait_ge(w_loaded[b], 16)
                split(b)
                split_lo(b + 1, b)
            period(0, True)
            with dve.Fori(1, PERIODS - 1) as i:
                period(i, False)
            period(PERIODS - 1, False, last=True)
            for u in (UNITS * PERIODS - 2, UNITS * PERIODS - 1):
                low(u, u % RING, P, True)
            for c in range(NCHUNK):
                dve.wait_ge(outT_ps, c + 1)
                xi = slice(c * S, (c + 1) * S)
                v.tensor_tensor(x[:, xi, :], x[:, xi, :], bank[4 + c][:, :].rearrange("p (s e) -> p s e", s=S),
                                ALU.add).then_inc(res_ready, 1)

        @block.tensor
        def _(pe):
            t = nc.tensor

            def three(out, hi, lo, mhi, mlo, start, stop):
                t.matmul(out, hi, mhi, start=start, stop=False)
                t.matmul(out, hi, mlo, start=False, stop=False)
                return t.matmul(out, lo, mhi, start=False, stop=stop)

            def up(u, slot, rows, hi, lo, q, wait_slot):
                xs = slice(q * CHUNK, (q + 1) * CHUNK)
                if wait_slot:
                    pe.wait_ge(silu_ready, u - 1)
                three(bank[4 + slot % 2][0:rows, :], hi[:, 0, 0:rows], lo[:, 0, 0:rows], xhi[:, xs], xlo[:, xs],
                      True, True).then_inc(gate_ps, 1)
                if wait_slot:
                    pe.wait_ge(au_ready, u - 1)
                three(bank[6 + slot % 2][0:rows, :], hi[:, 1, 0:rows], lo[:, 1, 0:rows], xhi[:, xs], xlo[:, xs],
                      True, True).then_inc(up_ps, 1)

            def down(u, slot, rows, hi, lo, q, start, stop):
                pe.wait_ge(hlo_ready, u + 1)
                three(bank[q][:, :], hi[0:rows, 2, :], lo[0:rows, 2, :], hhi[0:rows, slot, :], hlo[0:rows, slot, :],
                      start, stop).then_inc(down_ps, 1)

            def period(i, first):
                for b in range(PERIOD):
                    pe.wait_ge(wlo_ready, i * PERIOD + b + 1)
                    for q in range(NCHUNK):
                        u = b * NCHUNK + q
                        up(i * UNITS + u, u % RING, P, whi[:, b], wlo[:, b], q,
                           not (first and u < 2))
                        if not (first and u < LAG):
                            w = (u - LAG) % UNITS
                            wb = w // NCHUNK
                            down(i * UNITS + u - LAG, w % RING, P, whi[:, wb], wlo[:, wb], w % NCHUNK,
                                 first and w < NCHUNK, False)

            period(0, True)
            with pe.Fori(1, PERIODS) as i:
                period(i, False)
            for n in range(LAG):
                w = UNITS * PERIODS - LAG + n
                wb = PERIOD - LAG // NCHUNK
                down(w, w % RING, P, whi[:, wb], wlo[:, wb], w % NCHUNK, False, True)
            for c in range(NCHUNK):
                pe.wait_ge(outT_ready, c + 1)
                for s in range(S):
                    ins = t.transpose(bank[4 + c][:, s * P:(s + 1) * P],
                                      outT[:, c, s * P:(s + 1) * P], ident[:, :])
                ins.then_inc(outT_ps, 1)


def _layouts(np_, i):
    c = np_.ascontiguousarray

    def rows(a):
        return c(np_.broadcast_to(a[None, :], (P, a.shape[0])))

    def blocks(g, u, d):
        n, k, _ = g.shape
        out = np_.zeros((n, P, 3, P), np_.float32)
        out[:, :, 0, :k] = g.transpose(0, 2, 1)
        out[:, :, 1, :k] = u.transpose(0, 2, 1)
        out[:, :k, 2, :] = d
        return out

    pre, ffn = "L0_attn_", "L0_ffn_"
    gates = i[pre + "entanglement_gates"][:, :, 0:2]
    own = np_.repeat(gates, D, axis=1).transpose(1, 0, 2)
    prev = np_.repeat(np_.roll(gates, 1, axis=1), D, axis=1).transpose(1, 0, 2)
    wg = i[ffn + "Wg"].reshape(MT, P, E)
    wu = i[ffn + "Wu"].reshape(MT, P, E)
    wd = i[ffn + "Wd"].transpose(0, 2, 1).reshape(MT, P, E)
    shared = blocks(i[ffn + "Sg"].reshape(2, NI, E), i[ffn + "Su"].reshape(2, NI, E),
                    i[ffn + "Sd"].T.reshape(2, NI, E))
    return {
        "x": c(i[pre + "query"]),
        "wqkv": c(i[pre + "W_qkv"].T),
        "bqkv": rows(i[pre + "b_qkv"]),
        "wout": c(i[pre + "W_out"].T),
        "bout": rows(i[pre + "b_out"]),
        "qw": rows(i[pre + "quantum_weights"][:, 0, 0]),
        "phase": c(np_.tile(np_.diagonal(i[pre + "photonic_phases"][:D, :D]), HEADS)[:, None]),
        "gates": c(np_.stack([own, prev], axis=2)),
        "logit": rows(i[pre + "superposition_logits"]),
        "gw": c(i[ffn + "gate_w"].T),
        "gbias": rows(i[ffn + "gate_bias"]),
        "wpack": np_.concatenate([blocks(wg, wu, wd), shared]),
    }


def kernel(**inputs):
    import concourse.bacc as _bacc
    from concourse import mybir as _mybir
    from concourse.bass_utils import run_bass_kernel_spmd as _run

    nc = _bacc.Bacc("TRN2", target_bir_lowering=False, num_devices=1)
    arrays = _layouts(np, {k: np.asarray(v) for k, v in inputs.items()})
    args = [nc.dram_tensor(f"in_{n}", a.shape, _mybir.dt.float32, kind="ExternalInput").ap()
            for n, a in arrays.items()]
    out = nc.dram_tensor("out_0", (2, 1024, E), _mybir.dt.float32, kind="ExternalOutput").ap()
    build(nc, *args, out)
    r = _run(nc, [{f"in_{n}": a for n, a in arrays.items()}], core_ids=[0])
    return r.results[0]["out_0"]
```
